# Optimizing a Trainium2 kernel written in Bass

```python
import numpy as np
import jax
import jax.numpy as jnp

def _softmax(x, axis=-1):
    return jax.nn.softmax(x, axis=axis)

def _gelu(x):
    return jax.nn.gelu(x, approximate=True)

def _silu(x):
    return jax.nn.silu(x)

def _sigmoid(x):
    return jax.nn.sigmoid(x)

def _layernorm(x, axis=-1, eps=1e-05):
    m = jnp.mean(x, axis=axis, keepdims=True)
    v = jnp.var(x, axis=axis, keepdims=True)
    return (x - m) / jnp.sqrt(v + eps)

def _scatter_add(tgt, idx, src, axis=0):
    return tgt.at[idx].add(src)

def _segment_sum(src, seg, n):
    return jax.ops.segment_sum(src, seg, n)
kernel_name = 'mk_gps_d2_gnn_r32_a1f4c3'

def setup_inputs(seed: int=0):
    np.random.seed(seed)
    _w = jnp.asarray

    def _rec_inputs():
        import jax
        import jax.numpy as jnp
        _gk = jax.random.key(seed)
        x = -0.0003713 + 1 * jax.random.normal(jax.random.fold_in(_gk, 1), (3125, 256), jnp.float32)
        _s = jax.random.randint(jax.random.fold_in(_gk, 2), (25000,), 0, 3125, jnp.int32)
        _d = jax.random.randint(jax.random.fold_in(_gk, 3), (25000,), 0, 3125, jnp.int32)
        _loop = jnp.arange(3125, dtype=jnp.int32)
        src = jnp.concatenate([_s, _d, _loop])
        dst = jnp.concatenate([_d, _s, _loop])
        _o = jnp.argsort(dst, stable=True)
        src = src[_o]
        dst = dst[_o]
        return (x, src, dst)
    x, src, dst = _rec_inputs()

    def _L0_gnn_setup():
        import jax, jax.numpy as jnp
        import numpy as np
        LN_EPS = 1e-05

        def layer_norm(x, g, b):
            m = jnp.mean(x, axis=-1, keepdims=True)
            v = jnp.mean((x - m) ** 2, axis=-1, keepdims=True)
            return (x - m) * jax.lax.rsqrt(v + LN_EPS) * g + b

        def gin_conv(x, src, dst, eps, W1, ln_g, ln_b, W2):
            n = x.shape[0]
            agg = jax.ops.segment_sum(x[src], dst, num_segments=n)
            h = (1.0 + eps) * x + agg
            h = jax.nn.relu(layer_norm(h @ W1, ln_g, ln_b))
            return h @ W2
        key = jax.random.key(seed)
        ks = jax.random.split(key, 8)
        N, E, H, B = (50000, 50000, 256, 64)
        x = jax.random.normal(ks[0], (N, H), dtype=jnp.float32)
        edge_index = jax.random.randint(ks[1], (2, E), 0, N, dtype=jnp.int64)
        scale = 0.02
        return {'x': x, 'edge_index': edge_index, 'eps_down': jnp.zeros((), jnp.float32), 'W1_down': jax.random.normal(ks[2], (H, B), jnp.float32) * scale, 'lng_down': jnp.ones((B,), jnp.float32), 'lnb_down': jnp.zeros((B,), jnp.float32), 'W2_down': jax.random.normal(ks[3], (B, H), jnp.float32) * scale, 'eps_up': jnp.zeros((), jnp.float32), 'W1_up': jax.random.normal(ks[4], (H, B), jnp.float32) * scale, 'lng_up': jnp.ones((B,), jnp.float32), 'lnb_up': jnp.zeros((B,), jnp.float32), 'W2_up': jax.random.normal(ks[5], (B, H), jnp.float32) * scale, 'ln1_g': jnp.ones((H,), jnp.float32), 'ln1_b': jnp.zeros((H,), jnp.float32), 'ln2_g': jnp.ones((H,), jnp.float32), 'ln2_b': jnp.zeros((H,), jnp.float32), 'dir_emb': jax.random.normal(ks[6], (2, H), jnp.float32) * 0.02}
    _L0_gnn_all = _L0_gnn_setup()
    _L0_gnn_in = {k: v for k, v in _L0_gnn_all.items() if k in ('eps_down', 'W1_down', 'lng_down', 'lnb_down', 'W2_down', 'eps_up', 'W1_up', 'lng_up', 'lnb_up', 'W2_up', 'ln1_g', 'ln1_b', 'ln2_g', 'ln2_b', 'dir_emb')}
    del _L0_gnn_all

    def _L0_mix_setup():
        import jax, jax.numpy as jnp
        import numpy as np
        N, F, C, H = (32, 128, 256, 8)
        D = C // H
        EPS_ATTN = 1e-06
        EPS_LN = 1e-05

        def layer_norm(x, g, b):
            mu = jnp.mean(x, axis=-1, keepdims=True)
            var = jnp.var(x, axis=-1, keepdims=True)
            return (x - mu) * jax.lax.rsqrt(var + EPS_LN) * g + b
        key = jax.random.key(seed)
        ks = jax.random.split(key, 8)
        s = 1.0 / np.sqrt(C)
        return {'x': jax.random.normal(ks[0], (N, F, C), jnp.float32), 'Wqkv': jax.random.uniform(ks[1], (3 * C, C), jnp.float32, -s, s), 'ln1_g': jnp.ones((C,), jnp.float32), 'ln1_b': jnp.zeros((C,), jnp.float32), 'W1': jax.random.uniform(ks[2], (C, C), jnp.float32, -s, s), 'b1': jax.random.uniform(ks[3], (C,), jnp.float32, -s, s), 'W2': jax.random.uniform(ks[4], (C, C), jnp.float32, -s, s), 'b2': jax.random.uniform(ks[5], (C,), jnp.float32, -s, s), 'ln2_g': jnp.ones((C,), jnp.float32), 'ln2_b': jnp.zeros((C,), jnp.float32)}
    _L0_mix_all = _L0_mix_setup()
    _L0_mix_in = {k: v for k, v in _L0_mix_all.items() if k in ('Wqkv', 'ln1_g', 'ln1_b', 'W1', 'b1', 'W2', 'b2', 'ln2_g', 'ln2_b')}
    del _L0_mix_all

    def _L0_ffn_setup():
        import jax, jax.numpy as jnp
        import numpy as np
        E = 8
        K = 2
        D = 256
        H = 512
        DOUT = 256
        EPS = 1e-05
        key = jax.random.key(seed)
        ks = jax.random.split(key, 9)
        s = 0.02
        return {'x': jax.random.normal(ks[0], (4, 256, D), jnp.float32), 'gamma': 1.0 + 0.05 * jax.random.normal(ks[1], (D,), jnp.float32), 'beta': 0.05 * jax.random.normal(ks[2], (D,), jnp.float32), 'Wr': 0.01 * jax.random.normal(ks[3], (D, E), jnp.float32), 'br': jnp.zeros((E,), jnp.float32), 'W1': s * jax.random.normal(ks[4], (E, D, H), jnp.float32), 'b1': s * jax.random.normal(ks[5], (E, H), jnp.float32), 'W2': s * jax.random.normal(ks[6], (E, H, DOUT), jnp.float32), 'b2': s * jax.random.normal(ks[7], (E, DOUT), jnp.float32)}
    _L0_ffn_all = _L0_ffn_setup()
    _L0_ffn_in = {k: v for k, v in _L0_ffn_all.items() if k in ('gamma', 'beta', 'Wr', 'br', 'W1', 'b1', 'W2', 'b2')}
    del _L0_ffn_all

    def _L1_gnn_setup():
        import jax, jax.numpy as jnp
        import numpy as np
        N, E, D = (10000, 10000, 256)

        def _add_self_loops(src, dst, n):
            loop = jnp.arange(n, dtype=src.dtype)
            return (jnp.concatenate([src, loop]), jnp.concatenate([dst, loop]))

        def _gcn_conv(x, W, b, src, dst, n):
            xw = x @ W
            deg = jax.ops.segment_sum(jnp.ones(src.shape[0], x.dtype), dst, num_segments=n)
            dinv = jnp.where(deg > 0, jax.lax.rsqrt(deg), 0.0)
            norm = dinv[src] * dinv[dst]
            agg = jax.ops.segment_sum(xw[src] * norm[:, None], dst, num_segments=n)
            return agg + b

        def _gat_conv(x, W, a_src, a_dst, b, src, dst, n):
            xw = x @ W
            e = jax.nn.leaky_relu((xw @ a_src)[src] + (xw @ a_dst)[dst], 0.2)
            m = jax.ops.segment_max(e, dst, num_segments=n)
            ex = jnp.exp(e - m[dst])
            s = jax.ops.segment_sum(ex, dst, num_segments=n)
            alpha = ex / (s[dst] + 1e-16)
            agg = jax.ops.segment_sum(alpha[:, None] * xw[src], dst, num_segments=n)
            return agg + b
        key = jax.random.key(seed)
        ks = jax.random.split(key, 6)
        return {'event_emb': jax.random.normal(ks[0], (N, D), jnp.float32), 'edge_index': jax.random.randint(ks[1], (2, E), 0, N), 'W1': jax.random.normal(ks[2], (D, D), jnp.float32) / np.sqrt(D).astype(np.float32), 'b1': jnp.zeros((D,), jnp.float32), 'W2': jax.random.normal(ks[3], (D, D), jnp.float32) / np.sqrt(D).astype(np.float32), 'att_src': jax.random.normal(ks[4], (D,), jnp.float32) / np.sqrt(D).astype(np.float32), 'att_dst': jax.random.normal(ks[5], (D,), jnp.float32) / np.sqrt(D).astype(np.float32), 'b2': jnp.zeros((D,), jnp.float32)}
    _L1_gnn_all = _L1_gnn_setup()
    _L1_gnn_in = {k: v for k, v in _L1_gnn_all.items() if k in ('W1', 'b1', 'W2', 'att_src', 'att_dst', 'b2')}
    del _L1_gnn_all

    def _L1_mix_setup():
        import jax, jax.numpy as jnp
        import numpy as np
        NUM_HEADS = 8
        key = jax.random.key(seed)
        ks = jax.random.split(key, 5)
        B, N, C = (8, 512, 256)
        x = jax.random.normal(ks[0], (B, N, C), dtype=jnp.float32)
        Wq = jax.random.normal(ks[1], (C, C), dtype=jnp.float32) * 0.02
        Wkv = jax.random.normal(ks[2], (2 * C, C), dtype=jnp.float32) * 0.02
        Wproj = jax.random.normal(ks[3], (C, C), dtype=jnp.float32) * 0.02
        bproj = jnp.zeros((C,), dtype=jnp.float32)
        return {'x': x, 'Wq': Wq, 'Wkv': Wkv, 'Wproj': Wproj, 'bproj': bproj}
    _L1_mix_all = _L1_mix_setup()
    _L1_mix_in = {k: v for k, v in _L1_mix_all.items() if k in ('Wq', 'Wkv', 'Wproj', 'bproj')}
    del _L1_mix_all

    def _L1_ffn_setup():
        import jax, jax.numpy as jnp
        import numpy as np
        D_MODEL = 256
        N_EXPERTS = 16
        HIDDEN = 512
        SCALE = 0.02
        key = jax.random.key(seed)
        ks = jax.random.split(key, 5)
        x = jax.random.normal(ks[0], (4, 256, D_MODEL), dtype=jnp.float32)
        gate_w = jax.random.normal(ks[1], (D_MODEL, N_EXPERTS), dtype=jnp.float32) * SCALE
        gate_b = jnp.zeros((N_EXPERTS,), dtype=jnp.float32)
        w1 = jax.random.normal(ks[2], (N_EXPERTS, D_MODEL, HIDDEN), dtype=jnp.float32) * SCALE
        w2 = jax.random.normal(ks[3], (N_EXPERTS, D_MODEL, HIDDEN), dtype=jnp.float32) * SCALE
        w3 = jax.random.normal(ks[4], (N_EXPERTS, HIDDEN, D_MODEL), dtype=jnp.float32) * SCALE
        return {'x': x, 'gate_w': gate_w, 'gate_b': gate_b, 'w1': w1, 'w2': w2, 'w3': w3}
    _L1_ffn_all = _L1_ffn_setup()
    _L1_ffn_in = {k: v for k, v in _L1_ffn_all.items() if k in ('gate_w', 'gate_b', 'w1', 'w2', 'w3')}
    del _L1_ffn_all
    return {'x': x, 'src': src, 'dst': dst, 'L0_gnn_eps_down': _L0_gnn_in['eps_down'], 'L0_gnn_W1_down': _L0_gnn_in['W1_down'], 'L0_gnn_lng_down': _L0_gnn_in['lng_down'], 'L0_gnn_lnb_down': _L0_gnn_in['lnb_down'], 'L0_gnn_W2_down': _L0_gnn_in['W2_down'], 'L0_gnn_eps_up': _L0_gnn_in['eps_up'], 'L0_gnn_W1_up': _L0_gnn_in['W1_up'], 'L0_gnn_lng_up': _L0_gnn_in['lng_up'], 'L0_gnn_lnb_up': _L0_gnn_in['lnb_up'], 'L0_gnn_W2_up': _L0_gnn_in['W2_up'], 'L0_gnn_ln1_g': _L0_gnn_in['ln1_g'], 'L0_gnn_ln1_b': _L0_gnn_in['ln1_b'], 'L0_gnn_ln2_g': _L0_gnn_in['ln2_g'], 'L0_gnn_ln2_b': _L0_gnn_in['ln2_b'], 'L0_gnn_dir_emb': _L0_gnn_in['dir_emb'], 'L0_mix_Wqkv': _L0_mix_in['Wqkv'], 'L0_mix_ln1_g': _L0_mix_in['ln1_g'], 'L0_mix_ln1_b': _L0_mix_in['ln1_b'], 'L0_mix_W1': _L0_mix_in['W1'], 'L0_mix_b1': _L0_mix_in['b1'], 'L0_mix_W2': _L0_mix_in['W2'], 'L0_mix_b2': _L0_mix_in['b2'], 'L0_mix_ln2_g': _L0_mix_in['ln2_g'], 'L0_mix_ln2_b': _L0_mix_in['ln2_b'], 'L0_ffn_gamma': _L0_ffn_in['gamma'], 'L0_ffn_beta': _L0_ffn_in['beta'], 'L0_ffn_Wr': _L0_ffn_in['Wr'], 'L0_ffn_br': _L0_ffn_in['br'], 'L0_ffn_W1': _L0_ffn_in['W1'], 'L0_ffn_b1': _L0_ffn_in['b1'], 'L0_ffn_W2': _L0_ffn_in['W2'], 'L0_ffn_b2': _L0_ffn_in['b2'], 'L1_gnn_W1': _L1_gnn_in['W1'], 'L1_gnn_b1': _L1_gnn_in['b1'], 'L1_gnn_W2': _L1_gnn_in['W2'], 'L1_gnn_att_src': _L1_gnn_in['att_src'], 'L1_gnn_att_dst': _L1_gnn_in['att_dst'], 'L1_gnn_b2': _L1_gnn_in['b2'], 'L1_mix_Wq': _L1_mix_in['Wq'], 'L1_mix_Wkv': _L1_mix_in['Wkv'], 'L1_mix_Wproj': _L1_mix_in['Wproj'], 'L1_mix_bproj': _L1_mix_in['bproj'], 'L1_ffn_gate_w': _L1_ffn_in['gate_w'], 'L1_ffn_gate_b': _L1_ffn_in['gate_b'], 'L1_ffn_w1': _L1_ffn_in['w1'], 'L1_ffn_w2': _L1_ffn_in['w2'], 'L1_ffn_w3': _L1_ffn_in['w3']}

def reference(x, src, dst, L0_gnn_eps_down, L0_gnn_W1_down, L0_gnn_lng_down, L0_gnn_lnb_down, L0_gnn_W2_down, L0_gnn_eps_up, L0_gnn_W1_up, L0_gnn_lng_up, L0_gnn_lnb_up, L0_gnn_W2_up, L0_gnn_ln1_g, L0_gnn_ln1_b, L0_gnn_ln2_g, L0_gnn_ln2_b, L0_gnn_dir_emb, L0_mix_Wqkv, L0_mix_ln1_g, L0_mix_ln1_b, L0_mix_W1, L0_mix_b1, L0_mix_W2, L0_mix_b2, L0_mix_ln2_g, L0_mix_ln2_b, L0_ffn_gamma, L0_ffn_beta, L0_ffn_Wr, L0_ffn_br, L0_ffn_W1, L0_ffn_b1, L0_ffn_W2, L0_ffn_b2, L1_gnn_W1, L1_gnn_b1, L1_gnn_W2, L1_gnn_att_src, L1_gnn_att_dst, L1_gnn_b2, L1_mix_Wq, L1_mix_Wkv, L1_mix_Wproj, L1_mix_bproj, L1_ffn_gate_w, L1_ffn_gate_b, L1_ffn_w1, L1_ffn_w2, L1_ffn_w3):
    import jax
    import jax.numpy as jnp

    def _L0_gnn_ref(x, edge_index, eps_down, W1_down, lng_down, lnb_down, W2_down, eps_up, W1_up, lng_up, lnb_up, W2_up, ln1_g, ln1_b, ln2_g, ln2_b, dir_emb):
        import jax, jax.numpy as jnp
        import numpy as np
        LN_EPS = 1e-05

        def layer_norm(x, g, b):
            m = jnp.mean(x, axis=-1, keepdims=True)
            v = jnp.mean((x - m) ** 2, axis=-1, keepdims=True)
            return (x - m) * jax.lax.rsqrt(v + LN_EPS) * g + b

        def gin_conv(x, src, dst, eps, W1, ln_g, ln_b, W2):
            n = x.shape[0]
            agg = jax.ops.segment_sum(x[src], dst, num_segments=n)
            h = (1.0 + eps) * x + agg
            h = jax.nn.relu(layer_norm(h @ W1, ln_g, ln_b))
            return h @ W2
        src, dst = (edge_index[0], edge_index[1])
        h = gin_conv(x, src, dst, eps_down, W1_down, lng_down, lnb_down, W2_down)
        x = layer_norm(jax.nn.relu(h + x + dir_emb[0]), ln1_g, ln1_b)
        h = gin_conv(x, dst, src, eps_up, W1_up, lng_up, lnb_up, W2_up)
        x = layer_norm(jax.nn.relu(h + x + dir_emb[1]), ln2_g, ln2_b)
        return x

    def _L0_mix_ref(x, Wqkv, ln1_g, ln1_b, W1, b1, W2, b2, ln2_g, ln2_b):
        import jax, jax.numpy as jnp
        import numpy as np
        N, F, C, H = (32, 128, 256, 8)
        D = C // H
        EPS_ATTN = 1e-06
        EPS_LN = 1e-05

        def layer_norm(x, g, b):
            mu = jnp.mean(x, axis=-1, keepdims=True)
            var = jnp.var(x, axis=-1, keepdims=True)
            return (x - mu) * jax.lax.rsqrt(var + EPS_LN) * g + b
        n, f, c = x.shape
        qkv = jnp.einsum('nfc,oc->nfo', x, Wqkv)
        q, k, v = jnp.split(qkv, 3, axis=-1)
        q = q.reshape(n, f, H, D)
        k = k.reshape(n, f, H, D)
        v = v.reshape(n, f, H, D)
        q = jax.nn.elu(q) + 1.0
        k = jax.nn.elu(k) + 1.0
        kv = jnp.einsum('nshd,nshm->nhmd', k, v)
        ksum = jnp.sum(k, axis=1)
        z = 1.0 / (jnp.einsum('nlhd,nhd->nlh', q, ksum) + EPS_ATTN)
        t = jnp.einsum('nlhd,nhmd,nlh->nlhm', q, kv, z)
        t = t.reshape(n, f, c)
        x1 = layer_norm(t + x, ln1_g, ln1_b)
        h = jax.nn.gelu(jnp.einsum('nfc,oc->nfo', x1, W1) + b1, approximate=False)
        y = jnp.einsum('nfc,oc->nfo', h, W2) + b2
        return layer_norm(y + x1, ln2_g, ln2_b)

    def _L0_ffn_ref(x, gamma, beta, Wr, br, W1, b1, W2, b2):
        import jax, jax.numpy as jnp
        import numpy as np
        E = 8
        K = 2
        D = 256
        H = 512
        DOUT = 256
        EPS = 1e-05
        mu = jnp.mean(x, axis=-1, keepdims=True)
        var = jnp.mean(jnp.square(x - mu), axis=-1, keepdims=True)
        xn = (x - mu) * jax.lax.rsqrt(var + EPS) * gamma + beta
        logits = jnp.einsum('bsd,de->bse', xn, Wr) + br
        top_vals, top_idx = jax.lax.top_k(logits, K)
        w = jax.nn.softmax(top_vals, axis=-1)
        w_full = jnp.einsum('bsk,bske->bse', w, jax.nn.one_hot(top_idx, E, dtype=w.dtype))
        y = jnp.zeros(x.shape[:-1] + (DOUT,), x.dtype)
        for e in range(E):
            h = jax.nn.gelu(jnp.einsum('bsd,dh->bsh', xn, W1[e]) + b1[e], approximate=False)
            y_e = jnp.einsum('bsh,hd->bsd', h, W2[e]) + b2[e]
            y = y + y_e * w_full[..., e, None]
        return y

    def _L1_gnn_ref(event_emb, edge_index, W1, b1, W2, att_src, att_dst, b2):
        import jax, jax.numpy as jnp
        import numpy as np
        N, E, D = (10000, 10000, 256)

        def _add_self_loops(src, dst, n):
            loop = jnp.arange(n, dtype=src.dtype)
            return (jnp.concatenate([src, loop]), jnp.concatenate([dst, loop]))

        def _gcn_conv(x, W, b, src, dst, n):
            xw = x @ W
            deg = jax.ops.segment_sum(jnp.ones(src.shape[0], x.dtype), dst, num_segments=n)
            dinv = jnp.where(deg > 0, jax.lax.rsqrt(deg), 0.0)
            norm = dinv[src] * dinv[dst]
            agg = jax.ops.segment_sum(xw[src] * norm[:, None], dst, num_segments=n)
            return agg + b

        def _gat_conv(x, W, a_src, a_dst, b, src, dst, n):
            xw = x @ W
            e = jax.nn.leaky_relu((xw @ a_src)[src] + (xw @ a_dst)[dst], 0.2)
            m = jax.ops.segment_max(e, dst, num_segments=n)
            ex = jnp.exp(e - m[dst])
            s = jax.ops.segment_sum(ex, dst, num_segments=n)
            alpha = ex / (s[dst] + 1e-16)
            agg = jax.ops.segment_sum(alpha[:, None] * xw[src], dst, num_segments=n)
            return agg + b
        n = event_emb.shape[0]
        src, dst = _add_self_loops(edge_index[0], edge_index[1], n)
        x = jax.nn.relu(_gcn_conv(event_emb, W1, b1, src, dst, n))
        x = jax.nn.relu(_gat_conv(x, W2, att_src, att_dst, b2, src, dst, n))
        return x

    def _L1_mix_ref(x, Wq, Wkv, Wproj, bproj):
        import jax, jax.numpy as jnp
        import numpy as np
        NUM_HEADS = 8
        B, N, C = x.shape
        h = NUM_HEADS
        d = C // h
        q = jnp.einsum('bnc,oc->bno', x, Wq).reshape(B, N, h, d).transpose(0, 2, 1, 3)
        kv = jnp.einsum('bnc,oc->bno', x, Wkv).reshape(B, N, 2, h, d)
        k = kv[:, :, 0].transpose(0, 2, 1, 3)
        v = kv[:, :, 1].transpose(0, 2, 1, 3)
        q = jax.nn.elu(q) + 1.0
        k = jax.nn.elu(k) + 1.0
        k_sum = k.sum(axis=2)
        D_inv = 1.0 / jnp.maximum(jnp.einsum('bhnd,bhd->bhn', q, k_sum), 1e-06)
        context = jnp.einsum('bhnd,bhne->bhde', k, v)
        attn = jnp.einsum('bhnd,bhde->bhne', q, context) * D_inv[..., None]
        out = attn.transpose(0, 2, 1, 3).reshape(B, N, C)
        out = jnp.einsum('bnc,oc->bno', out, Wproj) + bproj
        return out

    def _L1_ffn_ref(x, gate_w, gate_b, w1, w2, w3):
        import jax, jax.numpy as jnp
        import numpy as np
        D_MODEL = 256
        N_EXPERTS = 16
        HIDDEN = 512
        SCALE = 0.02
        n_experts = w1.shape[0]
        logits = jnp.einsum('bsd,de->bse', x, gate_w) + gate_b
        probs = jax.nn.softmax(logits, axis=-1)
        top_probs, top_idx = jax.lax.top_k(probs, 2)
        top_probs = top_probs / jnp.sum(top_probs, axis=-1, keepdims=True)
        dispatch = jnp.sum(jax.nn.one_hot(top_idx, n_experts, dtype=x.dtype) * top_probs[..., None], axis=-2)
        h1 = jnp.einsum('bsd,edh->bseh', x, w1)
        h2 = jnp.einsum('bsd,edh->bseh', x, w2)
        hidden = jax.nn.silu(h1) * h2
        expert_out = jnp.einsum('bseh,eho->bseo', hidden, w3)
        return jnp.einsum('bseo,bse->bso', expert_out, dispatch)
    edge_index = jnp.stack([src, dst])
    xn = _layernorm(x, axis=-1)
    x = x + _L0_gnn_ref(xn, edge_index, L0_gnn_eps_down, L0_gnn_W1_down, L0_gnn_lng_down, L0_gnn_lnb_down, L0_gnn_W2_down, L0_gnn_eps_up, L0_gnn_W1_up, L0_gnn_lng_up, L0_gnn_lnb_up, L0_gnn_W2_up, L0_gnn_ln1_g, L0_gnn_ln1_b, L0_gnn_ln2_g, L0_gnn_ln2_b, L0_gnn_dir_emb) + _L0_mix_ref(xn[None], L0_mix_Wqkv, L0_mix_ln1_g, L0_mix_ln1_b, L0_mix_W1, L0_mix_b1, L0_mix_W2, L0_mix_b2, L0_mix_ln2_g, L0_mix_ln2_b)[0]
    x = x + _L0_ffn_ref(_layernorm(x, axis=-1)[None], L0_ffn_gamma, L0_ffn_beta, L0_ffn_Wr, L0_ffn_br, L0_ffn_W1, L0_ffn_b1, L0_ffn_W2, L0_ffn_b2)[0]
    xn = _layernorm(x, axis=-1)
    x = x + _L1_gnn_ref(xn, edge_index, L1_gnn_W1, L1_gnn_b1, L1_gnn_W2, L1_gnn_att_src, L1_gnn_att_dst, L1_gnn_b2) + _L1_mix_ref(xn[None], L1_mix_Wq, L1_mix_Wkv, L1_mix_Wproj, L1_mix_bproj)[0]
    x = x + _L1_ffn_ref(_layernorm(x, axis=-1)[None], L1_ffn_gate_w, L1_ffn_gate_b, L1_ffn_w1, L1_ffn_w2, L1_ffn_w3)[0]
    return x

_drawn_inputs = setup_inputs


def setup_inputs(seed=0):
    import zlib

    import numpy as np

    out = dict(_drawn_inputs(seed))
    spreads = {'L0_gnn_lng_down': (1.0, 0.6),
     'L0_gnn_lnb_down': (0.0, 0.8),
     'L0_gnn_lng_up': (1.0, 0.6),
     'L0_gnn_lnb_up': (0.0, 0.8),
     'L0_gnn_ln1_g': (1.0, 0.2),
     'L0_gnn_ln1_b': (0.0, 0.28),
     'L0_gnn_ln2_g': (1.0, 0.2),
     'L0_gnn_ln2_b': (0.0, 0.1),
     'L0_mix_ln1_g': (1.0, 0.2),
     'L0_mix_ln1_b': (0.0, 0.1),
     'L0_mix_ln2_g': (1.0, 0.2),
     'L0_mix_ln2_b': (0.0, 0.1),
     'L0_ffn_br': (0.0, 0.412),
     'L1_gnn_b1': (0.0, 0.629),
     'L1_gnn_b2': (0.0, 0.321),
     'L1_mix_bproj': (0.0, 0.1),
     'L1_ffn_gate_b': (0.0, 0.8)}
    factors = {'L0_gnn_dir_emb': 5.267,
     'L0_mix_Wqkv': 8.0,
     'L0_mix_b1': 8.0,
     'L0_mix_b2': 4.475,
     'L0_ffn_gamma': 8.0,
     'L0_ffn_beta': 8.0,
     'L0_ffn_Wr': 4.097,
     'L0_ffn_W1': 2.993,
     'L0_ffn_b1': 8.0,
     'L0_ffn_W2': 2.91,
     'L0_ffn_b2': 8.0,
     'L1_gnn_W1': 3.358,
     'L1_gnn_att_src': 8.0,
     'L1_gnn_att_dst': 8.0,
     'L1_mix_Wq': 8.0,
     'L1_mix_Wkv': 8.0,
     'L1_mix_Wproj': 8.0,
     'L1_ffn_gate_w': 8.0,
     'L1_ffn_w1': 8.0,
     'L1_ffn_w2': 8.0,
     'L1_ffn_w3': 8.0}
    for name, (base, spread) in spreads.items():
        noise = np.random.default_rng([zlib.crc32(name.encode()), seed]).standard_normal(out[name].shape)
        drawn = base * np.exp(spread * noise) if base else spread * noise
        out[name] = jnp.asarray(drawn.astype(out[name].dtype))
    for name, factor in factors.items():
        out[name] = (out[name] * factor).astype(out[name].dtype)
    return out
```

```python
from contextlib import ExitStack

import concourse.bass as bass
from concourse import mybir

F32 = mybir.dt.float32
BF16 = mybir.dt.bfloat16
F16 = mybir.dt.float16
I32 = mybir.dt.int32
ALU = mybir.AluOpType
ACT = mybir.ActivationFunctionType
AX = mybir.AxisListType

NODES = 3125
EDGES = 53125
C = 256
KC = C // 128
ROWS = 125
TILES = NODES // ROWS
GROUP = 5
GROUPS = TILES // GROUP
GROWS = GROUP * ROWS
HEADS = 8
HD = C // HEADS
HPB = 128 // HD
KVW = 128 + HPB
WIN = 25
WINS = NODES // WIN
WPT = ROWS // WIN
CH = 128
CHUNKS = -(-EDGES // CH)
CHUNKS_PAD = CHUNKS + 4
PAIRS_MAX = CHUNKS // 2 + 1
CHUNK_ROWS = 512
DMA_ROWS = 112
START = 1
LN_EPS = 1e-5
SPLIT = ((0, 500), (500, 625))


def rows_dma(eng, out, in_, sem):
    eng.dma_start(out[0:DMA_ROWS], in_[0:DMA_ROWS]).then_inc(sem, 16)
    eng.dma_start(out[DMA_ROWS:ROWS], in_[DMA_ROWS:ROWS]).then_inc(sem, 16)


class Memory:

    def __init__(self, nc, stack, stage):
        self.nc, self.stack, self.stage = nc, stack, stage
        self.sems, self.starts = [], []
        stack.callback(self.clear)
        self.tick = self.sem("tick")

    def sb(self, name, shape, dt=F32):
        return self.stack.enter_context(self.nc.sbuf_tensor(f"{self.stage}_{name}", list(shape), dt))

    def ps(self, name, shape=(128, 512), dt=F32):
        return self.stack.enter_context(self.nc.psum_tensor(f"{self.stage}_{name}", list(shape), dt))

    def sem(self, name, start=START):
        self.sems.append(self.nc.alloc_semaphore(f"{self.stage}_{name}"))
        self.starts.append(start)
        return self.sems[-1]

    def block(self):
        for sem, start in zip(self.sems, self.starts):
            if start:
                self.nc.gpsimd.sem_inc(sem, start)
        self.nc.all_engine_barrier()
        return self.stack.enter_context(self.nc.Block())

    def clear(self):
        self.nc.clear_and_free_semaphores(self.sems)


def carry(eng, m):
    eng.nop().then_inc(m.tick, 1)


def layer_norm_stats(dve, nc, src, stats, mv, var_eps, n):
    for u in range(n):
        nc.vector.bn_stats(stats[:, u, :], src(u))
    dve.drain()
    for u in range(n):
        nc.vector.bn_aggr(mv[:, u, :], stats[:, u, :])
    dve.drain()
    return nc.vector.tensor_scalar(var_eps[:], mv[:, :, 1], LN_EPS, None, ALU.add)


def split3(dve, nc, whole, rest, parts):
    nc.vector.tensor_copy(parts[0], whole)
    dve.drain()
    nc.vector.tensor_tensor(rest, whole, parts[0], ALU.subtract)
    dve.drain()
    nc.vector.tensor_copy(parts[1], rest)
    dve.drain()
    return nc.vector.tensor_tensor(parts[2], rest, parts[1], ALU.subtract)


def transpose_group(nc, K, rows, banks):
    for k in range(KC):
        for u in range(GROUP):
            out = banks[k][:, u * ROWS:(u + 1) * ROWS] if u < 4 else banks[2][:, k * ROWS:(k + 1) * ROWS]
            last = nc.tensor.transpose(out, rows[:, u, k * 128:(k + 1) * 128], K.ident_f[0:ROWS, 0:ROWS])
    return last


def copy_transposed(nc, dst, banks, fn=ACT.Copy, bias=None):
    for k in range(KC):
        more = {} if bias is None else {"bias": bias[:, k:k + 1]}
        nc.scalar.activation(dst[:, k, 0:4 * ROWS], banks[k][:, 0:4 * ROWS], fn, **more)
        last = nc.scalar.activation(dst[:, k, 4 * ROWS:GROWS], banks[2][:, k * ROWS:(k + 1) * ROWS], fn, **more)
    return last


def matmul_group(nc, banks, block, weight, xt):
    for lo, hi in SPLIT:
        out = banks[block][:, 0:4 * ROWS] if lo == 0 else banks[2][:, block * ROWS:(block + 1) * ROWS]
        for k in range(KC):
            last = nc.tensor.matmul(out, weight(k), xt[:, k, lo:hi], start=(k == 0), stop=(k == KC - 1))
    return last


def zero_bank(nc, K, bank, width, start):
    return nc.tensor.matmul(bank[:, 0:width], K.zeros[0:1, 0:128], K.zeros[0:1, 0:width],
                            start=start, stop=not start)


def two_by_two(eng, count, body):
    with eng.Fori(0, count // 2) as i:
        body(i * 2, 0, i)
        body(i * 2 + 1, 1, i)
    body(count - 1, 0, count // 2)


def constants(nc, K):
    with ExitStack() as st:
        m = Memory(nc, st, "const")
        zeroed = m.sem("zeroed")
        block = m.block()

        @block.gpsimd
        def _(pool):
            nc.gpsimd.memset(K.zeros[:], 0.0)
            nc.gpsimd.memset(K.ones[:], 1.0)
            nc.gpsimd.memset(K.ident_f[:], 0.0)
            nc.gpsimd.memset(K.ident_b[:], 0.0).then_inc(zeroed, 1)
            pool.wait_ge(zeroed, 1 + START)
            for ident in (K.ident_f, K.ident_b):
                nc.gpsimd.affine_select(out=ident[:], in_=ident[:], compare_op=ALU.not_equal, fill=1.0,
                                        base=0, pattern=[[-1, 128]], channel_multiplier=1)
            nc.gpsimd.iota(K.number_f[:], [[1, 128]], base=0, channel_multiplier=0,
                           allow_small_or_imprecise_dtypes=True)
            nc.gpsimd.iota(K.number_row[:], [[1, 128]], base=0, channel_multiplier=0,
                           allow_small_or_imprecise_dtypes=True)


def front(nc, K, stage, D, w_y, y_width, w_kv, w_q, y_scale):
    with ExitStack() as st:
        m = Memory(nc, st, stage)
        wy = m.sb("wy", (128, KC, y_width))
        wkv = m.sb("wkv", (128, KC, 2 * C))
        wq = m.sb("wq", (128, KC, C))
        stats, mv = m.sb("stats", (ROWS, GROUP, 6)), m.sb("mv", (ROWS, GROUP, 2))
        var_eps, std, rstd = (m.sb(n, (ROWS, GROUP)) for n in ("var_eps", "std", "rstd"))
        xn = m.sb("xn", (ROWS, GROUP, C))
        xt = m.sb("xt", (128, KC, GROWS))
        e_kv, r_kv = m.sb("e_kv", (ROWS, 2, C)), m.sb("r_kv", (ROWS, 2, C))
        key, val = m.sb("key", (ROWS, 2, C)), m.sb("val", (ROWS, 2, KC, 129))
        e_q, r_q = m.sb("e_q", (128, KC, GROWS)), m.sb("r_q", (128, KC, GROWS))
        y_rest = m.sb("y_rest", (ROWS, y_width))
        ps_t = [m.ps(f"ps_t{i}") for i in range(3)]
        ps_y = m.ps("ps_y")
        ps_kv = [m.ps(f"ps_kv{i}") for i in range(2)]
        ps_acc = [m.ps(f"ps_acc{i}") for i in range(KC)]
        w_in, x_in, var_ready, std_ready, xn_ready, xn_saved = (
            m.sem(n) for n in ("w_in", "x_in", "var_ready", "std_ready", "xn_ready", "xn_saved"))
        t_done, xt_ready, y_done, y_used, kv_done, kv_read, kv_exp, key_ready, key_used = (
            m.sem(n) for n in ("t_done", "xt_ready", "y_done", "y_used", "kv_done", "kv_read", "kv_exp",
                               "key_ready", "key_used"))
        q_done, q_read, q_used, sum_done = m.sem("q_done"), m.sem("q_read"), m.sem("q_used"), m.sem("sum_done")
        block = m.block()

        @block.sync
        def _(sp):
            sp.dma_start(wkv[:], w_kv.rearrange("(k p) o -> p k o", p=128)).then_inc(w_in, 16)
            sp.dma_start(wq[:], w_q.rearrange("(k p) o -> p k o", p=128)).then_inc(w_in, 16)
            sp.dma_start(wy[:], w_y.rearrange("(k p) o -> p k o", p=128)).then_inc(w_in, 16)
            if D is not None:
                rows_dma(sp, K.X, D.rearrange("(t p) c -> p t c", p=ROWS), x_in)
                sp.wait_ge(x_in, 32 + START)
            sp.wait_ge(w_in, 48 + START)

        @block.vector
        def _(dve):
            if D is not None:
                dve.wait_ge(x_in, 32 + START)
            nc.vector.memset(val[:], 1.0)
            nc.vector.memset(K.kv[:], 0.0)
            if y_width == 64:
                nc.vector.memset(K.Yp[:], 1.0)
            with dve.Fori(0, GROUPS) as g:
                layer_norm_stats(dve, nc, lambda u: K.X[:, g * GROUP + u, :], stats, mv, var_eps,
                                 GROUP).then_inc(var_ready, 1)
                dve.wait_ge(std_ready, g + 1 + START)
                nc.vector.reciprocal(rstd[:], std[:])
                dve.drain()
                dve.wait_ge(t_done, g + START)
                dve.wait_ge(xn_saved, g + START)
                for u in range(GROUP):
                    last = nc.vector.tensor_scalar(xn[:, u, :], K.X[:, g * GROUP + u, :], mv[:, u, 0:1],
                                                   rstd[:, u:u + 1], ALU.subtract, ALU.mult)
                last.then_inc(xn_ready, 1)
                for u in range(GROUP):
                    t = g * GROUP + u
                    dve.wait_ge(y_done, t + 1 + START)
                    y = K.Y[:, t, 0:y_width]
                    if y_scale is None:
                        nc.vector.tensor_copy(y, ps_y[0:ROWS, 0:y_width]).then_inc(y_used, 1)
                    else:
                        nc.vector.tensor_scalar(y, ps_y[0:ROWS, 0:y_width], y_scale[:, bass.ds(t, 1)], None,
                                                ALU.mult).then_inc(y_used, 1)
                    dve.drain()
                    split3(dve, nc, y, y_rest[:], [K.Yp[:, t, i * y_width:(i + 1) * y_width] for i in range(3)])
                    dve.wait_ge(kv_exp, t + 1 + START)
                    b = u % 2
                    nc.vector.scalar_tensor_tensor(key[:, b, :], e_kv[:, b, :], 1.0, r_kv[:, b, :],
                                                   ALU.min, ALU.add).then_inc(key_ready, 1)
                dve.wait_ge(q_read, g + 1 + START)
                for h in range(KC):
                    last = nc.vector.scalar_tensor_tensor(K.QT[:, h, bass.ds(g * GROWS, GROWS)],
                                                          e_q[:, h, :], 1.0, r_q[:, h, :], ALU.min, ALU.add)
                last.then_inc(q_used, 1)
            dve.wait_ge(sum_done, 1 + START)
            for h in range(KC):
                for a in range(HPB):
                    p = slice(HD * a, HD * a + HD)
                    nc.vector.tensor_copy(K.kv[p, h, HD * a:HD * a + HD], ps_acc[h][p, HD * a:HD * a + HD])
                    nc.vector.tensor_copy(K.kv[p, h, 128 + a:129 + a], ps_acc[h][p, 128:129])

        @block.gpsimd
        def _(pool):
            with pool.Fori(0, GROUPS) as g:
                pool.wait_ge(xn_ready, g + 1 + START)
                nc.gpsimd.tensor_copy(K.XN[:, bass.ds(g * GROUP, GROUP), :], xn[:]).then_inc(xn_saved, 1)

        @block.scalar
        def _(act):
            with act.Fori(0, GROUPS) as g:
                act.wait_ge(var_ready, g + 1 + START)
                nc.scalar.activation(std[:], var_eps[:], ACT.Sqrt).then_inc(std_ready, 1)
                act.wait_ge(t_done, g + 1 + START)
                copy_transposed(nc, xt, ps_t).then_inc(xt_ready, 1)
                for u in range(GROUP):
                    t = g * GROUP + u
                    b = u % 2
                    act.wait_ge(kv_done, t + 1 + START)
                    act.wait_ge(key_ready, (t if u == 0 else t - 1) + START)
                    act.wait_ge(key_used, (t if u == 0 else t - 1) + START)
                    nc.scalar.activation(e_kv[:, b, :], ps_kv[b][0:ROWS, 0:C], ACT.Exp)
                    nc.scalar.activation(r_kv[:, b, :], ps_kv[b][0:ROWS, 0:C], ACT.Relu)
                    nc.scalar.activation(val[:, b, :, 0:128],
                                         ps_kv[b][0:ROWS, C:2 * C].rearrange("p (k f) -> p k f", k=KC),
                                         ACT.Copy).then_inc(kv_exp, 1)
                act.wait_ge(q_done, g + 1 + START)
                act.wait_ge(q_used, g + START)
                for dst, fn in ((e_q, ACT.Exp), (r_q, ACT.Relu)):
                    last = copy_transposed(nc, dst, ps_t, fn)
                last.then_inc(q_read, 1)

        @block.tensor
        def _(pe):
            def key_value_sum(g, u):
                pe.wait_ge(key_ready, g * GROUP + u + 1 + START)
                for h in range(KC):
                    last = nc.tensor.matmul(ps_acc[h][:, 0:129], key[:, u % 2, h * 128:(h + 1) * 128],
                                            val[:, u % 2, h, :], start=False, stop=False)
                last.then_inc(key_used, 1)

            for h in range(KC):
                zero_bank(nc, K, ps_acc[h], 129, start=True)
            pe.wait_ge(w_in, 48 + START)
            with pe.Fori(0, GROUPS) as g:
                pe.wait_ge(xn_ready, g + 1 + START)
                pe.wait_ge(q_read, g + START)
                transpose_group(nc, K, xn, ps_t).then_inc(t_done, 1)
                pe.wait_ge(xt_ready, g + 1 + START)
                for u in range(GROUP):
                    t = g * GROUP + u
                    cols = slice(u * ROWS, (u + 1) * ROWS)
                    pe.wait_ge(y_used, t + START)
                    for k in range(KC):
                        last = nc.tensor.matmul(ps_y[0:ROWS, 0:y_width], xt[:, k, cols], wy[:, k, :],
                                                start=(k == 0), stop=(k == KC - 1))
                    last.then_inc(y_done, 1)
                    pe.wait_ge(kv_exp, (t if u == 0 else t - 1) + START)
                    for k in range(KC):
                        last = nc.tensor.matmul(ps_kv[u % 2][0:ROWS, :], xt[:, k, cols], wkv[:, k, :],
                                                start=(k == 0), stop=(k == KC - 1))
                    last.then_inc(kv_done, 1)
                    if u:
                        key_value_sum(g, u - 1)
                for h in range(KC):
                    last = matmul_group(nc, ps_t, h, lambda k: wq[:, k, h * 128:(h + 1) * 128], xt)
                last.then_inc(q_done, 1)
                key_value_sum(g, GROUP - 1)
            for h in range(KC):
                last = zero_bank(nc, K, ps_acc[h], 129, start=False)
            last.then_inc(sum_done, 1)


def mix_tail_l0(nc, K, D):
    with ExitStack() as st:
        m = Memory(nc, st, "mix0")
        w1, w2 = m.sb("w1", (128, KC, C)), m.sb("w2", (128, KC, C))
        b1 = m.sb("b1", (128, KC))
        vec = m.sb("vec", (ROWS, 5, C))
        stats, mv = m.sb("stats", (ROWS, GROUP, 6)), m.sb("mv", (ROWS, GROUP, 2))
        var_eps, std, rstd = (m.sb(n, (ROWS, GROUP)) for n in ("var_eps", "std", "rstd"))
        qt = m.sb("qt", (128, KC, GROWS))
        den = m.sb("den", (ROWS, GROUP, KC, HPB))
        att = m.sb("att", (ROWS, GROUP, C))
        x1 = m.sb("x1", (ROWS, GROUP, C))
        x1t, ht = m.sb("x1t", (128, KC, GROWS)), m.sb("ht", (128, KC, GROWS))
        ps_t = [m.ps(f"ps_t{i}") for i in range(3)]
        ps_a = [m.ps(f"ps_a{i}") for i in range(2)]
        ps_o = [m.ps(f"ps_o{i}") for i in range(2)]
        w_in, qt_ready, a_done, a_used, var_ready, std_ready = (
            m.sem(n) for n in ("w_in", "qt_ready", "a_done", "a_used", "var_ready", "std_ready"))
        x1_ready, t_done, x1t_ready, h_done, ht_ready, o_done, o_used = (
            m.sem(n) for n in ("x1_ready", "t_done", "x1t_ready", "h_done", "ht_ready", "o_done", "o_used"))
        block = m.block()

        @block.sync
        def _(sp):
            sp.dma_start(w1[:], D["L0_mix_W1"].rearrange("(k p) o -> p k o", p=128)).then_inc(w_in, 16)
            sp.dma_start(w2[:], D["L0_mix_W2"].rearrange("(k p) o -> p k o", p=128)).then_inc(w_in, 16)
            sp.dma_start(b1[:], D["L0_mix_b1"]).then_inc(w_in, 16)
            for n, name in enumerate(("ln1_g", "ln1_b", "ln2_g", "ln2_b", "b2")):
                sp.dma_start(vec[:, n, :], D["L0_mix_" + name].partition_broadcast(ROWS)).then_inc(w_in, 16)
            sp.wait_ge(w_in, 8 * 16 + START)

        @block.gpsimd
        def _(pool):
            with pool.Fori(0, GROUPS) as g:
                pool.wait_ge(a_done, g * GROUP + START)
                nc.gpsimd.tensor_copy(qt[:], K.QT[:, :, bass.ds(g * GROWS, GROWS)]).then_inc(qt_ready, 1)

        @block.vector
        def _(dve):
            def bc(n):
                return vec[:, n, :].unsqueeze(1).broadcast_to([ROWS, GROUP, C])

            def normalise(src, out, n):
                layer_norm_stats(dve, nc, lambda u: src[:, u, :], stats, mv, var_eps, GROUP).then_inc(var_ready, 1)
                dve.wait_ge(std_ready, g * 2 + 1 + n + START)
                nc.vector.reciprocal(rstd[:], std[:])
                dve.drain()
                for u in range(GROUP):
                    nc.vector.tensor_scalar(out[:, u, :], src[:, u, :], mv[:, u, 0:1], rstd[:, u:u + 1],
                                            ALU.subtract, ALU.mult)
                dve.drain()
                nc.vector.tensor_tensor(out[:], out[:], bc(2 * n), ALU.mult)
                dve.drain()
                return nc.vector.tensor_tensor(out[:], out[:], bc(2 * n + 1), ALU.add)

            dve.wait_ge(w_in, 8 * 16 + START)
            with dve.Fori(0, GROUPS) as g:
                for u in range(GROUP):
                    t = g * GROUP + u
                    dve.wait_ge(a_done, t + 1 + START)
                    a = ps_a[u % 2][0:ROWS, 0:KC * KVW].rearrange("p (k w) -> p k w", k=KC)
                    nc.vector.tensor_scalar(den[:, u], a[:, :, 128:KVW], 1e-6, None, ALU.add)
                    dve.drain()
                    nc.vector.reciprocal(den[:, u], den[:, u])
                    dve.drain()
                    for k in range(KC):
                        last = nc.vector.tensor_tensor(
                            att[:, u, k * 128:(k + 1) * 128].rearrange("p (a d) -> p a d", d=HD),
                            a[:, k, 0:128].rearrange("p (a d) -> p a d", d=HD),
                            den[:, u, k, :].unsqueeze(2).broadcast_to([ROWS, HPB, HD]), ALU.mult)
                    last.then_inc(a_used, 1)
                dve.drain()
                nc.vector.tensor_tensor(att[:], att[:], K.XN[:, bass.ds(g * GROUP, GROUP), :], ALU.add)
                dve.drain()
                normalise(att, x1, 0).then_inc(x1_ready, 1)
                for u in range(GROUP):
                    dve.wait_ge(o_done, g * GROUP + u + 1 + START)
                    nc.vector.tensor_tensor(att[:, u, :], ps_o[u % 2][0:ROWS, 0:C], x1[:, u, :],
                                            ALU.add).then_inc(o_used, 1)
                dve.drain()
                nc.vector.tensor_tensor(att[:], att[:], bc(4), ALU.add)
                dve.drain()
                normalise(att, x1, 1)
                dve.drain()
                nc.vector.tensor_tensor(K.X[:, bass.ds(g * GROUP, GROUP), :],
                                        K.X[:, bass.ds(g * GROUP, GROUP), :], x1[:], ALU.add)

        @block.scalar
        def _(act):
            act.wait_ge(w_in, 8 * 16 + START)
            with act.Fori(0, GROUPS) as g:
                act.wait_ge(var_ready, g * 2 + 1 + START)
                nc.scalar.activation(std[:], var_eps[:], ACT.Sqrt).then_inc(std_ready, 1)
                act.wait_ge(t_done, g + 1 + START)
                copy_transposed(nc, x1t, ps_t).then_inc(x1t_ready, 1)
                act.wait_ge(h_done, g + 1 + START)
                copy_transposed(nc, ht, ps_t, ACT.Gelu, b1).then_inc(ht_ready, 1)
                act.wait_ge(var_ready, g * 2 + 2 + START)
                nc.scalar.activation(std[:], var_eps[:], ACT.Sqrt).then_inc(std_ready, 1)

        @block.tensor
        def _(pe):
            pe.wait_ge(w_in, 8 * 16 + START)
            with pe.Fori(0, GROUPS) as g:
                pe.wait_ge(qt_ready, g + 1 + START)
                for u in range(GROUP):
                    t = g * GROUP + u
                    pe.wait_ge(a_used, (t if u == 0 else t - 1) + START)
                    for k in range(KC):
                        last = nc.tensor.matmul(ps_a[u % 2][0:ROWS, k * KVW:(k + 1) * KVW],
                                                qt[:, k, u * ROWS:(u + 1) * ROWS], K.kv[:, k, :],
                                                start=True, stop=True)
                    last.then_inc(a_done, 1)
                pe.wait_ge(x1_ready, g + 1 + START)
                pe.wait_ge(ht_ready, g + START)
                transpose_group(nc, K, x1, ps_t).then_inc(t_done, 1)
                pe.wait_ge(x1t_ready, g + 1 + START)
                for h in range(KC):
                    last = matmul_group(nc, ps_t, h, lambda k: w1[:, k, h * 128:(h + 1) * 128], x1t)
                last.then_inc(h_done, 1)
                pe.wait_ge(ht_ready, g + 1 + START)
                for u in range(GROUP):
                    t = g * GROUP + u
                    pe.wait_ge(o_used, (t if u == 0 else t - 1) + START)
                    for k in range(KC):
                        last = nc.tensor.matmul(ps_o[u % 2][0:ROWS, 0:C], ht[:, k, u * ROWS:(u + 1) * ROWS],
                                                w2[:, k, :], start=(k == 0), stop=(k == KC - 1))
                    last.then_inc(o_done, 1)


def build_adjacency(nc, K, D):
    with ExitStack() as st:
        m = Memory(nc, st, "adj")
        src_i, dst_i = m.sb("src_i", (CH, CHUNKS_PAD), I32), m.sb("dst_i", (CH, CHUNKS_PAD), I32)
        dst_rows_i = m.sb("dst_rows_i", (128, CHUNK_ROWS), I32)
        src_f, dst_f = m.sb("src_f", (CH, CHUNKS_PAD)), m.sb("dst_f", (CH, CHUNKS_PAD))
        dst_rows = m.sb("dst_rows", (128, 4, CH))
        hi = m.sb("hi", (CH, CHUNKS_PAD))
        low_all = m.sb("low", (CH, CHUNKS + 2 * PAIRS_MAX))
        key_all = m.sb("key", (CH, CHUNKS + 2 * PAIRS_MAX))
        low = low_all[:, 0:CHUNKS_PAD]
        key = key_all[:, 0:CHUNKS_PAD]
        hi_i = m.sb("hi_i", (CH, CHUNKS_PAD), I32)
        off = m.sb("off", (CH, CHUNKS_PAD))
        least, most = m.sb("least", (128, 4)), m.sb("most", (128, 4))
        win_first = m.sb("win_first", (128, WINS))
        chunk_no = m.sb("chunk_no", (128, 4))
        rank_up, rank_down = m.sb("rank_up", (128, 4)), m.sb("rank_down", (128, 4))
        here, here2 = m.sb("here", (128, 4, WINS)), m.sb("here2", (128, 4, WINS))
        span = m.sb("span", (128, 2, 4, WINS))
        span_all = m.sb("span_all", (128, 2, 4, WINS))
        ends = m.sb("ends", (1, 2, WINS))
        row = m.sb("row", (1, 4, WINS))
        table = m.sb("table", (1, 3, WINS), I32)
        key_row = m.sb("key_row", (CH, TILES * WIN), F16)
        win_key = m.sb("win_key", (CH, WINS))
        one_s = [m.sb(f"one_s{i}", (CH, ROWS), BF16) for i in range(2)]
        one_k = [m.sb(f"one_k{i}", (CH, TILES * WIN), BF16) for i in range(2)]
        adj = [m.sb(f"tile{i}", (ROWS, TILES, ROWS), BF16) for i in range(2)]
        adj_t = [m.sb(f"tile_t{i}", (ROWS, NODES), BF16) for i in range(2)]
        ps_w = [[m.ps(f"ps_w{i}{j}") for j in range(2)] for i in range(2)]
        ps_t = [m.ps(f"ps_t{i}", (128, 1024), BF16) for i in range(4)]
        e_in, made, span_ready, spread, table_ready = (
            m.sem(n) for n in ("e_in", "made", "span_ready", "spread", "table_ready"))
        one_ready, one_used, win_done, win_read, t_done, t_read, stored, tile_used = (
            m.sem(n) for n in ("one_ready", "one_used", "win_done", "win_read", "t_done", "t_read",
                               "stored", "tile_used"))
        block = m.block()

        @block.sync
        def _(sp):
            sp.dma_start(src_i[:], D["src_cols"]).then_inc(e_in, 16)
            sp.dma_start(dst_i[:], D["dst_cols"]).then_inc(e_in, 16)
            sp.dma_start(dst_rows_i[:], D["dst_rows"]).then_inc(e_in, 16)

            def store(t, b, i):
                sp.wait_ge(stored, t * 64 + START)
                sp.nop().then_inc(tile_used, 1)
                sp.wait_ge(win_read, t * WPT + WPT + START)
                rows_dma(sp, K.adj[bass.ds(t, 1)].rearrange("t p n -> (t p) n"),
                         adj[b][:].rearrange("p t d -> p (t d)"), stored)
                sp.wait_ge(t_read, t * 2 + 2 + START)
                rows_dma(sp, K.adj_t[bass.ds(t, 1)].rearrange("t p n -> (t p) n"), adj_t[b][:], stored)

            two_by_two(sp, TILES, store)
            sp.wait_ge(stored, TILES * 64 + START)

        @block.gpsimd
        def _(pool):
            nc.gpsimd.iota(key_row[:], [[1, TILES], [TILES, WIN]], base=0, channel_multiplier=0,
                           allow_small_or_imprecise_dtypes=True)
            nc.gpsimd.iota(win_first[:], [[WIN, WINS]], base=0, channel_multiplier=0,
                           allow_small_or_imprecise_dtypes=True)
            nc.gpsimd.iota(win_key[:], [[WIN * TILES, WINS]], base=0, channel_multiplier=0,
                           allow_small_or_imprecise_dtypes=True)
            nc.gpsimd.iota(chunk_no[:], [[1, 4]], base=0, channel_multiplier=4,
                           allow_small_or_imprecise_dtypes=True).then_inc(made, 1)
            pool.wait_ge(span_ready, 1 + START)
            nc.gpsimd.partition_all_reduce(span_all[:].rearrange("p a q w -> p (a q w)"),
                                           span[:].rearrange("p a q w -> p (a q w)"), 128,
                                           bass.bass_isa.ReduceOp.max).then_inc(spread, 1)

        @block.vector
        def _(dve):
            v = nc.vector
            dve.wait_ge(e_in, 48 + START)
            v.tensor_copy(src_f[:], src_i[:])
            v.tensor_copy(dst_f[:], dst_i[:])
            v.tensor_copy(dst_rows[:].rearrange("p q e -> p (q e)"), dst_rows_i[:])
            dve.drain()
            v.tensor_scalar(off[:], src_f[:], 0.5, 1.0 / ROWS, ALU.add, ALU.mult)
            dve.drain()
            v.tensor_copy(hi_i[:], off[:])
            dve.drain()
            v.tensor_copy(hi[:], hi_i[:])
            dve.drain()
            v.scalar_tensor_tensor(off[:], hi[:], float(ROWS), src_f[:], ALU.mult, ALU.is_gt)
            dve.drain()
            v.tensor_tensor(hi[:], hi[:], off[:], ALU.subtract)
            dve.drain()
            v.scalar_tensor_tensor(low, hi[:], -float(ROWS), src_f[:], ALU.mult, ALU.add)
            v.scalar_tensor_tensor(key, dst_f[:], float(TILES), hi[:], ALU.mult, ALU.add)
            v.tensor_reduce(least[:], dst_rows[:], AX.X, ALU.min)
            v.tensor_reduce(most[:], dst_rows[:], AX.X, ALU.max)
            dve.wait_ge(made, 1 + START)
            v.tensor_scalar(rank_up[:], chunk_no[:], 1.0, None, ALU.add)
            v.tensor_scalar(rank_down[:], chunk_no[:], -1.0, float(CHUNK_ROWS), ALU.mult, ALU.add)
            dve.drain()
            for q in range(4):
                v.tensor_scalar(here[:, q, :], win_first[:], float(WIN - 1), least[:, q:q + 1], ALU.add, ALU.is_ge)
                v.tensor_scalar(here2[:, q, :], win_first[:], most[:, q:q + 1], None, ALU.is_le)
            dve.drain()
            v.tensor_tensor(here[:], here[:], here2[:], ALU.mult)
            dve.drain()
            for q in range(4):
                v.tensor_scalar(span[:, 0, q, :], here[:, q, :], rank_up[:, q:q + 1], None, ALU.mult)
                last = v.tensor_scalar(span[:, 1, q, :], here[:, q, :], rank_down[:, q:q + 1], None, ALU.mult)
            last.then_inc(span_ready, 1)
            dve.wait_ge(spread, 1 + START)
            v.tensor_reduce(ends[:], span_all[0:1].rearrange("p a q w -> p a w q"), AX.X, ALU.max)
            dve.drain()
            v.tensor_scalar(row[:, 0, :], ends[:, 1, :], -1.0, float(CHUNK_ROWS), ALU.mult, ALU.add)
            dve.drain()
            v.tensor_scalar(row[:, 0, :], row[:, 0, :], float(CHUNKS), None, ALU.min)
            dve.drain()
            v.tensor_tensor(row[:, 1, :], ends[:, 0, :], row[:, 0, :], ALU.subtract)
            dve.drain()
            v.tensor_scalar(row[:, 1, :], row[:, 1, :], 3.0, 1.0, ALU.max, ALU.add)
            dve.drain()
            v.tensor_copy(table[:, 0:2, :], row[:, 0:2, :])
            dve.drain()
            v.tensor_scalar(table[:, 1, :], table[:, 1, :], 1, None, ALU.arith_shift_right)
            dve.drain()
            v.tensor_copy(row[:, 1, :], table[:, 1, :])
            v.memset(row[:, 3, :], 1.0)
            dve.drain()
            v.tensor_tensor_scan(row[:, 2, :], row[:, 3, :], row[:, 1, :], 0.0, ALU.mult, ALU.add)
            dve.drain()
            v.tensor_tensor(row[:, 2, :], row[:, 2, :], row[:, 1, :], ALU.subtract)
            dve.drain()
            v.tensor_copy(table[:, 2, :], row[:, 2, :]).then_inc(table_ready, 1)
            dve.wait_ge(table_ready, 1 + START)

            def tile(t, b, i):
                for w in range(WPT):
                    win = t * WPT + w
                    first = dve.value_load(table[:, 0, bass.ds(win, 1)], min_val=0, max_val=CHUNKS)
                    pairs = dve.value_load(table[:, 1, bass.ds(win, 1)], min_val=2, max_val=PAIRS_MAX)
                    before = dve.value_load(table[:, 2, bass.ds(win, 1)], min_val=0, max_val=WINS * PAIRS_MAX)
                    with dve.Fori(0, pairs) as n:
                        for j in range(2):
                            c = first + n * 2 + j
                            dve.wait_ge(one_used, (before + n) * 2 + j + 1 + START)
                            v.tensor_scalar(one_s[j][:], K.number_row[:, 0:ROWS], low_all[:, bass.ds(c, 1)],
                                            None, ALU.is_equal)
                            v.tensor_scalar(one_k[j][:], key_row[:], win_key[:, bass.ds(win, 1)],
                                            key_all[:, bass.ds(c, 1)], ALU.add, ALU.is_equal).then_inc(one_ready, 1)
                dve.wait_ge(t_done, t + 1 + START)
                dve.wait_ge(tile_used, t + START)
                for n in range(2):
                    last = v.tensor_copy(adj_t[b][:, n * 1000:(n + 1) * 1000].rearrange("p (u s) -> p u s", s=ROWS),
                                         ps_t[n][0:ROWS, :].rearrange("p (u s) -> p u s", s=128)[:, :, 0:ROWS])
                last.then_inc(t_read, 1)

            two_by_two(dve, TILES, tile)

        @block.scalar
        def _(act):
            def tile(t, b, i):
                for w in range(WPT):
                    win = t * WPT + w
                    act.wait_ge(win_done, win + 1 + START)
                    if w == 0:
                        act.wait_ge(tile_used, t + START)
                    for bank, (a, z) in enumerate(((0, 20), (20, 25))):
                        last = nc.scalar.activation(
                            adj[b][:, a:z, w * WIN:(w + 1) * WIN],
                            ps_w[w % 2][bank][0:ROWS, 0:(z - a) * WIN].rearrange("p (s d) -> p s d", d=WIN),
                            ACT.Copy)
                    last.then_inc(win_read, 1)
                act.wait_ge(t_done, t + 1 + START)
                nc.scalar.activation(adj_t[b][:, 2000:3000].rearrange("p (u s) -> p u s", s=ROWS),
                                     ps_t[2][0:ROWS, :].rearrange("p (u s) -> p u s", s=128)[:, :, 0:ROWS], ACT.Copy)
                nc.scalar.activation(adj_t[b][:, 3000:3125], ps_t[3][0:ROWS, 0:ROWS], ACT.Copy).then_inc(t_read, 1)

            two_by_two(act, TILES, tile)

        @block.tensor
        def _(pe):
            pe.nop().then_inc(one_used, 2)
            pe.wait_ge(table_ready, 1 + START)

            def tile(t, b, i):
                for w in range(WPT):
                    win = t * WPT + w
                    pairs = pe.value_load(table[:, 1, bass.ds(win, 1)], min_val=2, max_val=PAIRS_MAX)
                    before = pe.value_load(table[:, 2, bass.ds(win, 1)], min_val=0, max_val=WINS * PAIRS_MAX)
                    pe.wait_ge(win_read, (win if w == 0 else win - 1) + START)

                    def pair(n, start):
                        for j in range(2):
                            pe.wait_ge(one_ready, (before + n) * 2 + j + 1 + START)
                            for bank, (a, z) in enumerate(((0, 500), (500, 625))):
                                last = nc.tensor.matmul(ps_w[w % 2][bank][0:ROWS, 0:z - a], one_s[j][:],
                                                        one_k[j][:, a:z], start=start and j == 0, stop=False)
                            last.then_inc(one_used, 1)
                    pair(0, True)
                    with pe.Fori(1, pairs) as n:
                        pair(n, False)
                    for bank in range(2):
                        last = nc.tensor.matmul(ps_w[w % 2][bank][0:ROWS, 0:2], K.zeros[0:1, 0:ROWS],
                                                K.zeros[0:1, 0:2], start=False, stop=True)
                    last.then_inc(win_done, 1)
                pe.wait_ge(win_read, t * WPT + WPT + START)
                pe.wait_ge(t_read, t * 2 + START)
                for s in range(TILES):
                    last = nc.tensor.transpose(ps_t[s // 8][0:ROWS, (s % 8) * 128:(s % 8) * 128 + ROWS],
                                               adj[b][:, s, :], K.ident_b[0:ROWS, 0:ROWS])
                last.then_inc(t_done, 1)

            two_by_two(pe, TILES, tile)


def load_tiles(sp, buffers, source, arrived, used):
    def tile(t, b, i):
        sp.wait_ge(used, t + START)
        rows_dma(sp, buffers[b], source[bass.ds(t, 1)].rearrange("t p n -> (t p) n"), arrived[b])
    two_by_two(sp, TILES, tile)


def gin_down(nc, K):
    with ExitStack() as st:
        m = Memory(nc, st, "down")
        adj = [m.sb(f"adj{i}", (ROWS, TILES * ROWS), BF16) for i in range(2)]
        ps = [m.ps(f"ps{i}") for i in range(2)]
        arrived = [m.sem(f"in{i}") for i in range(2)]
        adj_used, done, used = m.sem("adj_used"), m.sem("done"), m.sem("used")
        block = m.block()

        @block.sync
        def _(sp):
            load_tiles(sp, adj, K.adj, arrived, done)

        @block.tensor
        def _(pe):
            pe.nop().then_inc(done, 1)

            def tile(t, b, i):
                pe.wait_ge(arrived[b], (i + 1) * 32 + START)
                pe.wait_ge(used, (t if b == 0 else t - 1) + START)
                for s in range(TILES):
                    last = nc.tensor.matmul(ps[b][0:ROWS, 0:193], adj[b][:, s * ROWS:(s + 1) * ROWS],
                                            K.Yp[:, s, 0:193], start=(s == 0), stop=(s == TILES - 1))
                last.then_inc(done, 1)
            two_by_two(pe, TILES, tile)

        @block.vector
        def _(dve):
            def tile(t, b, i):
                dve.wait_ge(done, t + 2 + START)
                nc.vector.tensor_reduce(K.AGG[:, t, :], ps[b][0:ROWS, 0:192].rearrange("p (i f) -> p f i", i=3),
                                        AX.X, ALU.add)
                nc.vector.tensor_copy(K.DEG[:, bass.ds(t, 1)], ps[b][0:ROWS, 192:193]).then_inc(used, 1)
            two_by_two(dve, TILES, tile)


def gin_up(nc, K):
    cuts = [(a, min(a + 500, NODES)) for a in range(0, NODES, 500)]
    with ExitStack() as st:
        m = Memory(nc, st, "up")
        adj_t = [m.sb(f"adj_t{i}", (ROWS, NODES), BF16) for i in range(2)]
        agg_t = m.sb("agg_t", (128, NODES))
        ps = [m.ps(f"ps{i}") for i in range(7)]
        arrived = [m.sem(f"in{i}") for i in range(2)]
        used, summed, moved, turned = m.sem("used"), m.sem("summed"), m.sem("moved"), m.sem("turned")
        block = m.block()

        @block.sync
        def _(sp):
            load_tiles(sp, adj_t, K.adj_t, arrived, used)

        @block.tensor
        def _(pe):
            pe.nop().then_inc(used, 1)
            for i, (a, z) in enumerate(cuts):
                zero_bank(nc, K, ps[i], z - a, start=True)

            def tile(t, b, i):
                pe.wait_ge(arrived[b], (i + 1) * 32 + START)
                for half in range(2):
                    for n, (a, z) in enumerate(cuts):
                        last = nc.tensor.matmul(ps[n][:, 0:z - a], K.Yp[:, t, half * 128:half * 128 + 128],
                                                adj_t[b][:, a:z], start=False, stop=False)
                last.then_inc(used, 1)
            two_by_two(pe, TILES, tile)
            for i, (a, z) in enumerate(cuts):
                last = zero_bank(nc, K, ps[i], z - a, start=False)
            last.then_inc(summed, 1)
            pe.wait_ge(moved, len(cuts) + START)
            for t in range(TILES):
                last = nc.tensor.transpose(ps[t // 4][0:ROWS, (t % 4) * 128:(t % 4) * 128 + 128],
                                           agg_t[:, t * ROWS:(t + 1) * ROWS], K.ident_f[:])
            last.then_inc(turned, 1)

        @block.scalar
        def _(act):
            act.wait_ge(summed, 1 + START)
            for i, (a, z) in enumerate(cuts):
                nc.scalar.activation(agg_t[:, a:z], ps[i][:, 0:z - a], ACT.Copy).then_inc(moved, 1)

        @block.vector
        def _(dve):
            dve.wait_ge(turned, 1 + START)
            for i in range(7):
                n = min(4, TILES - 4 * i)
                nc.vector.tensor_reduce(K.AGG[:, 4 * i:4 * i + n, :],
                                        ps[i][0:ROWS, 0:n * 128].rearrange("p (t i f) -> p t f i", i=2, f=64),
                                        AX.X, ALU.add)


def gin_tail(nc, K, stage, D, way, base, out):
    first = way == "down"
    with ExitStack() as st:
        m = Memory(nc, st, stage)
        w2 = m.sb("w2", (64, C))
        wy = m.sb("wy", (128, KC, 64))
        eps1 = m.sb("eps1", (ROWS, 1))
        narrow = m.sb("narrow", (ROWS, 2, 64))
        wide = m.sb("wide", (ROWS, 3, C))
        stats, mv = m.sb("stats", (ROWS, GROUP, 6)), m.sb("mv", (ROWS, GROUP, 2))
        var_eps, std, rstd = (m.sb(n, (ROWS, GROUP)) for n in ("var_eps", "std", "rstd"))
        hid = m.sb("hid", (ROWS, GROUP, 64))
        hid_t = m.sb("hid_t", (64, GROWS))
        row = m.sb("row", (ROWS, GROUP, C))
        xt = m.sb("xt", (128, KC, GROWS))
        rest = m.sb("rest", (ROWS, 64))
        ps_t = [m.ps(f"ps_t{i}") for i in range(3)]
        ps_h = [m.ps(f"ps_h{i}") for i in range(2)]
        ps_o = [m.ps(f"ps_o{i}") for i in range(2)]
        ps_y = m.ps("ps_y")
        w_in, var_ready, std_ready, hid_ready, h_done, hid_moved, o_done, o_used = (
            m.sem(n) for n in ("w_in", "var_ready", "std_ready", "hid_ready", "h_done", "hid_moved",
                               "o_done", "o_used"))
        row_ready, t_done, xt_ready, y_done, y_used = (
            m.sem(n) for n in ("row_ready", "t_done", "xt_ready", "y_done", "y_used"))
        block = m.block()
        loads = 8 if first else 7

        @block.sync
        def _(sp):
            g = "L0_gnn_"
            sp.dma_start(w2[:], D[g + "W2_" + way]).then_inc(w_in, 16)
            sp.dma_start(eps1[:], D[g + "eps_" + way].partition_broadcast(ROWS)).then_inc(w_in, 16)
            sp.dma_start(narrow[:, 0, :], D[g + "lng_" + way].partition_broadcast(ROWS)).then_inc(w_in, 16)
            sp.dma_start(narrow[:, 1, :], D[g + "lnb_" + way].partition_broadcast(ROWS)).then_inc(w_in, 16)
            n = "1" if first else "2"
            sp.dma_start(wide[:, 0, :], D[g + f"ln{n}_g"].partition_broadcast(ROWS)).then_inc(w_in, 16)
            sp.dma_start(wide[:, 1, :], D[g + f"ln{n}_b"].partition_broadcast(ROWS)).then_inc(w_in, 16)
            sp.dma_start(wide[:, 2, :], D[g + "dir_emb"][0 if first else 1].partition_broadcast(ROWS)).then_inc(w_in, 16)
            if first:
                sp.dma_start(wy[:], D[g + "W1_up"].rearrange("(k p) o -> p k o", p=128)).then_inc(w_in, 16)
            sp.wait_ge(w_in, loads * 16 + START)

        @block.vector
        def _(dve):
            v = nc.vector

            def normalise(buf, scale, shift, width, n, g):
                layer_norm_stats(dve, nc, lambda u: buf[:, u, :], stats, mv, var_eps, GROUP).then_inc(var_ready, 1)
                dve.wait_ge(std_ready, g * 2 + 1 + n + START)
                v.reciprocal(rstd[:], std[:])
                dve.drain()
                for u in range(GROUP):
                    v.tensor_scalar(buf[:, u, :], buf[:, u, :], mv[:, u, 0:1], rstd[:, u:u + 1],
                                    ALU.subtract, ALU.mult)
                dve.drain()
                v.tensor_tensor(buf[:], buf[:], scale.unsqueeze(1).broadcast_to([ROWS, GROUP, width]), ALU.mult)
                dve.drain()
                return v.tensor_tensor(buf[:], buf[:], shift.unsqueeze(1).broadcast_to([ROWS, GROUP, width]), ALU.add)

            dve.wait_ge(w_in, loads * 16 + START)
            v.tensor_scalar(eps1[:], eps1[:], 1.0, None, ALU.add)
            if first:
                v.memset(K.Yp[:, :, 192:256], 0.0)
            dve.drain()
            with dve.Fori(0, GROUPS) as g:
                tiles = bass.ds(g * GROUP, GROUP)
                dve.wait_ge(h_done, g + START)
                v.scalar_tensor_tensor(hid[:], K.Y[:, tiles, 0:64], eps1[:], K.AGG[:, tiles, :], ALU.mult, ALU.add)
                dve.drain()
                normalise(hid, narrow[:, 0, :], narrow[:, 1, :], 64, 0, g)
                dve.drain()
                v.tensor_scalar(hid[:], hid[:], 0.0, None, ALU.max).then_inc(hid_ready, 1)
                if first:
                    dve.wait_ge(t_done, g + START)
                for u in range(GROUP):
                    t = g * GROUP + u
                    dve.wait_ge(o_done, t + 1 + START)
                    v.tensor_tensor(row[:, u, :], ps_o[u % 2][0:ROWS, 0:C], base[:, t, :], ALU.add).then_inc(o_used, 1)
                dve.drain()
                v.tensor_tensor(row[:], row[:], wide[:, 2, :].unsqueeze(1).broadcast_to([ROWS, GROUP, C]), ALU.add)
                dve.drain()
                v.tensor_scalar(row[:], row[:], 0.0, None, ALU.max)
                dve.drain()
                last = normalise(row, wide[:, 0, :], wide[:, 1, :], C, 1, g)
                if first:
                    last.then_inc(row_ready, 1)
                    dve.drain()
                    v.tensor_copy(out[:, tiles, :], row[:])
                    for u in range(GROUP):
                        t = g * GROUP + u
                        dve.wait_ge(y_done, t + 1 + START)
                        carry(dve, m)
                        v.tensor_copy(K.Y[:, t, 0:64], ps_y[0:ROWS, 0:64]).then_inc(y_used, 1)
                        dve.drain()
                        split3(dve, nc, K.Y[:, t, 0:64], rest[:],
                               [K.Yp[:, t, i * 64:(i + 1) * 64] for i in range(3)])
                else:
                    dve.drain()
                    v.tensor_tensor(K.X[:, tiles, :], K.X[:, tiles, :], row[:], ALU.add)

        @block.scalar
        def _(act):
            with act.Fori(0, GROUPS) as g:
                act.wait_ge(var_ready, g * 2 + 1 + START)
                nc.scalar.activation(std[:], var_eps[:], ACT.Sqrt).then_inc(std_ready, 1)
                act.wait_ge(h_done, g + 1 + START)
                nc.scalar.activation(hid_t[:, 0:500], ps_h[0][0:64, 0:500], ACT.Copy)
                nc.scalar.activation(hid_t[:, 500:625], ps_h[1][0:64, 0:125], ACT.Copy).then_inc(hid_moved, 1)
                act.wait_ge(var_ready, g * 2 + 2 + START)
                nc.scalar.activation(std[:], var_eps[:], ACT.Sqrt).then_inc(std_ready, 1)
                if first:
                    act.wait_ge(t_done, g + 1 + START)
                    copy_transposed(nc, xt, ps_t).then_inc(xt_ready, 1)

        @block.tensor
        def _(pe):
            pe.wait_ge(w_in, loads * 16 + START)
            with pe.Fori(0, GROUPS) as g:
                pe.wait_ge(hid_ready, g + 1 + START)
                pe.wait_ge(hid_moved, g + START)
                carry(pe, m)
                for u in range(GROUP):
                    out_h = ps_h[0][0:64, u * ROWS:(u + 1) * ROWS] if u < 4 else ps_h[1][0:64, 0:ROWS]
                    last = nc.tensor.transpose(out_h, hid[:, u, :], K.ident_f[0:ROWS, 0:ROWS])
                last.then_inc(h_done, 1)
                pe.wait_ge(hid_moved, g + 1 + START)
                for u in range(GROUP):
                    t = g * GROUP + u
                    pe.wait_ge(o_used, (t if u == 0 else t - 1) + START)
                    nc.tensor.matmul(ps_o[u % 2][0:ROWS, 0:C], hid_t[:, u * ROWS:(u + 1) * ROWS], w2[:],
                                     start=True, stop=True).then_inc(o_done, 1)
                if first:
                    pe.wait_ge(row_ready, g + 1 + START)
                    pe.wait_ge(xt_ready, g + START)
                    transpose_group(nc, K, row, ps_t).then_inc(t_done, 1)
                    pe.wait_ge(xt_ready, g + 1 + START)
                    for u in range(GROUP):
                        t = g * GROUP + u
                        pe.wait_ge(y_used, t + START)
                        for k in range(KC):
                            last = nc.tensor.matmul(ps_y[0:ROWS, 0:64], xt[:, k, u * ROWS:(u + 1) * ROWS],
                                                    wy[:, k, :], start=(k == 0), stop=(k == KC - 1))
                        last.then_inc(y_done, 1)


class Experts:

    def __init__(self, layer):
        self.layer = layer
        self.n = 8 if layer == 0 else 16
        self.slot_tiles = 2 * NODES // 128 + self.n
        self.slot_tiles += 1 - self.slot_tiles % 2
        self.hidden = 512


def route(nc, K, D, X):
    E, L0 = X.n, X.layer == 0
    names = ("L0_ffn_Wr", "L0_ffn_br") if L0 else ("L1_ffn_gate_w", "L1_ffn_gate_b")
    with ExitStack() as st:
        m = Memory(nc, st, f"route{X.layer}")
        wr = m.sb("wr", (128, KC, E))
        bias = m.sb("bias", (ROWS, E))
        wide = m.sb("wide", (ROWS, 2, C))
        stats, mv = m.sb("stats", (ROWS, GROUP, 6)), m.sb("mv", (ROWS, GROUP, 2))
        var_eps, std, rstd = (m.sb(n, (ROWS, GROUP)) for n in ("var_eps", "std", "rstd"))
        row = m.sb("row", (ROWS, GROUP, C))
        xt = m.sb("xt", (128, KC, GROWS))
        logit = m.sb("logit", (ROWS, GROUP, E))
        top, top_at = m.sb("top", (ROWS, GROUP, 8)), m.sb("top_at", (ROWS, GROUP, 8), mybir.dt.uint32)
        at_f = m.sb("at_f", (ROWS, GROUP, 8))
        gap, grown, denom = (m.sb(n, (ROWS, GROUP)) for n in ("gap", "grown", "denom"))
        pick = m.sb("pick", (ROWS, TILES, 2, E))
        both = m.sb("both", (ROWS, TILES, E))
        below = m.sb("below", (ROWS, ROWS))
        keep = m.sb("keep", (ROWS, E, TILES))
        total = m.sb("total", (ROWS, E, TILES))
        run = m.sb("run", (ROWS, E, TILES))
        base = m.sb("base", (ROWS, 4, E))
        base_i = m.sb("base_i", (ROWS, E), I32)
        place = m.sb("place", (ROWS, TILES, E))
        picked = m.sb("picked", (ROWS, TILES, 2, E))
        slot_f = m.sb("slot_f", (ROWS, TILES, 2))
        tile_no = m.sb("tile_no", (ROWS, X.slot_tiles))
        passed = m.sb("passed", (1, X.slot_tiles, E))
        owner = m.sb("owner", (1, X.slot_tiles))
        node = m.sb("node", (ROWS, TILES), I32)
        slot_g, node_g = m.sb("slot_g", (ROWS, GROUP * 2), I32), m.sb("node_g", (ROWS, GROUP), I32)
        blank = m.sb("blank", (X.slot_tiles, 128), I32)
        ps_t = [m.ps(f"ps_t{i}") for i in range(3)]
        ps_l, ps_p, ps_s = m.ps("ps_l"), m.ps("ps_p"), m.ps("ps_s")
        w_in, var_ready, std_ready, row_ready, saved, t_done, xt_ready, l_done, l_used, gap_ready, grown_ready = (
            m.sem(n) for n in ("w_in", "var_ready", "std_ready", "row_ready", "saved", "t_done", "xt_ready",
                               "l_done", "l_used", "gap_ready", "grown_ready"))
        picks_ready, counted, slots_ready, made, blanked, copied = (
            m.sem(n) for n in ("picks_ready", "counted", "slots_ready", "made", "blanked", "copied"))
        scattered = m.sem("scattered", start=0)
        block = m.block()
        loads = 4 if L0 else 2
        norms = 2 if L0 else 1

        @block.sync
        def _(sp):
            sp.dma_start(wr[:], D[names[0]].rearrange("(k p) o -> p k o", p=128)).then_inc(w_in, 16)
            sp.dma_start(bias[:], D[names[1]].partition_broadcast(ROWS)).then_inc(w_in, 16)
            if L0:
                sp.dma_start(wide[:, 0, :], D["L0_ffn_gamma"].partition_broadcast(ROWS)).then_inc(w_in, 16)
                sp.dma_start(wide[:, 1, :], D["L0_ffn_beta"].partition_broadcast(ROWS)).then_inc(w_in, 16)
            sp.wait_ge(made, 1 + START)
            sp.dma_start(K.slot_row[0:X.slot_tiles * 128, :].rearrange("(t s) o -> t (s o)", s=128), blank[:]).then_inc(blanked, 16)
            with sp.Fori(0, GROUPS) as g:
                sp.wait_ge(row_ready, g + 1 + START)
                rows_dma(sp, K.rows_dram[bass.ds(g * GROUP, GROUP)].rearrange("t p c -> p t c"), row, saved)
            sp.wait_ge(saved, GROUPS * 32 + START)
            sp.wait_ge(w_in, loads * 16 + START)
            sp.wait_ge(blanked, 16 + START)

        @block.gpsimd
        def _(pool):
            nc.gpsimd.memset(below[:], 1.0).then_inc(copied, 1)
            pool.wait_ge(copied, 1 + START)
            nc.gpsimd.affine_select(out=below[:], in_=below[:], compare_op=ALU.is_gt, fill=0.0,
                                    base=0, pattern=[[1, ROWS]], channel_multiplier=-1)
            nc.gpsimd.iota(tile_no[:], [[128, X.slot_tiles]], base=0, channel_multiplier=0,
                           allow_small_or_imprecise_dtypes=True)
            nc.gpsimd.iota(node[:], [[ROWS, TILES]], base=0, channel_multiplier=1)
            nc.gpsimd.memset(blank[:], 0).then_inc(made, 1)
            pool.wait_ge(slots_ready, 1 + START)
            pool.wait_ge(blanked, 16 + START)
            with pool.Fori(0, GROUPS) as g:
                nc.gpsimd.tensor_copy(slot_g[:], K.slot[:, bass.ds(g * (GROUP * 2), GROUP * 2)])
                nc.gpsimd.tensor_copy(node_g[:], node[:, bass.ds(g * GROUP, GROUP)]).then_inc(copied, 1)
                pool.wait_ge(copied, g + 2 + START)
                carry(pool, m)
                for n in range(GROUP * 2):
                    nc.gpsimd.indirect_dma_start(
                        out=K.slot_row[:, :], out_offset=bass.IndirectOffsetOnAxis(ap=slot_g[:, n:n + 1], axis=0),
                        in_=node_g[:, n // 2:n // 2 + 1], in_offset=None).then_inc(scattered, 16)
                pool.wait_ge(scattered, (g + 1) * (GROUP * 2 * 16))

        @block.vector
        def _(dve):
            v = nc.vector

            def normalise(src, out, g, n):
                layer_norm_stats(dve, nc, src, stats, mv, var_eps, GROUP).then_inc(var_ready, 1)
                dve.wait_ge(std_ready, g * norms + n + 1 + START)
                v.reciprocal(rstd[:], std[:])
                dve.drain()
                for u in range(GROUP):
                    last = v.tensor_scalar(out[:, u, :], src(u), mv[:, u, 0:1], rstd[:, u:u + 1],
                                           ALU.subtract, ALU.mult)
                return last

            dve.wait_ge(w_in, loads * 16 + START)
            dve.wait_ge(made, 1 + START)
            with dve.Fori(0, GROUPS) as g:
                tiles = bass.ds(g * GROUP, GROUP)
                dve.wait_ge(t_done, g + START)
                dve.wait_ge(saved, g * 32 + START)
                last = normalise(lambda u: K.X[:, g * GROUP + u, :], row, g, 0)
                if L0:
                    dve.drain()
                    normalise(lambda u: row[:, u, :], row, g, 1)
                    dve.drain()
                    v.tensor_tensor(row[:], row[:], wide[:, 0, :].unsqueeze(1).broadcast_to([ROWS, GROUP, C]), ALU.mult)
                    dve.drain()
                    last = v.tensor_tensor(row[:], row[:], wide[:, 1, :].unsqueeze(1).broadcast_to([ROWS, GROUP, C]), ALU.add)
                last.then_inc(row_ready, 1)
                dve.wait_ge(l_done, g + 1 + START)
                v.tensor_tensor(logit[:], ps_l[0:ROWS, 0:GROUP * E].rearrange("p (u e) -> p u e", e=E),
                                bias[:].unsqueeze(1).broadcast_to([ROWS, GROUP, E]), ALU.add).then_inc(l_used, 1)
                dve.drain()
                for u in range(GROUP):
                    v.max(top[:, u, :], logit[:, u, :])
                dve.drain()
                for u in range(GROUP):
                    v.max_index(top_at[:, u, :], top[:, u, :], logit[:, u, :])
                v.tensor_tensor(gap[:], top[:, :, 1], top[:, :, 0], ALU.subtract).then_inc(gap_ready, 1)
                dve.drain()
                v.tensor_copy(at_f[:], top_at[:])
                dve.drain()
                for n in range(2):
                    v.tensor_tensor(pick[:, tiles, n, :],
                                    K.number_f[0:ROWS, 0:E].unsqueeze(1).broadcast_to([ROWS, GROUP, E]),
                                    at_f[:, :, n:n + 1].broadcast_to([ROWS, GROUP, E]), ALU.is_equal)
                dve.wait_ge(grown_ready, g + 1 + START)
                v.tensor_scalar(denom[:], grown[:], 1.0, None, ALU.add)
                dve.drain()
                v.reciprocal(denom[:], denom[:])
                dve.drain()
                v.tensor_copy(K.gate[:, tiles, 0], denom[:])
                v.tensor_tensor(K.gate[:, tiles, 1], grown[:], denom[:], ALU.mult)
                dve.drain()
            v.tensor_tensor(both[:], pick[:, :, 0, :], pick[:, :, 1, :], ALU.add).then_inc(picks_ready, 1)
            v.memset(keep[:], 1.0)
            dve.drain()
            v.memset(keep[:, :, 0:1], 0.0)
            dve.wait_ge(counted, 1 + START)
            v.tensor_copy(total[:], ps_s[0:ROWS, 0:TILES * E].rearrange("p (t e) -> p e t", e=E))
            dve.drain()
            v.tensor_tensor_scan(run[:].rearrange("p e t -> p (e t)"), keep[:].rearrange("p e t -> p (e t)"),
                                 total[:].rearrange("p e t -> p (e t)"), 0.0, ALU.mult, ALU.add)
            dve.drain()
            v.tensor_scalar(base[:, 0, :], run[:, :, TILES - 1], 127.0, None, ALU.add)
            v.tensor_tensor(total[:], run[:], total[:], ALU.subtract)
            dve.drain()
            v.tensor_copy(base_i[:], base[:, 0, :])
            dve.drain()
            v.tensor_scalar(base_i[:], base_i[:], 7, 7, ALU.arith_shift_right, ALU.logical_shift_left)
            dve.drain()
            v.tensor_copy(base[:, 0, :], base_i[:])
            v.memset(base[:, 1, :], 1.0)
            dve.drain()
            v.tensor_tensor_scan(base[:, 2, :], base[:, 1, :], base[:, 0, :], 0.0, ALU.mult, ALU.add)
            dve.drain()
            v.tensor_tensor(base[:, 3, :], base[:, 2, :], base[:, 0, :], ALU.subtract)
            v.tensor_tensor(place[:], ps_p[0:ROWS, 0:TILES * E].rearrange("p (t e) -> p t e", e=E),
                            total[:].rearrange("p e t -> p t e"), ALU.add)
            v.tensor_tensor(passed[:], tile_no[0:1].unsqueeze(2).broadcast_to([1, X.slot_tiles, E]),
                            base[0:1, 2, :].unsqueeze(1).broadcast_to([1, X.slot_tiles, E]), ALU.is_ge)
            dve.drain()
            v.tensor_tensor(place[:], place[:], base[:, 3, :].unsqueeze(1).broadcast_to([ROWS, TILES, E]), ALU.add)
            v.tensor_reduce(owner[:], passed[:], AX.X, ALU.add)
            dve.drain()
            v.tensor_scalar(K.owner[:, 0:X.slot_tiles], owner[:], float(E - 1), None, ALU.min)
            for n in range(2):
                v.tensor_tensor(picked[:, :, n, :], pick[:, :, n, :], place[:], ALU.mult)
            dve.drain()
            v.tensor_reduce(slot_f[:], picked[:], AX.X, ALU.add)
            dve.drain()
            v.tensor_copy(K.slot[:], slot_f[:].rearrange("p t n -> p (t n)")).then_inc(slots_ready, 1)

        @block.scalar
        def _(act):
            with act.Fori(0, GROUPS) as g:
                for n in range(norms):
                    act.wait_ge(var_ready, g * norms + n + 1 + START)
                    nc.scalar.activation(std[:], var_eps[:], ACT.Sqrt).then_inc(std_ready, 1)
                act.wait_ge(t_done, g + 1 + START)
                copy_transposed(nc, xt, ps_t).then_inc(xt_ready, 1)
                act.wait_ge(gap_ready, g + 1 + START)
                nc.scalar.activation(grown[:], gap[:], ACT.Exp).then_inc(grown_ready, 1)

        @block.tensor
        def _(pe):
            pe.wait_ge(w_in, loads * 16 + START)
            with pe.Fori(0, GROUPS) as g:
                pe.wait_ge(row_ready, g + 1 + START)
                pe.wait_ge(xt_ready, g + START)
                transpose_group(nc, K, row, ps_t).then_inc(t_done, 1)
                pe.wait_ge(xt_ready, g + 1 + START)
                pe.wait_ge(l_used, g + START)
                for u in range(GROUP):
                    for k in range(KC):
                        last = nc.tensor.matmul(ps_l[0:ROWS, u * E:(u + 1) * E], xt[:, k, u * ROWS:(u + 1) * ROWS],
                                                wr[:, k, :], start=(k == 0), stop=(k == KC - 1))
                last.then_inc(l_done, 1)
            pe.wait_ge(picks_ready, 1 + START)
            flat = both[:].rearrange("p t e -> p (t e)")
            nc.tensor.matmul(ps_p[0:ROWS, 0:TILES * E], below[:], flat, start=True, stop=True)
            nc.tensor.matmul(ps_s[0:ROWS, 0:TILES * E], K.ones[0:ROWS, 0:ROWS], flat, start=True, stop=True).then_inc(counted, 1)


def experts(nc, K, D, X):
    L0, H = X.layer == 0, X.hidden
    HB = H // 128
    with ExitStack() as st:
        m = Memory(nc, st, f"experts{X.layer}")
        idx = [m.sb(f"idx{i}", (128, 1), I32) for i in range(2)]
        rows = [m.sb(f"rows{i}", (128, C)) for i in range(2)]
        xt = [m.sb(f"xt{i}", (128, KC, 128)) for i in range(2)]
        w1 = [m.sb(f"w1_{i}", (128, KC, H)) for i in range(2)]
        w2 = [m.sb(f"w2_{i}", (128, KC, H)) for i in range(2)]
        w3 = [m.sb(f"w3_{i}", (128, HB, C)) for i in range(2)]
        b1 = [m.sb(f"b1_{i}", (128, HB)) for i in range(2)]
        b2 = [m.sb(f"b2_{i}", (128, C)) for i in range(2)]
        gate = [m.sb(f"gate{i}", (128, HB * 128)) for i in range(2)]
        hid = [m.sb(f"hid{i}", (128, HB * 128)) for i in range(2)]
        out = [m.sb(f"out{i}", (128, C)) for i in range(2)]
        ps_t = m.ps("ps_t")
        ps_h = [m.ps(f"ps_h{i}") for i in range(2)]
        ps_g = [m.ps(f"ps_g{i}") for i in range(2)]
        ps_o = [m.ps(f"ps_o{i}") for i in range(2)]
        idx_in, rows_in = ([m.sem(f"{n}{i}", start=0) for i in range(2)] for n in ("idx_in", "rows_in"))
        w_in, stored = ([m.sem(f"{n}{i}") for i in range(2)] for n in ("w_in", "stored"))
        rows_used, t_done, xt_ready, h_done, h_ready, hid_ready, o_done, out_ready = (
            m.sem(n) for n in ("rows_used", "t_done", "xt_ready", "h_done", "h_ready", "hid_ready",
                               "o_done", "out_ready"))
        block = m.block()
        w_loads = 4 if L0 else 3

        @block.sync
        def _(sp):
            def tile(t, b, i):
                e = sp.value_load(K.owner[:, bass.ds(t, 1)], min_val=0, max_val=X.n - 1)
                one = bass.ds(e, 1)
                sp.wait_ge(o_done, t + START)
                if L0:
                    sp.dma_start(w1[b][:], D["L0_ffn_W1"][one].rearrange("e (k p) h -> p (e k) h", p=128)).then_inc(w_in[b], 16)
                    sp.dma_start(b1[b][:], D["L0_ffn_b1"][one].rearrange("e p h -> p (e h)")).then_inc(w_in[b], 16)
                    sp.dma_start(w3[b][:], D["L0_ffn_W2"][one].rearrange("e (k p) h -> p (e k) h", p=128)).then_inc(w_in[b], 16)
                    sp.wait_ge(out_ready, t + START)
                    sp.dma_start(b2[b][:], D["L0_ffn_b2"][one].rearrange("e o -> (e o)").partition_broadcast(128)).then_inc(w_in[b], 16)
                else:
                    sp.dma_start(w1[b][:], D["L1_ffn_w1"][one].rearrange("e (k p) h -> p (e k) h", p=128)).then_inc(w_in[b], 16)
                    sp.dma_start(w2[b][:], D["L1_ffn_w2"][one].rearrange("e (k p) h -> p (e k) h", p=128)).then_inc(w_in[b], 16)
                    sp.dma_start(w3[b][:], D["L1_ffn_w3"][one].rearrange("e (k p) h -> p (e k) h", p=128)).then_inc(w_in[b], 16)
            two_by_two(sp, X.slot_tiles, tile)

        @block.gpsimd
        def _(pool):
            def tile(t, b, i):
                pool.wait_ge(rows_used, t + START)
                pool.dma_start(idx[b][:], K.slot_row[bass.ds(t * 128, 128), :]).then_inc(idx_in[b], 16)
                pool.wait_ge(idx_in[b], (i + 1) * 16)
                carry(pool, m)
                nc.gpsimd.indirect_dma_start(
                    out=rows[b][:], out_offset=None, in_=K.rows_dram.rearrange("t p c -> (t p) c"),
                    in_offset=bass.IndirectOffsetOnAxis(ap=idx[b][:, 0:1], axis=0)).then_inc(rows_in[b], 16)
            two_by_two(pool, X.slot_tiles, tile)

        @block.tensor
        def _(pe):
            pe.nop().then_inc(rows_used, 1)
            pe.nop().then_inc(o_done, 1)

            def tile(t, b, i):
                pe.wait_ge(rows_in[b], (i + 1) * 16)
                pe.wait_ge(xt_ready, t + START)
                for k in range(KC):
                    last = nc.tensor.transpose(ps_t[:, k * 128:(k + 1) * 128], rows[b][:, k * 128:(k + 1) * 128],
                                               K.ident_f[:])
                last.then_inc(rows_used, 1)
                pe.wait_ge(xt_ready, t + 1 + START)
                pe.wait_ge(w_in[b], (i + 1) * 16 * w_loads + START)
                pe.wait_ge(hid_ready, (t if b == 0 else t - 1) + START)
                for w, ps in ((w1, ps_h),) if L0 else ((w1, ps_h), (w2, ps_g)):
                    for h in range(HB):
                        for k in range(KC):
                            last = nc.tensor.matmul(ps[b][:, h * 128:(h + 1) * 128],
                                                    w[b][:, k, h * 128:(h + 1) * 128], xt[b][:, k, :],
                                                    start=(k == 0), stop=(k == KC - 1))
                last.then_inc(h_done, 1)
                pe.wait_ge(hid_ready, t + 1 + START)
                pe.wait_ge(out_ready, t + START)
                for h in range(HB):
                    last = nc.tensor.matmul(ps_o[b][:, 0:C], hid[b][:, h * 128:(h + 1) * 128], w3[b][:, h, :],
                                            start=(h == 0), stop=(h == HB - 1))
                last.then_inc(o_done, 1)
            two_by_two(pe, X.slot_tiles, tile)

        @block.scalar
        def _(act):
            def tile(t, b, i):
                act.wait_ge(rows_used, t + 2 + START)
                nc.scalar.activation(xt[b][:].rearrange("p k s -> p (k s)"), ps_t[:, 0:C], ACT.Copy).then_inc(xt_ready, 1)
                act.wait_ge(h_done, t + 1 + START)
                if L0:
                    for h in range(HB):
                        last = nc.scalar.activation(hid[b][:, h * 128:(h + 1) * 128], ps_h[b][:, h * 128:(h + 1) * 128],
                                                    ACT.Gelu, bias=b1[b][:, h:h + 1])
                    last.then_inc(hid_ready, 1)
                else:
                    act.wait_ge(hid_ready, (t if b == 0 else t - 1) + START)
                    nc.scalar.activation(gate[b][:], ps_h[b][:], ACT.Silu).then_inc(h_ready, 1)
                act.wait_ge(out_ready, t + 2 + START)
                act.dma_start(K.slot_out[bass.ds(t * 128, 128), :], out[b][:]).then_inc(stored[b], 16)
            two_by_two(act, X.slot_tiles, tile)
            act.wait_ge(stored[0], (X.slot_tiles // 2 + 1) * 16 + START)
            act.wait_ge(stored[1], (X.slot_tiles // 2) * 16 + START)

        @block.vector
        def _(dve):
            dve.nop().then_inc(out_ready, 1)

            def tile(t, b, i):
                if not L0:
                    dve.wait_ge(h_ready, t + 1 + START)
                    nc.vector.tensor_tensor(hid[b][:], gate[b][:], ps_g[b][:], ALU.mult).then_inc(hid_ready, 1)
                dve.wait_ge(o_done, t + 2 + START)
                dve.wait_ge(stored[b], i * 16 + START)
                if L0:
                    nc.vector.tensor_tensor(out[b][:], ps_o[b][:, 0:C], b2[b][:], ALU.add).then_inc(out_ready, 1)
                else:
                    nc.vector.tensor_copy(out[b][:], ps_o[b][:, 0:C]).then_inc(out_ready, 1)
            two_by_two(dve, X.slot_tiles, tile)


def combine(nc, K, X, result):
    with ExitStack() as st:
        m = Memory(nc, st, f"combine{X.layer}")
        slot_g = m.sb("slot_g", (ROWS, GROUP * 2), I32)
        got = m.sb("got", (ROWS, GROUP * 2, C))
        copied, added, stored = m.sem("copied"), m.sem("added"), m.sem("stored")
        gathered = m.sem("gathered", start=0)
        block = m.block()

        @block.gpsimd
        def _(pool):
            with pool.Fori(0, GROUPS) as g:
                pool.wait_ge(added, g + START)
                nc.gpsimd.tensor_copy(slot_g[:], K.slot[:, bass.ds(g * (GROUP * 2), GROUP * 2)]).then_inc(copied, 1)
                pool.wait_ge(copied, g + 1 + START)
                carry(pool, m)
                for n in range(GROUP * 2):
                    nc.gpsimd.indirect_dma_start(
                        out=got[:, n, :], out_offset=None, in_=K.slot_out[0:X.slot_tiles * 128, :],
                        in_offset=bass.IndirectOffsetOnAxis(ap=slot_g[:, n:n + 1], axis=0)).then_inc(gathered, 16)

        @block.vector
        def _(dve):
            with dve.Fori(0, GROUPS) as g:
                dve.wait_ge(gathered, (g + 1) * (GROUP * 2 * 16))
                for n in range(2):
                    for u in range(GROUP):
                        t = g * GROUP + u
                        last = nc.vector.scalar_tensor_tensor(K.X[:, t, :], got[:, 2 * u + n, :],
                                                              K.gate[:, t, n:n + 1], K.X[:, t, :],
                                                              ALU.mult, ALU.add)
                    if n == 0:
                        dve.drain()
                last.then_inc(added, 1)

        @block.sync
        def _(sp):
            if result is not None:
                view = result.rearrange("(t p) c -> p t c", p=ROWS)
                with sp.Fori(0, GROUPS) as g:
                    sp.wait_ge(added, g + 1 + START)
                    tiles = bass.ds(g * GROUP, GROUP)
                    for a, z in ((0, DMA_ROWS), (DMA_ROWS, ROWS)):
                        sp.dma_start(view[a:z, tiles, :], K.X[a:z, tiles, :]).then_inc(stored, 16)
                sp.wait_ge(stored, GROUPS * 32 + START)


def degree_scale(nc, K):
    with ExitStack() as st:
        m = Memory(nc, st, "degree")
        deg = m.sb("deg", (ROWS, TILES))
        ready, rooted = m.sem("ready"), m.sem("rooted")
        block = m.block()

        @block.vector
        def _(dve):
            nc.vector.tensor_scalar(deg[:], K.DEG[:], 1.0, None, ALU.add).then_inc(ready, 1)
            dve.wait_ge(rooted, 1 + START)
            nc.vector.reciprocal(K.DINV[:], K.DINV[:])

        @block.scalar
        def _(act):
            act.wait_ge(ready, 1 + START)
            nc.scalar.activation(K.DINV[:], deg[:], ACT.Sqrt).then_inc(rooted, 1)


def mix_tail_l1(nc, K, D):
    with ExitStack() as st:
        m = Memory(nc, st, "mix1")
        w = m.sb("w", (128, KC, C))
        bias = m.sb("bias", (ROWS, C))
        qt = m.sb("qt", (128, KC, GROWS))
        den = m.sb("den", (ROWS, GROUP, KC, HPB))
        att = m.sb("att", (ROWS, GROUP, C))
        att_t = m.sb("att_t", (128, KC, GROWS))
        ps_t = [m.ps(f"ps_t{i}") for i in range(3)]
        ps_a = [m.ps(f"ps_a{i}") for i in range(2)]
        ps_o = [m.ps(f"ps_o{i}") for i in range(2)]
        w_in, qt_ready, a_done, a_used, att_ready, t_done, att_t_ready, o_done, o_used = (
            m.sem(n) for n in ("w_in", "qt_ready", "a_done", "a_used", "att_ready", "t_done", "att_t_ready",
                               "o_done", "o_used"))
        block = m.block()

        @block.sync
        def _(sp):
            sp.dma_start(w[:], D["L1_mix_Wproj"].rearrange("(k p) o -> p k o", p=128)).then_inc(w_in, 16)
            sp.dma_start(bias[:], D["L1_mix_bproj"].partition_broadcast(ROWS)).then_inc(w_in, 16)
            sp.wait_ge(w_in, 32 + START)

        @block.gpsimd
        def _(pool):
            with pool.Fori(0, GROUPS) as g:
                pool.wait_ge(a_done, g * GROUP + START)
                nc.gpsimd.tensor_copy(qt[:], K.QT[:, :, bass.ds(g * GROWS, GROWS)]).then_inc(qt_ready, 1)

        @block.vector
        def _(dve):
            dve.wait_ge(w_in, 32 + START)
            with dve.Fori(0, GROUPS) as g:
                dve.wait_ge(t_done, g + START)
                for u in range(GROUP):
                    t = g * GROUP + u
                    dve.wait_ge(a_done, t + 1 + START)
                    a = ps_a[u % 2][0:ROWS, 0:KC * KVW].rearrange("p (k w) -> p k w", k=KC)
                    nc.vector.tensor_scalar(den[:, u], a[:, :, 128:KVW], 1e-6, None, ALU.max)
                    dve.drain()
                    nc.vector.reciprocal(den[:, u], den[:, u])
                    dve.drain()
                    for k in range(KC):
                        last = nc.vector.tensor_tensor(
                            att[:, u, k * 128:(k + 1) * 128].rearrange("p (a d) -> p a d", d=HD),
                            a[:, k, 0:128].rearrange("p (a d) -> p a d", d=HD),
                            den[:, u, k, :].unsqueeze(2).broadcast_to([ROWS, HPB, HD]), ALU.mult)
                    last.then_inc(a_used, 1)
                dve.drain()
                dve.nop().then_inc(att_ready, 1)
                tiles = bass.ds(g * GROUP, GROUP)
                nc.vector.tensor_tensor(K.X[:, tiles, :], K.X[:, tiles, :],
                                        bias[:].unsqueeze(1).broadcast_to([ROWS, GROUP, C]), ALU.add)
                dve.drain()
                for u in range(GROUP):
                    t = g * GROUP + u
                    dve.wait_ge(o_done, t + 1 + START)
                    nc.vector.tensor_tensor(K.X[:, t, :], ps_o[u % 2][0:ROWS, 0:C], K.X[:, t, :],
                                            ALU.add).then_inc(o_used, 1)

        @block.scalar
        def _(act):
            with act.Fori(0, GROUPS) as g:
                act.wait_ge(t_done, g + 1 + START)
                copy_transposed(nc, att_t, ps_t).then_inc(att_t_ready, 1)

        @block.tensor
        def _(pe):
            pe.wait_ge(w_in, 32 + START)
            with pe.Fori(0, GROUPS) as g:
                pe.wait_ge(qt_ready, g + 1 + START)
                for u in range(GROUP):
                    t = g * GROUP + u
                    pe.wait_ge(a_used, (t if u == 0 else t - 1) + START)
                    for k in range(KC):
                        last = nc.tensor.matmul(ps_a[u % 2][0:ROWS, k * KVW:(k + 1) * KVW],
                                                qt[:, k, u * ROWS:(u + 1) * ROWS], K.kv[:, k, :],
                                                start=True, stop=True)
                    last.then_inc(a_done, 1)
                pe.wait_ge(att_ready, g + 1 + START)
                pe.wait_ge(att_t_ready, g + START)
                transpose_group(nc, K, att, ps_t).then_inc(t_done, 1)
                pe.wait_ge(att_t_ready, g + 1 + START)
                for u in range(GROUP):
                    t = g * GROUP + u
                    pe.wait_ge(o_used, (t if u == 0 else t - 1) + START)
                    for k in range(KC):
                        last = nc.tensor.matmul(ps_o[u % 2][0:ROWS, 0:C], att_t[:, k, u * ROWS:(u + 1) * ROWS],
                                                w[:, k, :], start=(k == 0), stop=(k == KC - 1))
                    last.then_inc(o_done, 1)


def gcn(nc, K, D):
    with ExitStack() as st:
        m = Memory(nc, st, "gcn")
        adj = [m.sb(f"adj{i}", (ROWS, TILES * ROWS), BF16) for i in range(2)]
        bias = m.sb("bias", (ROWS, C))
        acc = m.sb("acc", (ROWS, C))
        ps_a = [m.ps(f"ps_a{i}") for i in range(2)]
        ps_b = [m.ps(f"ps_b{i}") for i in range(2)]
        arrived = [m.sem(f"in{i}") for i in range(2)]
        b_in, done, used = m.sem("b_in"), m.sem("done"), m.sem("used")
        block = m.block()

        @block.sync
        def _(sp):
            sp.dma_start(bias[:], D["L1_gnn_b1"].partition_broadcast(ROWS)).then_inc(b_in, 16)
            load_tiles(sp, adj, K.adj, arrived, done)

        @block.tensor
        def _(pe):
            pe.nop().then_inc(done, 1)

            def tile(t, b, i):
                pe.wait_ge(arrived[b], (i + 1) * 32 + START)
                pe.wait_ge(used, (t if b == 0 else t - 1) + START)
                for s in range(TILES):
                    w = adj[b][:, s * ROWS:(s + 1) * ROWS]
                    nc.tensor.matmul(ps_a[b][0:ROWS, :], w, K.Yp[:, s, 0:512], start=(s == 0), stop=(s == TILES - 1))
                    last = nc.tensor.matmul(ps_b[b][0:ROWS, 0:C], w, K.Yp[:, s, 512:768],
                                            start=(s == 0), stop=(s == TILES - 1))
                last.then_inc(done, 1)
            two_by_two(pe, TILES, tile)

        @block.vector
        def _(dve):
            dve.wait_ge(b_in, 16 + START)

            def tile(t, b, i):
                dve.wait_ge(done, t + 2 + START)
                nc.vector.tensor_tensor(acc[:], ps_a[b][0:ROWS, 0:C], K.Y[:, t, :], ALU.add)
                dve.drain()
                nc.vector.tensor_tensor(acc[:], acc[:], ps_a[b][0:ROWS, C:2 * C], ALU.add)
                dve.drain()
                nc.vector.tensor_tensor(acc[:], acc[:], ps_b[b][0:ROWS, 0:C], ALU.add).then_inc(used, 1)
                dve.drain()
                nc.vector.scalar_tensor_tensor(acc[:], acc[:], K.DINV[:, bass.ds(t, 1)], bias[:], ALU.mult, ALU.add)
                dve.drain()
                nc.vector.tensor_scalar(K.XN[:, t, :], acc[:], 0.0, None, ALU.max)
                dve.drain()
            two_by_two(dve, TILES, tile)


def gat_project(nc, K, D):
    with ExitStack() as st:
        m = Memory(nc, st, "gatp")
        w = m.sb("w", (128, KC, C))
        vec = m.sb("vec", (ROWS, 2, C))
        row = m.sb("row", (ROWS, GROUP, C))
        xt = m.sb("xt", (128, KC, GROWS))
        prod, dots = m.sb("prod", (ROWS, 2, C)), m.sb("dots", (ROWS, 2, GROUP))
        y = m.sb("y", (ROWS, GROUP, C))
        at_src = m.sb("at_src", (ROWS, TILES))
        line = m.sb("line", (TILES, ROWS))
        ps_t = [m.ps(f"ps_t{i}") for i in range(3)]
        ps_y = [m.ps(f"ps_y{i}") for i in range(2)]
        w_in, row_ready, t_done, xt_ready, y_done, y_used, src_ready, turned, line_ready, line_out, spread = (
            m.sem(n) for n in ("w_in", "row_ready", "t_done", "xt_ready", "y_done", "y_used", "src_ready",
                               "turned", "line_ready", "line_out", "spread"))
        block = m.block()

        @block.sync
        def _(sp):
            sp.dma_start(w[:], D["L1_gnn_W2"].rearrange("(k p) o -> p k o", p=128)).then_inc(w_in, 16)
            sp.dma_start(vec[:, 0, :], D["L1_gnn_att_src"].partition_broadcast(ROWS)).then_inc(w_in, 16)
            sp.dma_start(vec[:, 1, :], D["L1_gnn_att_dst"].partition_broadcast(ROWS)).then_inc(w_in, 16)
            sp.wait_ge(w_in, 48 + START)
            sp.wait_ge(line_ready, 1 + START)
            sp.dma_start(K.src_line, line[:]).then_inc(line_out, 16)
            sp.wait_ge(line_out, 16 + START)
            sp.dma_start(K.SRC[:], K.src_line.rearrange("t p -> (t p)").partition_broadcast(ROWS)).then_inc(spread, 16)
            sp.wait_ge(spread, 16 + START)

        @block.gpsimd
        def _(pool):
            with pool.Fori(0, GROUPS) as g:
                pool.wait_ge(t_done, g + START)
                nc.gpsimd.tensor_copy(row[:], K.XN[:, bass.ds(g * GROUP, GROUP), :]).then_inc(row_ready, 1)

        @block.scalar
        def _(act):
            with act.Fori(0, GROUPS) as g:
                act.wait_ge(t_done, g + 1 + START)
                copy_transposed(nc, xt, ps_t).then_inc(xt_ready, 1)

        @block.vector
        def _(dve):
            dve.wait_ge(w_in, 48 + START)
            with dve.Fori(0, GROUPS) as g:
                for u in range(GROUP):
                    t = g * GROUP + u
                    dve.wait_ge(y_done, t + 1 + START)
                    nc.vector.tensor_copy(y[:, u, :], ps_y[u % 2][0:ROWS, 0:C]).then_inc(y_used, 1)
                    dve.drain()
                    for n in range(2):
                        nc.vector.tensor_tensor_reduce(out=prod[:, n, :], in0=y[:, u, :], in1=vec[:, n, :], scale=1.0,
                                                       scalar=0.0, op0=ALU.mult, op1=ALU.add,
                                                       accum_out=dots[:, n, u:u + 1])
                    dve.drain()
                tiles = bass.ds(g * GROUP, GROUP)
                nc.vector.tensor_copy(K.Y[:, tiles, :], y[:])
                nc.vector.tensor_copy(at_src[:, tiles], dots[:, 0, :])
                nc.vector.tensor_copy(K.AT_DST[:, tiles], dots[:, 1, :])
                dve.drain()
            dve.nop().then_inc(src_ready, 1)
            dve.wait_ge(turned, 1 + START)
            nc.vector.tensor_copy(line[:], ps_t[0][0:TILES, 0:ROWS]).then_inc(line_ready, 1)

        @block.tensor
        def _(pe):
            pe.wait_ge(w_in, 48 + START)
            with pe.Fori(0, GROUPS) as g:
                pe.wait_ge(row_ready, g + 1 + START)
                pe.wait_ge(xt_ready, g + START)
                transpose_group(nc, K, row, ps_t).then_inc(t_done, 1)
                pe.wait_ge(xt_ready, g + 1 + START)
                for u in range(GROUP):
                    t = g * GROUP + u
                    pe.wait_ge(y_used, (t if u == 0 else t - 1) + START)
                    for k in range(KC):
                        last = nc.tensor.matmul(ps_y[u % 2][0:ROWS, 0:C], xt[:, k, u * ROWS:(u + 1) * ROWS],
                                                w[:, k, :], start=(k == 0), stop=(k == KC - 1))
                    last.then_inc(y_done, 1)
            pe.wait_ge(src_ready, 1 + START)
            nc.tensor.transpose(ps_t[0][0:TILES, 0:ROWS], at_src[:], K.ident_f[0:ROWS, 0:ROWS]).then_inc(turned, 1)


def gat(nc, K, D):
    quads = [(a, min(a + 4, TILES)) for a in range(0, TILES, 4)]
    with ExitStack() as st:
        m = Memory(nc, st, "gat")
        cnt = [m.sb(f"cnt{i}", (ROWS, NODES), BF16) for i in range(2)]
        absent = m.sb("absent", (ROWS, NODES), BF16)
        score = m.sb("score", (ROWS, NODES))
        fifth = m.sb("fifth", (ROWS, NODES))
        prob = m.sb("prob", (ROWS, NODES))
        prob_t = m.sb("prob_t", (ROWS, NODES))
        bias = m.sb("bias", (ROWS, C))
        small = m.sb("small", (ROWS, 8))
        acc = m.sb("acc", (ROWS, C))
        ps_t = [m.ps(f"ps_t{i}") for i in range(4)]
        ps_o = [m.ps(f"ps_o{i}") for i in range(2)]
        arrived = [m.sem(f"in{i}") for i in range(2)]
        b_in, cnt_used, scored, exped, weighed, t_done, t_read, o_done, o_used = (
            m.sem(n) for n in ("b_in", "cnt_used", "scored", "exped", "weighed", "t_done", "t_read", "o_done", "o_used"))
        fifths, leaky = m.sem("fifths"), m.sem("leaky")
        block = m.block()
        greatest, dst, dst5, top, low, neg_top, total, inv = (small[:, i:i + 1] for i in range(8))

        @block.sync
        def _(sp):
            sp.dma_start(bias[:], D["L1_gnn_b2"].partition_broadcast(ROWS)).then_inc(b_in, 16)
            load_tiles(sp, cnt, K.adj_t, arrived, cnt_used)

        @block.vector
        def _(dve):
            v = nc.vector
            dve.nop().then_inc(cnt_used, 1)
            dve.wait_ge(b_in, 16 + START)

            def tile(t, b, i):
                dve.wait_ge(arrived[b], (i + 1) * 32 + START)
                own = cnt[b][:, bass.ds(t * ROWS, ROWS)]
                v.tensor_tensor(own, own, K.ident_b[0:ROWS, 0:ROWS], ALU.add)
                v.tensor_copy(dst, K.AT_DST[:, bass.ds(t, 1)])
                v.tensor_scalar(dst5, K.AT_DST[:, bass.ds(t, 1)], 0.2, None, ALU.mult)
                dve.drain()
                v.tensor_scalar(absent[:], cnt[b][:], 0.0, -1e30, ALU.is_equal, ALU.mult)
                dve.drain()
                v.tensor_tensor_reduce(out=score[:], in0=absent[:], in1=K.SRC[:], scale=1.0, scalar=-3e38,
                                       op0=ALU.add, op1=ALU.max, accum_out=greatest)
                dve.drain()
                v.tensor_tensor(top, greatest, dst, ALU.add)
                dve.drain()
                v.tensor_scalar(low, top, 0.2, None, ALU.mult)
                dve.drain()
                v.tensor_tensor(top, top, low, ALU.max)
                dve.drain()
                v.tensor_scalar(neg_top, top, -1.0, None, ALU.mult).then_inc(scored, 1)
                dve.wait_ge(fifths, t + 1 + START)
                v.scalar_tensor_tensor(score[:], score[:], dst, fifth[:], ALU.add, ALU.max).then_inc(leaky, 1)
                dve.wait_ge(exped, t + 1 + START)
                dve.wait_ge(t_done, t * len(quads) + START)
                v.tensor_tensor_reduce(out=prob[:], in0=score[:], in1=cnt[b][:], scale=1.0, scalar=0.0,
                                       op0=ALU.mult, op1=ALU.add, accum_out=total).then_inc(weighed, 1)
                dve.drain()
                dve.nop().then_inc(cnt_used, 1)
                v.tensor_scalar(inv, total, 1e-16, None, ALU.add)
                dve.drain()
                v.reciprocal(inv, inv)
                dve.drain()
                dve.wait_ge(o_done, t + 1 + START)
                v.scalar_tensor_tensor(acc[:], ps_o[b][0:ROWS, 0:C], inv, bias[:], ALU.mult, ALU.add).then_inc(o_used, 1)
                dve.drain()
                v.scalar_tensor_tensor(K.X[:, t, :], acc[:], 0.0, K.X[:, t, :], ALU.max, ALU.add)
                dve.drain()
            two_by_two(dve, TILES, tile)

        @block.scalar
        def _(act):
            def tile(t, b, i):
                act.wait_ge(scored, t + 1 + START)
                nc.scalar.activation(fifth[:], score[:], ACT.Identity, bias=dst5, scale=0.2).then_inc(fifths, 1)
                act.wait_ge(leaky, t + 1 + START)
                nc.scalar.activation(score[:], score[:], ACT.Exp, bias=neg_top).then_inc(exped, 1)
                for n, (a, z) in enumerate(quads):
                    act.wait_ge(t_done, t * len(quads) + n + 1 + START)
                    if n == 0:
                        act.wait_ge(o_done, t + START)
                    nc.scalar.activation(prob_t[:, a * ROWS:z * ROWS], ps_t[n % 4][0:ROWS, 0:(z - a) * ROWS],
                                         ACT.Copy).then_inc(t_read, 1)
            two_by_two(act, TILES, tile)

        @block.tensor
        def _(pe):
            def tile(t, b, i):
                pe.wait_ge(weighed, t + 1 + START)
                pe.wait_ge(t_read, t * len(quads) + START)
                for n, (a, z) in enumerate(quads):
                    if n >= 4:
                        pe.wait_ge(t_read, t * len(quads) + n - 3 + START)
                    for s in range(a, z):
                        last = nc.tensor.transpose(ps_t[n % 4][0:ROWS, (s - a) * ROWS:(s - a + 1) * ROWS],
                                                   prob[:, s * ROWS:(s + 1) * ROWS], K.ident_f[0:ROWS, 0:ROWS])
                    last.then_inc(t_done, 1)
                pe.wait_ge(o_used, (t if b == 0 else t - 1) + START)
                for n, (a, z) in enumerate(quads):
                    pe.wait_ge(t_read, t * len(quads) + n + 1 + START)
                    for s in range(a, z):
                        last = nc.tensor.matmul(ps_o[b][0:ROWS, 0:C], prob_t[:, s * ROWS:(s + 1) * ROWS],
                                                K.Y[:, s, :], start=(s == 0), stop=(s == TILES - 1))
                last.then_inc(o_done, 1)
            two_by_two(pe, TILES, tile)


class Kept:
    pass


def program(nc, D, result):
    X0, X1 = Experts(0), Experts(1)
    slots = 128 * max(X0.slot_tiles, X1.slot_tiles)
    K = Kept()
    K.adj = nc.dram_tensor("adjacency", (TILES, ROWS, TILES * ROWS), BF16).ap()
    K.adj_t = nc.dram_tensor("adjacency_t", (TILES, ROWS, NODES), BF16).ap()
    K.rows_dram = nc.dram_tensor("expert_rows", (TILES, ROWS, C), F32).ap()
    K.slot_row = nc.dram_tensor("slot_row", (slots, 1), I32).ap()
    K.slot_out = nc.dram_tensor("slot_out", (slots, C), F32).ap()
    K.src_line = nc.dram_tensor("src_line", (TILES, ROWS), F32).ap()
    with ExitStack() as all_:
        def sb(stack, name, shape, dt=F32):
            return stack.enter_context(nc.sbuf_tensor(name, list(shape), dt))

        K.X = sb(all_, "X", (ROWS, TILES, C))
        K.ident_f, K.ident_b = sb(all_, "ident_f", (128, 128)), sb(all_, "ident_b", (128, 128), BF16)
        K.number_row, K.number_f = sb(all_, "number_row", (128, 128), F16), sb(all_, "number_f", (128, 128))
        K.zeros, K.ones = sb(all_, "zeros", (1, 512)), sb(all_, "ones", (128, 128))
        K.DEG, K.DINV, K.AT_DST = (sb(all_, n, (ROWS, TILES)) for n in ("DEG", "DINV", "AT_DST"))
        K.slot, K.gate = sb(all_, "slot", (ROWS, TILES * 2), I32), sb(all_, "gate", (ROWS, TILES, 2))
        K.owner = sb(all_, "owner", (1, 128), I32)
        K.kv = sb(all_, "kv", (128, KC, KVW))
        constants(nc, K)

        build_adjacency(nc, K, D)
        with ExitStack() as layer:
            K.XN, K.X1 = sb(layer, "XN0", (ROWS, TILES, C)), sb(layer, "X1", (ROWS, TILES, C))
            K.QT = sb(layer, "QT0", (128, KC, NODES))
            K.Y, K.AGG = sb(layer, "Y0", (ROWS, TILES, 64)), sb(layer, "AGG", (ROWS, TILES, 64))
            K.Yp = sb(layer, "Yp0", (ROWS, TILES, 256), BF16)
            front(nc, K, "front0", D["x"], D["L0_gnn_W1_down"], 64, D["L0_mix_Wkv"], D["L0_mix_Wq"], None)
            mix_tail_l0(nc, K, D)
            gin_down(nc, K)
            gin_tail(nc, K, "gin_down", D, "down", K.XN, K.X1)
            gin_up(nc, K)
            gin_tail(nc, K, "gin_up", D, "up", K.X1, None)
        route(nc, K, D, X0)
        experts(nc, K, D, X0)
        combine(nc, K, X0, None)
        with ExitStack() as layer:
            K.XN, K.Y = sb(layer, "XN1", (ROWS, TILES, C)), sb(layer, "Y1", (ROWS, TILES, C))
            with ExitStack() as early:
                K.QT = sb(early, "QT1", (128, KC, NODES))
                K.Yp = sb(early, "Yp1", (ROWS, TILES, 3 * C), BF16)
                degree_scale(nc, K)
                front(nc, K, "front1", None, D["L1_gnn_W1"], C, D["L1_mix_Wkv"], D["L1_mix_Wq"], K.DINV)
                mix_tail_l1(nc, K, D)
                gcn(nc, K, D)
            K.SRC = sb(layer, "SRC", (ROWS, NODES))
            gat_project(nc, K, D)
            gat(nc, K, D)
        route(nc, K, D, X1)
        experts(nc, K, D, X1)
        combine(nc, K, X1, result)


def lay_out(inputs):
    import numpy as np

    a = {k: np.ascontiguousarray(v) for k, v in inputs.items()}
    wqkv = a.pop("L0_mix_Wqkv")
    a["L0_mix_Wq"] = np.ascontiguousarray(wqkv[:C].T)
    a["L0_mix_Wkv"] = np.ascontiguousarray(wqkv[C:].T)
    for name in ("L0_mix_W1", "L0_mix_W2", "L1_mix_Wq", "L1_mix_Wkv", "L1_mix_Wproj"):
        a[name] = np.ascontiguousarray(a[name].T)
    a["L0_mix_b1"] = np.ascontiguousarray(a["L0_mix_b1"].reshape(KC, 128).T)
    a["L0_ffn_b1"] = np.ascontiguousarray(a["L0_ffn_b1"].reshape(8, 4, 128).transpose(0, 2, 1))
    for name in ("L0_gnn_eps_down", "L0_gnn_eps_up"):
        a[name] = a[name].reshape(1)
    src, dst = a.pop("src"), a.pop("dst")
    for name, e in (("src", src), ("dst", dst)):
        cols = np.full(CHUNKS_PAD * CH, NODES, np.int32)
        cols[:EDGES] = e
        a[name + "_cols"] = np.ascontiguousarray(cols.reshape(CHUNKS_PAD, CH).T)
    rows = np.full(CHUNK_ROWS * CH, NODES, np.int32)
    rows[:EDGES] = dst
    a["dst_rows"] = rows.reshape(128, 4 * CH)
    return a


def kernel(**inputs):
    import concourse.bacc as bacc
    import numpy as np
    from concourse.bass_utils import run_bass_kernel_spmd

    nc = bacc.Bacc("TRN2", target_bir_lowering=False, num_devices=1)
    arrays = {"in_" + k: v for k, v in lay_out(inputs).items()}
    D = {k[3:]: nc.dram_tensor(k, v.shape, mybir.dt.from_np(v.dtype), kind="ExternalInput").ap()
         for k, v in arrays.items()}
    out = nc.dram_tensor("out", (NODES, C), F32, kind="ExternalOutput").ap()
    program(nc, D, out)
    got = run_bass_kernel_spmd(nc, [arrays], core_ids=[0])
    return got.results[0]["out"]
```

```python
from contextlib import ExitStack

import concourse.bass as bass
from concourse import mybir

F32 = mybir.dt.float32
BF16 = mybir.dt.bfloat16
F16 = mybir.dt.float16
I32 = mybir.dt.int32
ALU = mybir.AluOpType
ACT = mybir.ActivationFunctionType
AX = mybir.AxisListType

NODES = 3125
EDGES = 53125
C = 256
KC = C // 128
ROWS = 125
TILES = NODES // ROWS
GROUP = 5
GROUPS = TILES // GROUP
GROWS = GROUP * ROWS
HEADS = 8
HD = C // HEADS
HPB = 128 // HD
KVW = 128 + HPB
WIN = 25
WINS = NODES // WIN
WPT = ROWS // WIN
CH = 128
CHUNKS = -(-EDGES // CH)
CHUNKS_PAD = CHUNKS + 4
FIXED = 4
MORE_MAX = CHUNKS
CHUNK_ROWS = 512
DMA_ROWS = 112
START = 1
LN_EPS = 1e-5
SPLIT = ((0, 500), (500, 625))


def rows_dma(eng, out, in_, sem):
    eng.dma_start(out[0:DMA_ROWS], in_[0:DMA_ROWS]).then_inc(sem, 16)
    eng.dma_start(out[DMA_ROWS:ROWS], in_[DMA_ROWS:ROWS]).then_inc(sem, 16)


class Memory:

    def __init__(self, nc, stack, stage):
        self.nc, self.stack, self.stage = nc, stack, stage
        self.sems, self.starts = [], []
        stack.callback(self.clear)
        self.tick = self.sem("tick")

    def sb(self, name, shape, dt=F32):
        return self.stack.enter_context(self.nc.sbuf_tensor(f"{self.stage}_{name}", list(shape), dt))

    def ps(self, name, shape=(128, 512), dt=F32):
        return self.stack.enter_context(self.nc.psum_tensor(f"{self.stage}_{name}", list(shape), dt))

    def sem(self, name, start=START):
        self.sems.append(self.nc.alloc_semaphore(f"{self.stage}_{name}"))
        self.starts.append(start)
        return self.sems[-1]

    def block(self):
        for sem, start in zip(self.sems, self.starts):
            if start:
                self.nc.gpsimd.sem_inc(sem, start)
        self.nc.all_engine_barrier()
        return self.stack.enter_context(self.nc.Block())

    def clear(self):
        self.nc.clear_and_free_semaphores(self.sems)


def carry(eng, m):
    eng.nop().then_inc(m.tick, 1)


def layer_norm_stats(dve, nc, src, stats, mv, var_eps, n):
    for u in range(n):
        nc.vector.bn_stats(stats[:, u, :], src(u))
    dve.drain()
    for u in range(n):
        nc.vector.bn_aggr(mv[:, u, :], stats[:, u, :])
    dve.drain()
    return nc.vector.tensor_scalar(var_eps[:], mv[:, :, 1], LN_EPS, None, ALU.add)


def split3(dve, nc, whole, rest, parts):
    nc.vector.tensor_copy(parts[0], whole)
    dve.drain()
    nc.vector.tensor_tensor(rest, whole, parts[0], ALU.subtract)
    dve.drain()
    nc.vector.tensor_copy(parts[1], rest)
    dve.drain()
    return nc.vector.tensor_tensor(parts[2], rest, parts[1], ALU.subtract)


def transpose_group(nc, K, rows, banks):
    for k in range(KC):
        for u in range(GROUP):
            out = banks[k][:, u * ROWS:(u + 1) * ROWS] if u < 4 else banks[2][:, k * ROWS:(k + 1) * ROWS]
            last = nc.tensor.transpose(out, rows[:, u, k * 128:(k + 1) * 128], K.ident_f[0:ROWS, 0:ROWS])
    return last


def copy_transposed(nc, dst, banks, fn=ACT.Copy, bias=None):
    for k in range(KC):
        more = {} if bias is None else {"bias": bias[:, k:k + 1]}
        nc.scalar.activation(dst[:, k, 0:4 * ROWS], banks[k][:, 0:4 * ROWS], fn, **more)
        last = nc.scalar.activation(dst[:, k, 4 * ROWS:GROWS], banks[2][:, k * ROWS:(k + 1) * ROWS], fn, **more)
    return last


def matmul_group(nc, banks, block, weight, xt):
    for lo, hi in SPLIT:
        out = banks[block][:, 0:4 * ROWS] if lo == 0 else banks[2][:, block * ROWS:(block + 1) * ROWS]
        for k in range(KC):
            last = nc.tensor.matmul(out, weight(k), xt[:, k, lo:hi], start=(k == 0), stop=(k == KC - 1))
    return last


def zero_bank(nc, K, bank, width, start):
    return nc.tensor.matmul(bank[:, 0:width], K.zeros[0:1, 0:128], K.zeros[0:1, 0:width],
                            start=start, stop=not start)


def two_by_two(eng, count, body):
    with eng.Fori(0, count // 2) as i:
        body(i * 2, 0, i)
        body(i * 2 + 1, 1, i)
    body(count - 1, 0, count // 2)


def constants(nc, K):
    with ExitStack() as st:
        m = Memory(nc, st, "const")
        zeroed = m.sem("zeroed")
        block = m.block()

        @block.gpsimd
        def _(pool):
            nc.gpsimd.memset(K.zeros[:], 0.0)
            nc.gpsimd.memset(K.ones[:], 1.0)
            nc.gpsimd.memset(K.ident_f[:], 0.0)
            nc.gpsimd.memset(K.ident_b[:], 0.0).then_inc(zeroed, 1)
            pool.wait_ge(zeroed, 1 + START)
            for ident in (K.ident_f, K.ident_b):
                nc.gpsimd.affine_select(out=ident[:], in_=ident[:], compare_op=ALU.not_equal, fill=1.0,
                                        base=0, pattern=[[-1, 128]], channel_multiplier=1)
            nc.gpsimd.iota(K.number_f[:], [[1, 128]], base=0, channel_multiplier=0,
                           allow_small_or_imprecise_dtypes=True)
            nc.gpsimd.iota(K.number_row[:], [[1, 128]], base=0, channel_multiplier=0,
                           allow_small_or_imprecise_dtypes=True)


def front(nc, K, stage, D, w_y, y_width, w_kv, w_q, y_scale):
    with ExitStack() as st:
        m = Memory(nc, st, stage)
        wy = m.sb("wy", (128, KC, y_width))
        wkv = m.sb("wkv", (128, KC, 2 * C))
        wq = m.sb("wq", (128, KC, C))
        stats, mv = m.sb("stats", (ROWS, GROUP, 6)), m.sb("mv", (ROWS, GROUP, 2))
        var_eps, std, rstd = (m.sb(n, (ROWS, GROUP)) for n in ("var_eps", "std", "rstd"))
        xn = m.sb("xn", (ROWS, GROUP, C))
        xt = m.sb("xt", (128, KC, GROWS))
        e_kv, r_kv = m.sb("e_kv", (ROWS, 2, C)), m.sb("r_kv", (ROWS, 2, C))
        key, val = m.sb("key", (ROWS, 2, C)), m.sb("val", (ROWS, 2, KC, 129))
        e_q, r_q = m.sb("e_q", (128, KC, GROWS)), m.sb("r_q", (128, KC, GROWS))
        y_rest = m.sb("y_rest", (ROWS, y_width))
        ps_t = [m.ps(f"ps_t{i}") for i in range(3)]
        ps_y = m.ps("ps_y")
        ps_kv = [m.ps(f"ps_kv{i}") for i in range(2)]
        ps_acc = [m.ps(f"ps_acc{i}") for i in range(KC)]
        w_in, x_in, var_ready, std_ready, xn_ready, xn_saved = (
            m.sem(n) for n in ("w_in", "x_in", "var_ready", "std_ready", "xn_ready", "xn_saved"))
        t_done, xt_ready, y_done, y_used, kv_done, kv_read, kv_exp, key_ready, key_used = (
            m.sem(n) for n in ("t_done", "xt_ready", "y_done", "y_used", "kv_done", "kv_read", "kv_exp",
                               "key_ready", "key_used"))
        q_done, q_read, q_used, sum_done = m.sem("q_done"), m.sem("q_read"), m.sem("q_used"), m.sem("sum_done")
        block = m.block()

        @block.sync
        def _(sp):
            sp.dma_start(wkv[:], w_kv.rearrange("(k p) o -> p k o", p=128)).then_inc(w_in, 16)
            sp.dma_start(wq[:], w_q.rearrange("(k p) o -> p k o", p=128)).then_inc(w_in, 16)
            sp.dma_start(wy[:], w_y.rearrange("(k p) o -> p k o", p=128)).then_inc(w_in, 16)
            if D is not None:
                rows_dma(sp, K.X, D.rearrange("(t p) c -> p t c", p=ROWS), x_in)
                sp.wait_ge(x_in, 32 + START)
            sp.wait_ge(w_in, 48 + START)

        @block.vector
        def _(dve):
            if D is not None:
                dve.wait_ge(x_in, 32 + START)
            nc.vector.memset(val[:], 1.0)
            nc.vector.memset(K.kv[:], 0.0)
            if y_width == 64:
                nc.vector.memset(K.Yp[:], 1.0)
            with dve.Fori(0, GROUPS) as g:
                layer_norm_stats(dve, nc, lambda u: K.X[:, g * GROUP + u, :], stats, mv, var_eps,
                                 GROUP).then_inc(var_ready, 1)
                dve.wait_ge(std_ready, g + 1 + START)
                nc.vector.reciprocal(rstd[:], std[:])
                dve.drain()
                dve.wait_ge(t_done, g + START)
                dve.wait_ge(xn_saved, g + START)
                for u in range(GROUP):
                    last = nc.vector.tensor_scalar(xn[:, u, :], K.X[:, g * GROUP + u, :], mv[:, u, 0:1],
                                                   rstd[:, u:u + 1], ALU.subtract, ALU.mult)
                last.then_inc(xn_ready, 1)
                for u in range(GROUP):
                    t = g * GROUP + u
                    dve.wait_ge(y_done, t + 1 + START)
                    y = K.Y[:, t, 0:y_width]
                    if y_scale is None:
                        nc.vector.tensor_copy(y, ps_y[0:ROWS, 0:y_width]).then_inc(y_used, 1)
                    else:
                        nc.vector.tensor_scalar(y, ps_y[0:ROWS, 0:y_width], y_scale[:, bass.ds(t, 1)], None,
                                                ALU.mult).then_inc(y_used, 1)
                    dve.drain()
                    split3(dve, nc, y, y_rest[:], [K.Yp[:, t, i * y_width:(i + 1) * y_width] for i in range(3)])
                    dve.wait_ge(kv_exp, t + 1 + START)
                    b = u % 2
                    nc.vector.scalar_tensor_tensor(key[:, b, :], e_kv[:, b, :], 1.0, r_kv[:, b, :],
                                                   ALU.min, ALU.add).then_inc(key_ready, 1)
                dve.wait_ge(q_read, g + 1 + START)
                for h in range(KC):
                    last = nc.vector.scalar_tensor_tensor(K.QT[:, h, bass.ds(g * GROWS, GROWS)],
                                                          e_q[:, h, :], 1.0, r_q[:, h, :], ALU.min, ALU.add)
                last.then_inc(q_used, 1)
            dve.wait_ge(sum_done, 1 + START)
            for h in range(KC):
                for a in range(HPB):
                    p = slice(HD * a, HD * a + HD)
                    nc.vector.tensor_copy(K.kv[p, h, HD * a:HD * a + HD], ps_acc[h][p, HD * a:HD * a + HD])
                    nc.vector.tensor_copy(K.kv[p, h, 128 + a:129 + a], ps_acc[h][p, 128:129])

        @block.gpsimd
        def _(pool):
            with pool.Fori(0, GROUPS) as g:
                pool.wait_ge(xn_ready, g + 1 + START)
                nc.gpsimd.tensor_copy(K.XN[:, bass.ds(g * GROUP, GROUP), :], xn[:]).then_inc(xn_saved, 1)

        @block.scalar
        def _(act):
            with act.Fori(0, GROUPS) as g:
                act.wait_ge(var_ready, g + 1 + START)
                nc.scalar.activation(std[:], var_eps[:], ACT.Sqrt).then_inc(std_ready, 1)
                act.wait_ge(t_done, g + 1 + START)
                copy_transposed(nc, xt, ps_t).then_inc(xt_ready, 1)
                for u in range(GROUP):
                    t = g * GROUP + u
                    b = u % 2
                    act.wait_ge(kv_done, t + 1 + START)
                    act.wait_ge(key_ready, (t if u == 0 else t - 1) + START)
                    act.wait_ge(key_used, (t if u == 0 else t - 1) + START)
                    nc.scalar.activation(e_kv[:, b, :], ps_kv[b][0:ROWS, 0:C], ACT.Exp)
                    nc.scalar.activation(r_kv[:, b, :], ps_kv[b][0:ROWS, 0:C], ACT.Relu)
                    nc.scalar.activation(val[:, b, :, 0:128],
                                         ps_kv[b][0:ROWS, C:2 * C].rearrange("p (k f) -> p k f", k=KC),
                                         ACT.Copy).then_inc(kv_exp, 1)
                act.wait_ge(q_done, g + 1 + START)
                act.wait_ge(q_used, g + START)
                for dst, fn in ((e_q, ACT.Exp), (r_q, ACT.Relu)):
                    last = copy_transposed(nc, dst, ps_t, fn)
                last.then_inc(q_read, 1)

        @block.tensor
        def _(pe):
            def key_value_sum(g, u):
                pe.wait_ge(key_ready, g * GROUP + u + 1 + START)
                for h in range(KC):
                    last = nc.tensor.matmul(ps_acc[h][:, 0:129], key[:, u % 2, h * 128:(h + 1) * 128],
                                            val[:, u % 2, h, :], start=False, stop=False)
                last.then_inc(key_used, 1)

            for h in range(KC):
                zero_bank(nc, K, ps_acc[h], 129, start=True)
            pe.wait_ge(w_in, 48 + START)
            with pe.Fori(0, GROUPS) as g:
                pe.wait_ge(xn_ready, g + 1 + START)
                pe.wait_ge(q_read, g + START)
                transpose_group(nc, K, xn, ps_t).then_inc(t_done, 1)
                pe.wait_ge(xt_ready, g + 1 + START)
                for u in range(GROUP):
                    t = g * GROUP + u
                    cols = slice(u * ROWS, (u + 1) * ROWS)
                    pe.wait_ge(y_used, t + START)
                    for k in range(KC):
                        last = nc.tensor.matmul(ps_y[0:ROWS, 0:y_width], xt[:, k, cols], wy[:, k, :],
                                                start=(k == 0), stop=(k == KC - 1))
                    last.then_inc(y_done, 1)
                    pe.wait_ge(kv_exp, (t if u == 0 else t - 1) + START)
                    for k in range(KC):
                        last = nc.tensor.matmul(ps_kv[u % 2][0:ROWS, :], xt[:, k, cols], wkv[:, k, :],
                                                start=(k == 0), stop=(k == KC - 1))
                    last.then_inc(kv_done, 1)
                    if u:
                        key_value_sum(g, u - 1)
                for h in range(KC):
                    last = matmul_group(nc, ps_t, h, lambda k: wq[:, k, h * 128:(h + 1) * 128], xt)
                last.then_inc(q_done, 1)
                key_value_sum(g, GROUP - 1)
            for h in range(KC):
                last = zero_bank(nc, K, ps_acc[h], 129, start=False)
            last.then_inc(sum_done, 1)


def mix_tail_l0(nc, K, D):
    with ExitStack() as st:
        m = Memory(nc, st, "mix0")
        w1, w2 = m.sb("w1", (128, KC, C)), m.sb("w2", (128, KC, C))
        b1 = m.sb("b1", (128, KC))
        vec = m.sb("vec", (ROWS, 5, C))
        stats, mv = m.sb("stats", (ROWS, GROUP, 6)), m.sb("mv", (ROWS, GROUP, 2))
        var_eps, std, rstd = (m.sb(n, (ROWS, GROUP)) for n in ("var_eps", "std", "rstd"))
        qt = m.sb("qt", (128, KC, GROWS))
        den = m.sb("den", (ROWS, GROUP, KC, HPB))
        att = m.sb("att", (ROWS, GROUP, C))
        x1 = m.sb("x1", (ROWS, GROUP, C))
        x1t, ht = m.sb("x1t", (128, KC, GROWS)), m.sb("ht", (128, KC, GROWS))
        ps_t = [m.ps(f"ps_t{i}") for i in range(3)]
        ps_a = [m.ps(f"ps_a{i}") for i in range(2)]
        ps_o = [m.ps(f"ps_o{i}") for i in range(2)]
        w_in, qt_ready, a_done, a_used, var_ready, std_ready = (
            m.sem(n) for n in ("w_in", "qt_ready", "a_done", "a_used", "var_ready", "std_ready"))
        x1_ready, t_done, x1t_ready, h_done, ht_ready, o_done, o_used = (
            m.sem(n) for n in ("x1_ready", "t_done", "x1t_ready", "h_done", "ht_ready", "o_done", "o_used"))
        block = m.block()

        @block.sync
        def _(sp):
            sp.dma_start(w1[:], D["L0_mix_W1"].rearrange("(k p) o -> p k o", p=128)).then_inc(w_in, 16)
            sp.dma_start(w2[:], D["L0_mix_W2"].rearrange("(k p) o -> p k o", p=128)).then_inc(w_in, 16)
            sp.dma_start(b1[:], D["L0_mix_b1"]).then_inc(w_in, 16)
            for n, name in enumerate(("ln1_g", "ln1_b", "ln2_g", "ln2_b", "b2")):
                sp.dma_start(vec[:, n, :], D["L0_mix_" + name].partition_broadcast(ROWS)).then_inc(w_in, 16)
            sp.wait_ge(w_in, 8 * 16 + START)

        @block.gpsimd
        def _(pool):
            with pool.Fori(0, GROUPS) as g:
                pool.wait_ge(a_done, g * GROUP + START)
                nc.gpsimd.tensor_copy(qt[:], K.QT[:, :, bass.ds(g * GROWS, GROWS)]).then_inc(qt_ready, 1)

        @block.vector
        def _(dve):
            def bc(n):
                return vec[:, n, :].unsqueeze(1).broadcast_to([ROWS, GROUP, C])

            def normalise(src, out, n):
                layer_norm_stats(dve, nc, lambda u: src[:, u, :], stats, mv, var_eps, GROUP).then_inc(var_ready, 1)
                dve.wait_ge(std_ready, g * 2 + 1 + n + START)
                nc.vector.reciprocal(rstd[:], std[:])
                dve.drain()
                for u in range(GROUP):
                    nc.vector.tensor_scalar(out[:, u, :], src[:, u, :], mv[:, u, 0:1], rstd[:, u:u + 1],
                                            ALU.subtract, ALU.mult)
                dve.drain()
                nc.vector.tensor_tensor(out[:], out[:], bc(2 * n), ALU.mult)
                dve.drain()
                return nc.vector.tensor_tensor(out[:], out[:], bc(2 * n + 1), ALU.add)

            dve.wait_ge(w_in, 8 * 16 + START)
            with dve.Fori(0, GROUPS) as g:
                for u in range(GROUP):
                    t = g * GROUP + u
                    dve.wait_ge(a_done, t + 1 + START)
                    a = ps_a[u % 2][0:ROWS, 0:KC * KVW].rearrange("p (k w) -> p k w", k=KC)
                    nc.vector.tensor_scalar(den[:, u], a[:, :, 128:KVW], 1e-6, None, ALU.add)
                    dve.drain()
                    nc.vector.reciprocal(den[:, u], den[:, u])
                    dve.drain()
                    for k in range(KC):
                        last = nc.vector.tensor_tensor(
                            att[:, u, k * 128:(k + 1) * 128].rearrange("p (a d) -> p a d", d=HD),
                            a[:, k, 0:128].rearrange("p (a d) -> p a d", d=HD),
                            den[:, u, k, :].unsqueeze(2).broadcast_to([ROWS, HPB, HD]), ALU.mult)
                    last.then_inc(a_used, 1)
                dve.drain()
                nc.vector.tensor_tensor(att[:], att[:], K.XN[:, bass.ds(g * GROUP, GROUP), :], ALU.add)
                dve.drain()
                normalise(att, x1, 0).then_inc(x1_ready, 1)
                for u in range(GROUP):
                    dve.wait_ge(o_done, g * GROUP + u + 1 + START)
                    nc.vector.tensor_tensor(att[:, u, :], ps_o[u % 2][0:ROWS, 0:C], x1[:, u, :],
                                            ALU.add).then_inc(o_used, 1)
                dve.drain()
                nc.vector.tensor_tensor(att[:], att[:], bc(4), ALU.add)
                dve.drain()
                normalise(att, x1, 1)
                dve.drain()
                nc.vector.tensor_tensor(K.X[:, bass.ds(g * GROUP, GROUP), :],
                                        K.X[:, bass.ds(g * GROUP, GROUP), :], x1[:], ALU.add)

        @block.scalar
        def _(act):
            act.wait_ge(w_in, 8 * 16 + START)
            with act.Fori(0, GROUPS) as g:
                act.wait_ge(var_ready, g * 2 + 1 + START)
                nc.scalar.activation(std[:], var_eps[:], ACT.Sqrt).then_inc(std_ready, 1)
                act.wait_ge(t_done, g + 1 + START)
                copy_transposed(nc, x1t, ps_t).then_inc(x1t_ready, 1)
                act.wait_ge(h_done, g + 1 + START)
                copy_transposed(nc, ht, ps_t, ACT.Gelu, b1).then_inc(ht_ready, 1)
                act.wait_ge(var_ready, g * 2 + 2 + START)
                nc.scalar.activation(std[:], var_eps[:], ACT.Sqrt).then_inc(std_ready, 1)

        @block.tensor
        def _(pe):
            pe.wait_ge(w_in, 8 * 16 + START)
            with pe.Fori(0, GROUPS) as g:
                pe.wait_ge(qt_ready, g + 1 + START)
                for u in range(GROUP):
                    t = g * GROUP + u
                    pe.wait_ge(a_used, (t if u == 0 else t - 1) + START)
                    for k in range(KC):
                        last = nc.tensor.matmul(ps_a[u % 2][0:ROWS, k * KVW:(k + 1) * KVW],
                                                qt[:, k, u * ROWS:(u + 1) * ROWS], K.kv[:, k, :],
                                                start=True, stop=True)
                    last.then_inc(a_done, 1)
                pe.wait_ge(x1_ready, g + 1 + START)
                pe.wait_ge(ht_ready, g + START)
                transpose_group(nc, K, x1, ps_t).then_inc(t_done, 1)
                pe.wait_ge(x1t_ready, g + 1 + START)
                for h in range(KC):
                    last = matmul_group(nc, ps_t, h, lambda k: w1[:, k, h * 128:(h + 1) * 128], x1t)
                last.then_inc(h_done, 1)
                pe.wait_ge(ht_ready, g + 1 + START)
                for u in range(GROUP):
                    t = g * GROUP + u
                    pe.wait_ge(o_used, (t if u == 0 else t - 1) + START)
                    for k in range(KC):
                        last = nc.tensor.matmul(ps_o[u % 2][0:ROWS, 0:C], ht[:, k, u * ROWS:(u + 1) * ROWS],
                                                w2[:, k, :], start=(k == 0), stop=(k == KC - 1))
                    last.then_inc(o_done, 1)


def build_adjacency(nc, K, D):
    with ExitStack() as st:
        m = Memory(nc, st, "adj")
        src_i, dst_i = m.sb("src_i", (CH, CHUNKS_PAD), I32), m.sb("dst_i", (CH, CHUNKS_PAD), I32)
        dst_rows_i = m.sb("dst_rows_i", (128, CHUNK_ROWS), I32)
        src_f, dst_f = m.sb("src_f", (CH, CHUNKS_PAD)), m.sb("dst_f", (CH, CHUNKS_PAD))
        dst_rows = m.sb("dst_rows", (128, 4, CH))
        hi = m.sb("hi", (CH, CHUNKS_PAD))
        low_all = m.sb("low", (CH, CHUNKS + FIXED + MORE_MAX))
        key_all = m.sb("key", (CH, CHUNKS + FIXED + MORE_MAX))
        low = low_all[:, 0:CHUNKS_PAD]
        key = key_all[:, 0:CHUNKS_PAD]
        hi_i = m.sb("hi_i", (CH, CHUNKS_PAD), I32)
        off = m.sb("off", (CH, CHUNKS_PAD))
        least, most = m.sb("least", (128, 4)), m.sb("most", (128, 4))
        win_first = m.sb("win_first", (128, WINS))
        most_chunks = m.sb("most_chunks", (1, 1))
        chunk_no = m.sb("chunk_no", (128, 4))
        rank_up, rank_down = m.sb("rank_up", (128, 4)), m.sb("rank_down", (128, 4))
        here, here2 = m.sb("here", (128, 4, WINS)), m.sb("here2", (128, 4, WINS))
        span = m.sb("span", (128, 2, 4, WINS))
        span_all = m.sb("span_all", (128, 2, 4, WINS))
        ends = m.sb("ends", (1, 2, WINS))
        row = m.sb("row", (1, 2, WINS))
        table = m.sb("table", (1, WINS + 1), I32)
        key_row = m.sb("key_row", (CH, TILES * WIN), F16)
        win_key = m.sb("win_key", (CH, WINS))
        one_s = [m.sb(f"one_s{i}", (CH, FIXED, ROWS), BF16) for i in range(2)]
        one_k = [m.sb(f"one_k{i}", (CH, FIXED, TILES * WIN), BF16) for i in range(2)]
        more_s, more_k = m.sb("more_s", (CH, ROWS), BF16), m.sb("more_k", (CH, TILES * WIN), BF16)
        key_here = [m.sb(f"key_here{i}", (CH, FIXED)) for i in range(2)]
        adj = [m.sb(f"tile{i}", (ROWS, TILES, ROWS), BF16) for i in range(2)]
        adj_t = [m.sb(f"tile_t{i}", (ROWS, NODES), BF16) for i in range(2)]
        ps_w = [[m.ps(f"ps_w{i}{j}") for j in range(2)] for i in range(2)]
        ps_t = [m.ps(f"ps_t{i}", (128, 1024), BF16) for i in range(4)]
        e_in, made, span_ready, spread, table_ready = (
            m.sem(n) for n in ("e_in", "made", "span_ready", "spread", "table_ready"))
        keyed, one_ready, more_ready, more_used, win_done, win_read, t_done, t_read, stored, tile_used = (
            m.sem(n) for n in ("keyed", "one_ready", "more_ready", "more_used", "win_done", "win_read", "t_done", "t_read",
                               "stored", "tile_used"))
        block = m.block()

        @block.sync
        def _(sp):
            sp.dma_start(src_i[:], D["src_cols"]).then_inc(e_in, 16)
            sp.dma_start(dst_i[:], D["dst_cols"]).then_inc(e_in, 16)
            sp.dma_start(dst_rows_i[:], D["dst_rows"]).then_inc(e_in, 16)

            def store(t, b, i):
                sp.wait_ge(stored, t * 64 + START)
                sp.nop().then_inc(tile_used, 1)
                sp.wait_ge(win_read, t * WPT + WPT + START)
                rows_dma(sp, K.adj[bass.ds(t, 1)].rearrange("t p n -> (t p) n"),
                         adj[b][:].rearrange("p t d -> p (t d)"), stored)
                sp.wait_ge(t_read, t + 1 + START)
                rows_dma(sp, K.adj_t[bass.ds(t, 1)].rearrange("t p n -> (t p) n"), adj_t[b][:], stored)

            two_by_two(sp, TILES, store)
            sp.wait_ge(stored, TILES * 64 + START)

        @block.gpsimd
        def _(pool):
            nc.gpsimd.iota(key_row[:], [[1, TILES], [TILES, WIN]], base=0, channel_multiplier=0,
                           allow_small_or_imprecise_dtypes=True)
            nc.gpsimd.iota(win_first[:], [[WIN, WINS]], base=0, channel_multiplier=0,
                           allow_small_or_imprecise_dtypes=True)
            nc.gpsimd.iota(win_key[:], [[WIN * TILES, WINS]], base=0, channel_multiplier=0,
                           allow_small_or_imprecise_dtypes=True)
            nc.gpsimd.iota(chunk_no[:], [[1, 4]], base=0, channel_multiplier=4,
                           allow_small_or_imprecise_dtypes=True).then_inc(made, 1)
            pool.wait_ge(span_ready, 1 + START)
            nc.gpsimd.partition_all_reduce(span_all[:].rearrange("p a q w -> p (a q w)"),
                                           span[:].rearrange("p a q w -> p (a q w)"), 128,
                                           bass.bass_isa.ReduceOp.max).then_inc(spread, 1)

        @block.vector
        def _(dve):
            v = nc.vector
            dve.wait_ge(e_in, 48 + START)
            v.tensor_copy(src_f[:], src_i[:])
            v.tensor_copy(dst_f[:], dst_i[:])
            v.tensor_copy(dst_rows[:].rearrange("p q e -> p (q e)"), dst_rows_i[:])
            dve.drain()
            v.tensor_scalar(off[:], src_f[:], 0.5, 1.0 / ROWS, ALU.add, ALU.mult)
            dve.drain()
            v.tensor_copy(hi_i[:], off[:])
            dve.drain()
            v.tensor_copy(hi[:], hi_i[:])
            dve.drain()
            v.scalar_tensor_tensor(off[:], hi[:], float(ROWS), src_f[:], ALU.mult, ALU.is_gt)
            dve.drain()
            v.tensor_tensor(hi[:], hi[:], off[:], ALU.subtract)
            dve.drain()
            v.memset(low_all[:, CHUNKS_PAD:], -1.0)
            v.memset(key_all[:, CHUNKS_PAD:], -1.0)
            v.scalar_tensor_tensor(low, hi[:], -float(ROWS), src_f[:], ALU.mult, ALU.add)
            v.scalar_tensor_tensor(key, dst_f[:], float(TILES), hi[:], ALU.mult, ALU.add)
            v.tensor_reduce(least[:], dst_rows[:], AX.X, ALU.min)
            v.tensor_reduce(most[:], dst_rows[:], AX.X, ALU.max)
            dve.wait_ge(made, 1 + START)
            v.tensor_scalar(rank_up[:], chunk_no[:], 1.0, None, ALU.add)
            v.tensor_scalar(rank_down[:], chunk_no[:], -1.0, float(CHUNK_ROWS), ALU.mult, ALU.add)
            dve.drain()
            for q in range(4):
                v.tensor_scalar(here[:, q, :], win_first[:], float(WIN - 1), least[:, q:q + 1], ALU.add, ALU.is_ge)
                v.tensor_scalar(here2[:, q, :], win_first[:], most[:, q:q + 1], None, ALU.is_le)
            dve.drain()
            v.tensor_tensor(here[:], here[:], here2[:], ALU.mult)
            dve.drain()
            for q in range(4):
                v.tensor_scalar(span[:, 0, q, :], here[:, q, :], rank_up[:, q:q + 1], None, ALU.mult)
                last = v.tensor_scalar(span[:, 1, q, :], here[:, q, :], rank_down[:, q:q + 1], None, ALU.mult)
            last.then_inc(span_ready, 1)
            dve.wait_ge(spread, 1 + START)
            v.tensor_reduce(ends[:], span_all[0:1].rearrange("p a q w -> p a w q"), AX.X, ALU.max)
            dve.drain()
            v.tensor_scalar(row[:, 0, :], ends[:, 1, :], -1.0, float(CHUNK_ROWS), ALU.mult, ALU.add)
            dve.drain()
            v.tensor_scalar(row[:, 0, :], row[:, 0, :], float(CHUNKS), None, ALU.min)
            dve.drain()
            v.tensor_tensor(row[:, 1, :], ends[:, 0, :], row[:, 0, :], ALU.subtract)
            dve.drain()
            v.tensor_copy(table[:, 0:WINS], row[:, 0, :])
            v.tensor_reduce(most_chunks[:], row[:, 1, :], AX.X, ALU.max)
            dve.drain()
            v.tensor_scalar(most_chunks[:], most_chunks[:], -float(FIXED), 1.0, ALU.add, ALU.max)
            dve.drain()
            v.tensor_copy(table[:, WINS:WINS + 1], most_chunks[:]).then_inc(table_ready, 1)
            dve.wait_ge(table_ready, 1 + START)
            more = dve.value_load(table[:, WINS:WINS + 1], min_val=1, max_val=MORE_MAX)

            def tile(t, b, i):
                for w in range(WPT):
                    win, half = t * WPT + w, (b * WPT + w) % 2
                    first = dve.value_load(table[:, bass.ds(win, 1)], min_val=0, max_val=CHUNKS)
                    dve.wait_ge(win_done, win + 1 + START)
                    v.tensor_scalar(key_here[half][:], key_all[:, bass.ds(first, FIXED)],
                                    win_key[:, bass.ds(win, 1)], None, ALU.subtract).then_inc(keyed, 1)
                    v.tensor_tensor(one_s[half][:], K.number_row[:, None, 0:ROWS].to_broadcast((CH, FIXED, ROWS)),
                                    low_all[:, bass.ds(first, FIXED)][:, :, None].to_broadcast((CH, FIXED, ROWS)),
                                    ALU.is_equal)
                    dve.wait_ge(keyed, win + 1 + START)
                    for j in range(FIXED):
                        v.tensor_scalar(one_k[half][:, j, :], key_row[:], key_here[half][:, j:j + 1], None,
                                        ALU.is_equal).then_inc(one_ready, 1)
                    with dve.Fori(0, more) as n:
                        dve.wait_ge(more_used, win * more + n + 1 + START)
                        v.tensor_scalar(more_s[:], K.number_row[:, 0:ROWS],
                                        low_all[:, bass.ds(first + n + FIXED, 1)], None, ALU.is_equal)
                        v.tensor_scalar(more_k[:], key_row[:], win_key[:, bass.ds(win, 1)],
                                        key_all[:, bass.ds(first + n + FIXED, 1)], ALU.add,
                                        ALU.is_equal).then_inc(more_ready, 1)

            two_by_two(dve, TILES, tile)

        @block.scalar
        def _(act):
            def tile(t, b, i):
                for w in range(WPT):
                    win = t * WPT + w
                    act.wait_ge(win_done, win + 3 + START)
                    if w == 0:
                        act.wait_ge(tile_used, t + START)
                    for bank, (a, z) in enumerate(((0, 20), (20, 25))):
                        last = nc.scalar.activation(
                            adj[b][:, a:z, w * WIN:(w + 1) * WIN],
                            ps_w[w % 2][bank][0:ROWS, 0:(z - a) * WIN].rearrange("p (s d) -> p s d", d=WIN),
                            ACT.Copy)
                    last.then_inc(win_read, 1)
                act.wait_ge(t_done, t + 1 + START)
                for n in range(4):
                    z = min((n + 1) * 8, TILES) - n * 8
                    last = nc.scalar.activation(
                        adj_t[b][:, n * 8 * ROWS:(n * 8 + z) * ROWS].rearrange("p (u s) -> p u s", s=ROWS),
                        ps_t[n][0:ROWS, 0:z * 128].rearrange("p (u s) -> p u s", s=128)[:, :, 0:ROWS], ACT.Copy)
                last.then_inc(t_read, 1)

            two_by_two(act, TILES, tile)

        @block.tensor
        def _(pe):
            pe.nop().then_inc(win_done, 2)
            pe.nop().then_inc(more_used, 1)
            pe.wait_ge(table_ready, 1 + START)
            more = pe.value_load(table[:, WINS:WINS + 1], min_val=1, max_val=MORE_MAX)

            def add(banks, ones, keys, start, stop):
                for bank, (a, z) in enumerate(SPLIT):
                    last = nc.tensor.matmul(banks[bank][0:ROWS, 0:z - a], ones, keys[:, a:z],
                                            start=start, stop=stop)
                return last

            def tile(t, b, i):
                for w in range(WPT):
                    win, half = t * WPT + w, (b * WPT + w) % 2

                    def fixed(j, start, stop):
                        pe.wait_ge(one_ready, win * FIXED + j + 1 + START)
                        return add(ps_w[w % 2], one_s[half][:, j, :], one_k[half][:, j, :], start, stop)

                    pe.wait_ge(win_read, (win if w == 0 else win - 1) + START)
                    for j in range(FIXED - 1):
                        fixed(j, j == 0, False)
                    with pe.Fori(0, more) as n:
                        pe.wait_ge(more_ready, win * more + n + 1 + START)
                        add(ps_w[w % 2], more_s[:], more_k[:], False, False).then_inc(more_used, 1)
                    fixed(FIXED - 1, False, True).then_inc(win_done, 1)
                pe.wait_ge(win_read, t * WPT + WPT + START)
                pe.wait_ge(t_read, t + START)
                for s in range(TILES):
                    last = nc.tensor.transpose(ps_t[s // 8][0:ROWS, (s % 8) * 128:(s % 8) * 128 + ROWS],
                                               adj[b][:, s, :], K.ident_b[0:ROWS, 0:ROWS])
                last.then_inc(t_done, 1)

            two_by_two(pe, TILES, tile)


def load_tiles(sp, buffers, source, arrived, used):
    def tile(t, b, i):
        sp.wait_ge(used, t + START)
        rows_dma(sp, buffers[b], source[bass.ds(t, 1)].rearrange("t p n -> (t p) n"), arrived[b])
    two_by_two(sp, TILES, tile)


def gin_down(nc, K):
    with ExitStack() as st:
        m = Memory(nc, st, "down")
        adj = [m.sb(f"adj{i}", (ROWS, TILES * ROWS), BF16) for i in range(2)]
        ps = [m.ps(f"ps{i}") for i in range(2)]
        arrived = [m.sem(f"in{i}") for i in range(2)]
        adj_used, done, used = m.sem("adj_used"), m.sem("done"), m.sem("used")
        block = m.block()

        @block.sync
        def _(sp):
            load_tiles(sp, adj, K.adj, arrived, done)

        @block.tensor
        def _(pe):
            pe.nop().then_inc(done, 1)

            def tile(t, b, i):
                pe.wait_ge(arrived[b], (i + 1) * 32 + START)
                pe.wait_ge(used, (t if b == 0 else t - 1) + START)
                for s in range(TILES):
                    last = nc.tensor.matmul(ps[b][0:ROWS, 0:193], adj[b][:, s * ROWS:(s + 1) * ROWS],
                                            K.Yp[:, s, 0:193], start=(s == 0), stop=(s == TILES - 1))
                last.then_inc(done, 1)
            two_by_two(pe, TILES, tile)

        @block.vector
        def _(dve):
            def tile(t, b, i):
                dve.wait_ge(done, t + 2 + START)
                nc.vector.tensor_reduce(K.AGG[:, t, :], ps[b][0:ROWS, 0:192].rearrange("p (i f) -> p f i", i=3),
                                        AX.X, ALU.add)
                nc.vector.tensor_copy(K.DEG[:, bass.ds(t, 1)], ps[b][0:ROWS, 192:193]).then_inc(used, 1)
            two_by_two(dve, TILES, tile)


def gin_up(nc, K):
    cuts = [(a, min(a + 500, NODES)) for a in range(0, NODES, 500)]
    with ExitStack() as st:
        m = Memory(nc, st, "up")
        adj_t = [m.sb(f"adj_t{i}", (ROWS, NODES), BF16) for i in range(2)]
        agg_t = m.sb("agg_t", (128, NODES))
        ps = [m.ps(f"ps{i}") for i in range(7)]
        arrived = [m.sem(f"in{i}") for i in range(2)]
        used, summed, moved, turned = m.sem("used"), m.sem("summed"), m.sem("moved"), m.sem("turned")
        block = m.block()

        @block.sync
        def _(sp):
            load_tiles(sp, adj_t, K.adj_t, arrived, used)

        @block.tensor
        def _(pe):
            pe.nop().then_inc(used, 1)
            for i, (a, z) in enumerate(cuts):
                zero_bank(nc, K, ps[i], z - a, start=True)

            def tile(t, b, i):
                pe.wait_ge(arrived[b], (i + 1) * 32 + START)
                for half in range(2):
                    for n, (a, z) in enumerate(cuts):
                        last = nc.tensor.matmul(ps[n][:, 0:z - a], K.Yp[:, t, half * 128:half * 128 + 128],
                                                adj_t[b][:, a:z], start=False, stop=False)
                last.then_inc(used, 1)
            two_by_two(pe, TILES, tile)
            for i, (a, z) in enumerate(cuts):
                last = zero_bank(nc, K, ps[i], z - a, start=False)
            last.then_inc(summed, 1)
            pe.wait_ge(moved, len(cuts) + START)
            for t in range(TILES):
                last = nc.tensor.transpose(ps[t // 4][0:ROWS, (t % 4) * 128:(t % 4) * 128 + 128],
                                           agg_t[:, t * ROWS:(t + 1) * ROWS], K.ident_f[:])
            last.then_inc(turned, 1)

        @block.scalar
        def _(act):
            act.wait_ge(summed, 1 + START)
            for i, (a, z) in enumerate(cuts):
                nc.scalar.activation(agg_t[:, a:z], ps[i][:, 0:z - a], ACT.Copy).then_inc(moved, 1)

        @block.vector
        def _(dve):
            dve.wait_ge(turned, 1 + START)
            for i in range(7):
                n = min(4, TILES - 4 * i)
                nc.vector.tensor_reduce(K.AGG[:, 4 * i:4 * i + n, :],
                                        ps[i][0:ROWS, 0:n * 128].rearrange("p (t i f) -> p t f i", i=2, f=64),
                                        AX.X, ALU.add)


def gin_tail(nc, K, stage, D, way, base, out):
    first = way == "down"
    with ExitStack() as st:
        m = Memory(nc, st, stage)
        w2 = m.sb("w2", (64, C))
        wy = m.sb("wy", (128, KC, 64))
        eps1 = m.sb("eps1", (ROWS, 1))
        narrow = m.sb("narrow", (ROWS, 2, 64))
        wide = m.sb("wide", (ROWS, 3, C))
        stats, mv = m.sb("stats", (ROWS, GROUP, 6)), m.sb("mv", (ROWS, GROUP, 2))
        var_eps, std, rstd = (m.sb(n, (ROWS, GROUP)) for n in ("var_eps", "std", "rstd"))
        hid = m.sb("hid", (ROWS, GROUP, 64))
        hid_t = m.sb("hid_t", (64, GROWS))
        row = m.sb("row", (ROWS, GROUP, C))
        xt = m.sb("xt", (128, KC, GROWS))
        rest = m.sb("rest", (ROWS, 64))
        ps_t = [m.ps(f"ps_t{i}") for i in range(3)]
        ps_h = [m.ps(f"ps_h{i}") for i in range(2)]
        ps_o = [m.ps(f"ps_o{i}") for i in range(2)]
        ps_y = m.ps("ps_y")
        w_in, var_ready, std_ready, hid_ready, h_done, hid_moved, o_done, o_used = (
            m.sem(n) for n in ("w_in", "var_ready", "std_ready", "hid_ready", "h_done", "hid_moved",
                               "o_done", "o_used"))
        row_ready, t_done, xt_ready, y_done, y_used = (
            m.sem(n) for n in ("row_ready", "t_done", "xt_ready", "y_done", "y_used"))
        block = m.block()
        loads = 8 if first else 7

        @block.sync
        def _(sp):
            g = "L0_gnn_"
            sp.dma_start(w2[:], D[g + "W2_" + way]).then_inc(w_in, 16)
            sp.dma_start(eps1[:], D[g + "eps_" + way].partition_broadcast(ROWS)).then_inc(w_in, 16)
            sp.dma_start(narrow[:, 0, :], D[g + "lng_" + way].partition_broadcast(ROWS)).then_inc(w_in, 16)
            sp.dma_start(narrow[:, 1, :], D[g + "lnb_" + way].partition_broadcast(ROWS)).then_inc(w_in, 16)
            n = "1" if first else "2"
            sp.dma_start(wide[:, 0, :], D[g + f"ln{n}_g"].partition_broadcast(ROWS)).then_inc(w_in, 16)
            sp.dma_start(wide[:, 1, :], D[g + f"ln{n}_b"].partition_broadcast(ROWS)).then_inc(w_in, 16)
            sp.dma_start(wide[:, 2, :], D[g + "dir_emb"][0 if first else 1].partition_broadcast(ROWS)).then_inc(w_in, 16)
            if first:
                sp.dma_start(wy[:], D[g + "W1_up"].rearrange("(k p) o -> p k o", p=128)).then_inc(w_in, 16)
            sp.wait_ge(w_in, loads * 16 + START)

        @block.vector
        def _(dve):
            v = nc.vector

            def normalise(buf, scale, shift, width, n, g):
                layer_norm_stats(dve, nc, lambda u: buf[:, u, :], stats, mv, var_eps, GROUP).then_inc(var_ready, 1)
                dve.wait_ge(std_ready, g * 2 + 1 + n + START)
                v.reciprocal(rstd[:], std[:])
                dve.drain()
                for u in range(GROUP):
                    v.tensor_scalar(buf[:, u, :], buf[:, u, :], mv[:, u, 0:1], rstd[:, u:u + 1],
                                    ALU.subtract, ALU.mult)
                dve.drain()
                v.tensor_tensor(buf[:], buf[:], scale.unsqueeze(1).broadcast_to([ROWS, GROUP, width]), ALU.mult)
                dve.drain()
                return v.tensor_tensor(buf[:], buf[:], shift.unsqueeze(1).broadcast_to([ROWS, GROUP, width]), ALU.add)

            dve.wait_ge(w_in, loads * 16 + START)
            v.tensor_scalar(eps1[:], eps1[:], 1.0, None, ALU.add)
            if first:
                v.memset(K.Yp[:, :, 192:256], 0.0)
            dve.drain()
            with dve.Fori(0, GROUPS) as g:
                tiles = bass.ds(g * GROUP, GROUP)
                dve.wait_ge(h_done, g + START)
                v.scalar_tensor_tensor(hid[:], K.Y[:, tiles, 0:64], eps1[:], K.AGG[:, tiles, :], ALU.mult, ALU.add)
                dve.drain()
                normalise(hid, narrow[:, 0, :], narrow[:, 1, :], 64, 0, g)
                dve.drain()
                v.tensor_scalar(hid[:], hid[:], 0.0, None, ALU.max).then_inc(hid_ready, 1)
                if first:
                    dve.wait_ge(t_done, g + START)
                for u in range(GROUP):
                    t = g * GROUP + u
                    dve.wait_ge(o_done, t + 1 + START)
                    v.tensor_tensor(row[:, u, :], ps_o[u % 2][0:ROWS, 0:C], base[:, t, :], ALU.add).then_inc(o_used, 1)
                dve.drain()
                v.tensor_tensor(row[:], row[:], wide[:, 2, :].unsqueeze(1).broadcast_to([ROWS, GROUP, C]), ALU.add)
                dve.drain()
                v.tensor_scalar(row[:], row[:], 0.0, None, ALU.max)
                dve.drain()
                last = normalise(row, wide[:, 0, :], wide[:, 1, :], C, 1, g)
                if first:
                    last.then_inc(row_ready, 1)
                    dve.drain()
                    v.tensor_copy(out[:, tiles, :], row[:])
                    for u in range(GROUP):
                        t = g * GROUP + u
                        dve.wait_ge(y_done, t + 1 + START)
                        carry(dve, m)
                        v.tensor_copy(K.Y[:, t, 0:64], ps_y[0:ROWS, 0:64]).then_inc(y_used, 1)
                        dve.drain()
                        split3(dve, nc, K.Y[:, t, 0:64], rest[:],
                               [K.Yp[:, t, i * 64:(i + 1) * 64] for i in range(3)])
                else:
                    dve.drain()
                    v.tensor_tensor(K.X[:, tiles, :], K.X[:, tiles, :], row[:], ALU.add)

        @block.scalar
        def _(act):
            with act.Fori(0, GROUPS) as g:
                act.wait_ge(var_ready, g * 2 + 1 + START)
                nc.scalar.activation(std[:], var_eps[:], ACT.Sqrt).then_inc(std_ready, 1)
                act.wait_ge(h_done, g + 1 + START)
                nc.scalar.activation(hid_t[:, 0:500], ps_h[0][0:64, 0:500], ACT.Copy)
                nc.scalar.activation(hid_t[:, 500:625], ps_h[1][0:64, 0:125], ACT.Copy).then_inc(hid_moved, 1)
                act.wait_ge(var_ready, g * 2 + 2 + START)
                nc.scalar.activation(std[:], var_eps[:], ACT.Sqrt).then_inc(std_ready, 1)
                if first:
                    act.wait_ge(t_done, g + 1 + START)
                    copy_transposed(nc, xt, ps_t).then_inc(xt_ready, 1)

        @block.tensor
        def _(pe):
            pe.wait_ge(w_in, loads * 16 + START)
            with pe.Fori(0, GROUPS) as g:
                pe.wait_ge(hid_ready, g + 1 + START)
                pe.wait_ge(hid_moved, g + START)
                carry(pe, m)
                for u in range(GROUP):
                    out_h = ps_h[0][0:64, u * ROWS:(u + 1) * ROWS] if u < 4 else ps_h[1][0:64, 0:ROWS]
                    last = nc.tensor.transpose(out_h, hid[:, u, :], K.ident_f[0:ROWS, 0:ROWS])
                last.then_inc(h_done, 1)
                pe.wait_ge(hid_moved, g + 1 + START)
                for u in range(GROUP):
                    t = g * GROUP + u
                    pe.wait_ge(o_used, (t if u == 0 else t - 1) + START)
                    nc.tensor.matmul(ps_o[u % 2][0:ROWS, 0:C], hid_t[:, u * ROWS:(u + 1) * ROWS], w2[:],
                                     start=True, stop=True).then_inc(o_done, 1)
                if first:
                    pe.wait_ge(row_ready, g + 1 + START)
                    pe.wait_ge(xt_ready, g + START)
                    transpose_group(nc, K, row, ps_t).then_inc(t_done, 1)
                    pe.wait_ge(xt_ready, g + 1 + START)
                    for u in range(GROUP):
                        t = g * GROUP + u
                        pe.wait_ge(y_used, t + START)
                        for k in range(KC):
                            last = nc.tensor.matmul(ps_y[0:ROWS, 0:64], xt[:, k, u * ROWS:(u + 1) * ROWS],
                                                    wy[:, k, :], start=(k == 0), stop=(k == KC - 1))
                        last.then_inc(y_done, 1)


class Experts:

    def __init__(self, layer):
        self.layer = layer
        self.n = 8 if layer == 0 else 16
        self.slot_tiles = 2 * NODES // 128 + self.n
        self.slot_tiles += 1 - self.slot_tiles % 2
        self.hidden = 512


def route(nc, K, D, X):
    E, L0 = X.n, X.layer == 0
    names = ("L0_ffn_Wr", "L0_ffn_br") if L0 else ("L1_ffn_gate_w", "L1_ffn_gate_b")
    with ExitStack() as st:
        m = Memory(nc, st, f"route{X.layer}")
        wr = m.sb("wr", (128, KC, E))
        bias = m.sb("bias", (ROWS, E))
        wide = m.sb("wide", (ROWS, 2, C))
        stats, mv = m.sb("stats", (ROWS, GROUP, 6)), m.sb("mv", (ROWS, GROUP, 2))
        var_eps, std, rstd = (m.sb(n, (ROWS, GROUP)) for n in ("var_eps", "std", "rstd"))
        row = m.sb("row", (ROWS, GROUP, C))
        xt = m.sb("xt", (128, KC, GROWS))
        logit = m.sb("logit", (ROWS, GROUP, E))
        top, top_at = m.sb("top", (ROWS, GROUP, 8)), m.sb("top_at", (ROWS, GROUP, 8), mybir.dt.uint32)
        at_f = m.sb("at_f", (ROWS, GROUP, 8))
        gap, grown, denom = (m.sb(n, (ROWS, GROUP)) for n in ("gap", "grown", "denom"))
        pick = m.sb("pick", (ROWS, TILES, 2, E))
        both = m.sb("both", (ROWS, TILES, E))
        below = m.sb("below", (ROWS, ROWS))
        keep = m.sb("keep", (ROWS, E, TILES))
        total = m.sb("total", (ROWS, E, TILES))
        run = m.sb("run", (ROWS, E, TILES))
        base = m.sb("base", (ROWS, 4, E))
        base_i = m.sb("base_i", (ROWS, E), I32)
        place = m.sb("place", (ROWS, TILES, E))
        picked = m.sb("picked", (ROWS, TILES, 2, E))
        slot_f = m.sb("slot_f", (ROWS, TILES, 2))
        tile_no = m.sb("tile_no", (ROWS, X.slot_tiles))
        passed = m.sb("passed", (1, X.slot_tiles, E))
        owner = m.sb("owner", (1, X.slot_tiles))
        node = m.sb("node", (ROWS, TILES), I32)
        slot_g, node_g = m.sb("slot_g", (ROWS, GROUP * 2), I32), m.sb("node_g", (ROWS, GROUP), I32)
        blank = m.sb("blank", (X.slot_tiles, 128), I32)
        ps_t = [m.ps(f"ps_t{i}") for i in range(3)]
        ps_l, ps_p, ps_s = m.ps("ps_l"), m.ps("ps_p"), m.ps("ps_s")
        w_in, var_ready, std_ready, row_ready, saved, t_done, xt_ready, l_done, l_used, gap_ready, grown_ready = (
            m.sem(n) for n in ("w_in", "var_ready", "std_ready", "row_ready", "saved", "t_done", "xt_ready",
                               "l_done", "l_used", "gap_ready", "grown_ready"))
        picks_ready, counted, slots_ready, made, blanked, copied = (
            m.sem(n) for n in ("picks_ready", "counted", "slots_ready", "made", "blanked", "copied"))
        scattered = m.sem("scattered", start=0)
        block = m.block()
        loads = 4 if L0 else 2
        norms = 2 if L0 else 1

        @block.sync
        def _(sp):
            sp.dma_start(wr[:], D[names[0]].rearrange("(k p) o -> p k o", p=128)).then_inc(w_in, 16)
            sp.dma_start(bias[:], D[names[1]].partition_broadcast(ROWS)).then_inc(w_in, 16)
            if L0:
                sp.dma_start(wide[:, 0, :], D["L0_ffn_gamma"].partition_broadcast(ROWS)).then_inc(w_in, 16)
                sp.dma_start(wide[:, 1, :], D["L0_ffn_beta"].partition_broadcast(ROWS)).then_inc(w_in, 16)
            sp.wait_ge(made, 1 + START)
            sp.dma_start(K.slot_row[0:X.slot_tiles * 128, :].rearrange("(t s) o -> t (s o)", s=128), blank[:]).then_inc(blanked, 16)
            with sp.Fori(0, GROUPS) as g:
                sp.wait_ge(row_ready, g + 1 + START)
                rows_dma(sp, K.rows_dram[bass.ds(g * GROUP, GROUP)].rearrange("t p c -> p t c"), row, saved)
            sp.wait_ge(saved, GROUPS * 32 + START)
            sp.wait_ge(w_in, loads * 16 + START)
            sp.wait_ge(blanked, 16 + START)

        @block.gpsimd
        def _(pool):
            nc.gpsimd.memset(below[:], 1.0).then_inc(copied, 1)
            pool.wait_ge(copied, 1 + START)
            nc.gpsimd.affine_select(out=below[:], in_=below[:], compare_op=ALU.is_gt, fill=0.0,
                                    base=0, pattern=[[1, ROWS]], channel_multiplier=-1)
            nc.gpsimd.iota(tile_no[:], [[128, X.slot_tiles]], base=0, channel_multiplier=0,
                           allow_small_or_imprecise_dtypes=True)
            nc.gpsimd.iota(node[:], [[ROWS, TILES]], base=0, channel_multiplier=1)
            nc.gpsimd.memset(blank[:], 0).then_inc(made, 1)
            pool.wait_ge(slots_ready, 1 + START)
            pool.wait_ge(blanked, 16 + START)
            with pool.Fori(0, GROUPS) as g:
                nc.gpsimd.tensor_copy(slot_g[:], K.slot[:, bass.ds(g * (GROUP * 2), GROUP * 2)])
                nc.gpsimd.tensor_copy(node_g[:], node[:, bass.ds(g * GROUP, GROUP)]).then_inc(copied, 1)
                pool.wait_ge(copied, g + 2 + START)
                carry(pool, m)
                for n in range(GROUP * 2):
                    nc.gpsimd.indirect_dma_start(
                        out=K.slot_row[:, :], out_offset=bass.IndirectOffsetOnAxis(ap=slot_g[:, n:n + 1], axis=0),
                        in_=node_g[:, n // 2:n // 2 + 1], in_offset=None).then_inc(scattered, 16)
                pool.wait_ge(scattered, (g + 1) * (GROUP * 2 * 16))

        @block.vector
        def _(dve):
            v = nc.vector

            def normalise(src, out, g, n):
                layer_norm_stats(dve, nc, src, stats, mv, var_eps, GROUP).then_inc(var_ready, 1)
                dve.wait_ge(std_ready, g * norms + n + 1 + START)
                v.reciprocal(rstd[:], std[:])
                dve.drain()
                for u in range(GROUP):
                    last = v.tensor_scalar(out[:, u, :], src(u), mv[:, u, 0:1], rstd[:, u:u + 1],
                                           ALU.subtract, ALU.mult)
                return last

            dve.wait_ge(w_in, loads * 16 + START)
            dve.wait_ge(made, 1 + START)
            with dve.Fori(0, GROUPS) as g:
                tiles = bass.ds(g * GROUP, GROUP)
                dve.wait_ge(t_done, g + START)
                dve.wait_ge(saved, g * 32 + START)
                last = normalise(lambda u: K.X[:, g * GROUP + u, :], row, g, 0)
                if L0:
                    dve.drain()
                    normalise(lambda u: row[:, u, :], row, g, 1)
                    dve.drain()
                    v.tensor_tensor(row[:], row[:], wide[:, 0, :].unsqueeze(1).broadcast_to([ROWS, GROUP, C]), ALU.mult)
                    dve.drain()
                    last = v.tensor_tensor(row[:], row[:], wide[:, 1, :].unsqueeze(1).broadcast_to([ROWS, GROUP, C]), ALU.add)
                last.then_inc(row_ready, 1)
                dve.wait_ge(l_done, g + 1 + START)
                v.tensor_tensor(logit[:], ps_l[0:ROWS, 0:GROUP * E].rearrange("p (u e) -> p u e", e=E),
                                bias[:].unsqueeze(1).broadcast_to([ROWS, GROUP, E]), ALU.add).then_inc(l_used, 1)
                dve.drain()
                for u in range(GROUP):
                    v.max(top[:, u, :], logit[:, u, :])
                dve.drain()
                for u in range(GROUP):
                    v.max_index(top_at[:, u, :], top[:, u, :], logit[:, u, :])
                v.tensor_tensor(gap[:], top[:, :, 1], top[:, :, 0], ALU.subtract).then_inc(gap_ready, 1)
                dve.drain()
                v.tensor_copy(at_f[:], top_at[:])
                dve.drain()
                for n in range(2):
                    v.tensor_tensor(pick[:, tiles, n, :],
                                    K.number_f[0:ROWS, 0:E].unsqueeze(1).broadcast_to([ROWS, GROUP, E]),
                                    at_f[:, :, n:n + 1].broadcast_to([ROWS, GROUP, E]), ALU.is_equal)
                dve.wait_ge(grown_ready, g + 1 + START)
                v.tensor_scalar(denom[:], grown[:], 1.0, None, ALU.add)
                dve.drain()
                v.reciprocal(denom[:], denom[:])
                dve.drain()
                v.tensor_copy(K.gate[:, tiles, 0], denom[:])
                v.tensor_tensor(K.gate[:, tiles, 1], grown[:], denom[:], ALU.mult)
                dve.drain()
            v.tensor_tensor(both[:], pick[:, :, 0, :], pick[:, :, 1, :], ALU.add).then_inc(picks_ready, 1)
            v.memset(keep[:], 1.0)
            dve.drain()
            v.memset(keep[:, :, 0:1], 0.0)
            dve.wait_ge(counted, 1 + START)
            v.tensor_copy(total[:], ps_s[0:ROWS, 0:TILES * E].rearrange("p (t e) -> p e t", e=E))
            dve.drain()
            v.tensor_tensor_scan(run[:].rearrange("p e t -> p (e t)"), keep[:].rearrange("p e t -> p (e t)"),
                                 total[:].rearrange("p e t -> p (e t)"), 0.0, ALU.mult, ALU.add)
            dve.drain()
            v.tensor_scalar(base[:, 0, :], run[:, :, TILES - 1], 127.0, None, ALU.add)
            v.tensor_tensor(total[:], run[:], total[:], ALU.subtract)
            dve.drain()
            v.tensor_copy(base_i[:], base[:, 0, :])
            dve.drain()
            v.tensor_scalar(base_i[:], base_i[:], 7, 7, ALU.arith_shift_right, ALU.logical_shift_left)
            dve.drain()
            v.tensor_copy(base[:, 0, :], base_i[:])
            v.memset(base[:, 1, :], 1.0)
            dve.drain()
            v.tensor_tensor_scan(base[:, 2, :], base[:, 1, :], base[:, 0, :], 0.0, ALU.mult, ALU.add)
            dve.drain()
            v.tensor_tensor(base[:, 3, :], base[:, 2, :], base[:, 0, :], ALU.subtract)
            v.tensor_tensor(place[:], ps_p[0:ROWS, 0:TILES * E].rearrange("p (t e) -> p t e", e=E),
                            total[:].rearrange("p e t -> p t e"), ALU.add)
            v.tensor_tensor(passed[:], tile_no[0:1].unsqueeze(2).broadcast_to([1, X.slot_tiles, E]),
                            base[0:1, 2, :].unsqueeze(1).broadcast_to([1, X.slot_tiles, E]), ALU.is_ge)
            dve.drain()
            v.tensor_tensor(place[:], place[:], base[:, 3, :].unsqueeze(1).broadcast_to([ROWS, TILES, E]), ALU.add)
            v.tensor_reduce(owner[:], passed[:], AX.X, ALU.add)
            dve.drain()
            v.tensor_scalar(K.owner[:, 0:X.slot_tiles], owner[:], float(E - 1), None, ALU.min)
            for n in range(2):
                v.tensor_tensor(picked[:, :, n, :], pick[:, :, n, :], place[:], ALU.mult)
            dve.drain()
            v.tensor_reduce(slot_f[:], picked[:], AX.X, ALU.add)
            dve.drain()
            v.tensor_copy(K.slot[:], slot_f[:].rearrange("p t n -> p (t n)")).then_inc(slots_ready, 1)

        @block.scalar
        def _(act):
            with act.Fori(0, GROUPS) as g:
                for n in range(norms):
                    act.wait_ge(var_ready, g * norms + n + 1 + START)
                    nc.scalar.activation(std[:], var_eps[:], ACT.Sqrt).then_inc(std_ready, 1)
                act.wait_ge(t_done, g + 1 + START)
                copy_transposed(nc, xt, ps_t).then_inc(xt_ready, 1)
                act.wait_ge(gap_ready, g + 1 + START)
                nc.scalar.activation(grown[:], gap[:], ACT.Exp).then_inc(grown_ready, 1)

        @block.tensor
        def _(pe):
            pe.wait_ge(w_in, loads * 16 + START)
            with pe.Fori(0, GROUPS) as g:
                pe.wait_ge(row_ready, g + 1 + START)
                pe.wait_ge(xt_ready, g + START)
                transpose_group(nc, K, row, ps_t).then_inc(t_done, 1)
                pe.wait_ge(xt_ready, g + 1 + START)
                pe.wait_ge(l_used, g + START)
                for u in range(GROUP):
                    for k in range(KC):
                        last = nc.tensor.matmul(ps_l[0:ROWS, u * E:(u + 1) * E], xt[:, k, u * ROWS:(u + 1) * ROWS],
                                                wr[:, k, :], start=(k == 0), stop=(k == KC - 1))
                last.then_inc(l_done, 1)
            pe.wait_ge(picks_ready, 1 + START)
            flat = both[:].rearrange("p t e -> p (t e)")
            nc.tensor.matmul(ps_p[0:ROWS, 0:TILES * E], below[:], flat, start=True, stop=True)
            nc.tensor.matmul(ps_s[0:ROWS, 0:TILES * E], K.ones[0:ROWS, 0:ROWS], flat, start=True, stop=True).then_inc(counted, 1)


def ahead(eng, count, early, late):
    early(0, 0, 0)
    with eng.Fori(0, count // 2) as i:
        early(i * 2 + 1, 1, i)
        late(i * 2, 0, i)
        early(i * 2 + 2, 0, i + 1)
        late(i * 2 + 1, 1, i)
    late(count - 1, 0, count // 2)


def experts(nc, K, D, X):
    L0, H = X.layer == 0, X.hidden
    HB = H // 128
    with ExitStack() as st:
        m = Memory(nc, st, f"experts{X.layer}")
        idx = [m.sb(f"idx{i}", (128, 1), I32) for i in range(2)]
        rows = [m.sb(f"rows{i}", (128, C)) for i in range(2)]
        xt = [m.sb(f"xt{i}", (128, KC, 128)) for i in range(2)]
        w1 = [m.sb(f"w1_{i}", (128, KC, H)) for i in range(2)]
        w2 = [m.sb(f"w2_{i}", (128, KC, H)) for i in range(2)]
        w3 = [m.sb(f"w3_{i}", (128, HB, C)) for i in range(2)]
        b1 = [m.sb(f"b1_{i}", (128, HB)) for i in range(2)]
        b2 = [m.sb(f"b2_{i}", (128, C)) for i in range(2)]
        gate = [m.sb(f"gate{i}", (128, HB * 128)) for i in range(2)]
        hid = [m.sb(f"hid{i}", (128, HB * 128)) for i in range(2)]
        out = [m.sb(f"out{i}", (128, C)) for i in range(2)]
        ps_t = m.ps("ps_t")
        ps_h = [m.ps(f"ps_h{i}") for i in range(2)]
        ps_g = [m.ps(f"ps_g{i}") for i in range(2)]
        ps_o = [m.ps(f"ps_o{i}") for i in range(2)]
        idx_in, rows_in = ([m.sem(f"{n}{i}", start=0) for i in range(2)] for n in ("idx_in", "rows_in"))
        up_in, down_in, stored = ([m.sem(f"{n}{i}") for i in range(2)] for n in ("up_in", "down_in", "stored"))
        rows_used, xt_ready, h_done, h_ready, hid_ready, o_done, out_ready = (
            m.sem(n) for n in ("rows_used", "xt_ready", "h_done", "h_ready", "hid_ready", "o_done", "out_ready"))
        block = m.block()
        names = ("L0_ffn_W1", None, "L0_ffn_W2") if L0 else ("L1_ffn_w1", "L1_ffn_w2", "L1_ffn_w3")
        LOADS = 2 * 16

        @block.sync
        def _(sp):
            def tile(t, b, i):
                e = sp.value_load(K.owner[:, bass.ds(t, 1)], min_val=0, max_val=X.n - 1)
                one = bass.ds(e, 1)

                def matrix(buf, name, sem):
                    sp.dma_start(buf[b][:], D[name][one].rearrange("e (k p) h -> p (e k) h", p=128)).then_inc(sem[b], 16)

                sp.wait_ge(h_done, t + START)
                matrix(w1, names[0], up_in)
                if L0:
                    sp.wait_ge(hid_ready, (t if b == 0 else t - 1) + START)
                    sp.dma_start(b1[b][:], D["L0_ffn_b1"][one].rearrange("e p h -> p (e h)")).then_inc(up_in[b], 16)
                else:
                    matrix(w2, names[1], up_in)
                sp.wait_ge(o_done, t + START)
                matrix(w3, names[2], down_in)
                if L0:
                    sp.wait_ge(out_ready, t + START)
                    sp.dma_start(b2[b][:], D["L0_ffn_b2"][one].rearrange("e o -> (e o)").partition_broadcast(128)).then_inc(down_in[b], 16)
            two_by_two(sp, X.slot_tiles, tile)

        @block.gpsimd
        def _(pool):
            def index(t, b, i):
                pool.dma_start(idx[b][:], K.slot_row[bass.ds(t * 128, 128), :]).then_inc(idx_in[b], 16)

            def gather(t, b, i):
                pool.wait_ge(rows_used, t + START)
                pool.wait_ge(idx_in[b], (i + 1) * 16)
                carry(pool, m)
                nc.gpsimd.indirect_dma_start(
                    out=rows[b][:], out_offset=None, in_=K.rows_dram.rearrange("t p c -> (t p) c"),
                    in_offset=bass.IndirectOffsetOnAxis(ap=idx[b][:, 0:1], axis=0)).then_inc(rows_in[b], 16)
                pool.wait_ge(rows_in[b], (i + 1) * 16)
            ahead(pool, X.slot_tiles, index, gather)

        @block.tensor
        def _(pe):
            pe.nop().then_inc(rows_used, 1)
            pe.nop().then_inc(h_done, 1)
            pe.nop().then_inc(o_done, 1)

            def turn(t, b, i):
                pe.wait_ge(rows_in[b], (i + 1) * 16)
                pe.wait_ge(xt_ready, t + START)
                for k in range(KC):
                    last = nc.tensor.transpose(ps_t[:, k * 128:(k + 1) * 128], rows[b][:, k * 128:(k + 1) * 128],
                                               K.ident_f[:])
                last.then_inc(rows_used, 1)

            def up(t, b, i):
                pe.wait_ge(xt_ready, t + 1 + START)
                pe.wait_ge(up_in[b], (i + 1) * LOADS + START)
                for w, ps in ((w1, ps_h),) if L0 else ((w1, ps_h), (w2, ps_g)):
                    for h in range(HB):
                        for k in range(KC):
                            last = nc.tensor.matmul(ps[b][:, h * 128:(h + 1) * 128],
                                                    w[b][:, k, h * 128:(h + 1) * 128], xt[b][:, k, :],
                                                    start=(k == 0), stop=(k == KC - 1))
                last.then_inc(h_done, 1)

            def down(t, b, i):
                pe.wait_ge(hid_ready, t + 1 + START)
                pe.wait_ge(down_in[b], (i + 1) * (LOADS if L0 else 16) + START)
                pe.wait_ge(out_ready, t + START)
                for h in range(HB):
                    last = nc.tensor.matmul(ps_o[b][:, 0:C], hid[b][:, h * 128:(h + 1) * 128], w3[b][:, h, :],
                                            start=(h == 0), stop=(h == HB - 1))
                last.then_inc(o_done, 1)

            last = X.slot_tiles - 1
            turn(0, 0, 0)
            up(0, 0, 0)
            turn(1, 1, 0)
            with pe.Fori(0, (last - 2) // 2) as i:
                up(i * 2 + 1, 1, i)
                turn(i * 2 + 2, 0, i + 1)
                down(i * 2, 0, i)
                up(i * 2 + 2, 0, i + 1)
                turn(i * 2 + 3, 1, i + 1)
                down(i * 2 + 1, 1, i)
            up(last - 1, 1, last // 2 - 1)
            turn(last, 0, last // 2)
            down(last - 2, 0, last // 2 - 1)
            up(last, 0, last // 2)
            down(last - 1, 1, last // 2 - 1)
            down(last, 0, last // 2)

        @block.scalar
        def _(act):
            def move(t, b, i):
                act.wait_ge(rows_used, t + 2 + START)
                nc.scalar.activation(xt[b][:].rearrange("p k s -> p (k s)"), ps_t[:, 0:C], ACT.Copy).then_inc(xt_ready, 1)

            def activate(t, b, i):
                act.wait_ge(h_done, t + 2 + START)
                if L0:
                    act.wait_ge(up_in[b], (i + 1) * LOADS + START)
                    act.wait_ge(o_done, t + START)
                    for h in range(HB):
                        last = nc.scalar.activation(hid[b][:, h * 128:(h + 1) * 128], ps_h[b][:, h * 128:(h + 1) * 128],
                                                    ACT.Gelu, bias=b1[b][:, h:h + 1])
                    last.then_inc(hid_ready, 1)
                else:
                    act.wait_ge(hid_ready, (t if b == 0 else t - 1) + START)
                    nc.scalar.activation(gate[b][:], ps_h[b][:], ACT.Silu).then_inc(h_ready, 1)

            def store(t, b, i):
                act.wait_ge(out_ready, t + 2 + START)
                act.dma_start(K.slot_out[bass.ds(t * 128, 128), :], out[b][:]).then_inc(stored[b], 16)

            last = X.slot_tiles - 1
            move(0, 0, 0)
            move(1, 1, 0)
            activate(0, 0, 0)
            with act.Fori(0, (last - 2) // 2) as i:
                move(i * 2 + 2, 0, i + 1)
                activate(i * 2 + 1, 1, i)
                store(i * 2, 0, i)
                move(i * 2 + 3, 1, i + 1)
                activate(i * 2 + 2, 0, i + 1)
                store(i * 2 + 1, 1, i)
            move(last, 0, last // 2)
            activate(last - 1, 1, last // 2 - 1)
            store(last - 2, 0, last // 2 - 1)
            activate(last, 0, last // 2)
            store(last - 1, 1, last // 2 - 1)
            store(last, 0, last // 2)
            act.wait_ge(stored[0], (X.slot_tiles // 2 + 1) * 16 + START)
            act.wait_ge(stored[1], (X.slot_tiles // 2) * 16 + START)

        @block.vector
        def _(dve):
            dve.nop().then_inc(out_ready, 1)

            def product(t, b, i):
                if not L0:
                    dve.wait_ge(h_ready, t + 1 + START)
                    dve.wait_ge(o_done, t + START)
                    nc.vector.tensor_tensor(hid[b][:], gate[b][:], ps_g[b][:], ALU.mult).then_inc(hid_ready, 1)

            def result(t, b, i):
                dve.wait_ge(o_done, t + 2 + START)
                dve.wait_ge(stored[b], i * 16 + START)
                if L0:
                    dve.wait_ge(down_in[b], (i + 1) * LOADS + START)
                    nc.vector.tensor_tensor(out[b][:], ps_o[b][:, 0:C], b2[b][:], ALU.add).then_inc(out_ready, 1)
                else:
                    nc.vector.tensor_copy(out[b][:], ps_o[b][:, 0:C]).then_inc(out_ready, 1)
            ahead(dve, X.slot_tiles, product, result)


def combine(nc, K, X, result):
    with ExitStack() as st:
        m = Memory(nc, st, f"combine{X.layer}")
        slot_g = m.sb("slot_g", (ROWS, GROUP * 2), I32)
        got = m.sb("got", (ROWS, GROUP * 2, C))
        copied, added, stored = m.sem("copied"), m.sem("added"), m.sem("stored")
        gathered = m.sem("gathered", start=0)
        block = m.block()

        @block.gpsimd
        def _(pool):
            with pool.Fori(0, GROUPS) as g:
                pool.wait_ge(added, g + START)
                nc.gpsimd.tensor_copy(slot_g[:], K.slot[:, bass.ds(g * (GROUP * 2), GROUP * 2)]).then_inc(copied, 1)
                pool.wait_ge(copied, g + 1 + START)
                carry(pool, m)
                for n in range(GROUP * 2):
                    nc.gpsimd.indirect_dma_start(
                        out=got[:, n, :], out_offset=None, in_=K.slot_out[0:X.slot_tiles * 128, :],
                        in_offset=bass.IndirectOffsetOnAxis(ap=slot_g[:, n:n + 1], axis=0)).then_inc(gathered, 16)

        @block.vector
        def _(dve):
            with dve.Fori(0, GROUPS) as g:
                dve.wait_ge(gathered, (g + 1) * (GROUP * 2 * 16))
                for n in range(2):
                    for u in range(GROUP):
                        t = g * GROUP + u
                        last = nc.vector.scalar_tensor_tensor(K.X[:, t, :], got[:, 2 * u + n, :],
                                                              K.gate[:, t, n:n + 1], K.X[:, t, :],
                                                              ALU.mult, ALU.add)
                    if n == 0:
                        dve.drain()
                last.then_inc(added, 1)

        @block.sync
        def _(sp):
            if result is not None:
                view = result.rearrange("(t p) c -> p t c", p=ROWS)
                with sp.Fori(0, GROUPS) as g:
                    sp.wait_ge(added, g + 1 + START)
                    tiles = bass.ds(g * GROUP, GROUP)
                    for a, z in ((0, DMA_ROWS), (DMA_ROWS, ROWS)):
                        sp.dma_start(view[a:z, tiles, :], K.X[a:z, tiles, :]).then_inc(stored, 16)
                sp.wait_ge(stored, GROUPS * 32 + START)


def degree_scale(nc, K):
    with ExitStack() as st:
        m = Memory(nc, st, "degree")
        deg = m.sb("deg", (ROWS, TILES))
        ready, rooted = m.sem("ready"), m.sem("rooted")
        block = m.block()

        @block.vector
        def _(dve):
            nc.vector.tensor_scalar(deg[:], K.DEG[:], 1.0, None, ALU.add).then_inc(ready, 1)
            dve.wait_ge(rooted, 1 + START)
            nc.vector.reciprocal(K.DINV[:], K.DINV[:])

        @block.scalar
        def _(act):
            act.wait_ge(ready, 1 + START)
            nc.scalar.activation(K.DINV[:], deg[:], ACT.Sqrt).then_inc(rooted, 1)


def mix_tail_l1(nc, K, D):
    with ExitStack() as st:
        m = Memory(nc, st, "mix1")
        w = m.sb("w", (128, KC, C))
        bias = m.sb("bias", (ROWS, C))
        qt = m.sb("qt", (128, KC, GROWS))
        den = m.sb("den", (ROWS, GROUP, KC, HPB))
        att = m.sb("att", (ROWS, GROUP, C))
        att_t = m.sb("att_t", (128, KC, GROWS))
        ps_t = [m.ps(f"ps_t{i}") for i in range(3)]
        ps_a = [m.ps(f"ps_a{i}") for i in range(2)]
        ps_o = [m.ps(f"ps_o{i}") for i in range(2)]
        w_in, qt_ready, a_done, a_used, att_ready, t_done, att_t_ready, o_done, o_used = (
            m.sem(n) for n in ("w_in", "qt_ready", "a_done", "a_used", "att_ready", "t_done", "att_t_ready",
                               "o_done", "o_used"))
        block = m.block()

        @block.sync
        def _(sp):
            sp.dma_start(w[:], D["L1_mix_Wproj"].rearrange("(k p) o -> p k o", p=128)).then_inc(w_in, 16)
            sp.dma_start(bias[:], D["L1_mix_bproj"].partition_broadcast(ROWS)).then_inc(w_in, 16)
            sp.wait_ge(w_in, 32 + START)

        @block.gpsimd
        def _(pool):
            with pool.Fori(0, GROUPS) as g:
                pool.wait_ge(a_done, g * GROUP + START)
                nc.gpsimd.tensor_copy(qt[:], K.QT[:, :, bass.ds(g * GROWS, GROWS)]).then_inc(qt_ready, 1)

        @block.vector
        def _(dve):
            dve.wait_ge(w_in, 32 + START)
            with dve.Fori(0, GROUPS) as g:
                dve.wait_ge(t_done, g + START)
                for u in range(GROUP):
                    t = g * GROUP + u
                    dve.wait_ge(a_done, t + 1 + START)
                    a = ps_a[u % 2][0:ROWS, 0:KC * KVW].rearrange("p (k w) -> p k w", k=KC)
                    nc.vector.tensor_scalar(den[:, u], a[:, :, 128:KVW], 1e-6, None, ALU.max)
                    dve.drain()
                    nc.vector.reciprocal(den[:, u], den[:, u])
                    dve.drain()
                    for k in range(KC):
                        last = nc.vector.tensor_tensor(
                            att[:, u, k * 128:(k + 1) * 128].rearrange("p (a d) -> p a d", d=HD),
                            a[:, k, 0:128].rearrange("p (a d) -> p a d", d=HD),
                            den[:, u, k, :].unsqueeze(2).broadcast_to([ROWS, HPB, HD]), ALU.mult)
                    last.then_inc(a_used, 1)
                dve.drain()
                dve.nop().then_inc(att_ready, 1)
                tiles = bass.ds(g * GROUP, GROUP)
                nc.vector.tensor_tensor(K.X[:, tiles, :], K.X[:, tiles, :],
                                        bias[:].unsqueeze(1).broadcast_to([ROWS, GROUP, C]), ALU.add)
                dve.drain()
                for u in range(GROUP):
                    t = g * GROUP + u
                    dve.wait_ge(o_done, t + 1 + START)
                    nc.vector.tensor_tensor(K.X[:, t, :], ps_o[u % 2][0:ROWS, 0:C], K.X[:, t, :],
                                            ALU.add).then_inc(o_used, 1)

        @block.scalar
        def _(act):
            with act.Fori(0, GROUPS) as g:
                act.wait_ge(t_done, g + 1 + START)
                copy_transposed(nc, att_t, ps_t).then_inc(att_t_ready, 1)

        @block.tensor
        def _(pe):
            pe.wait_ge(w_in, 32 + START)
            with pe.Fori(0, GROUPS) as g:
                pe.wait_ge(qt_ready, g + 1 + START)
                for u in range(GROUP):
                    t = g * GROUP + u
                    pe.wait_ge(a_used, (t if u == 0 else t - 1) + START)
                    for k in range(KC):
                        last = nc.tensor.matmul(ps_a[u % 2][0:ROWS, k * KVW:(k + 1) * KVW],
                                                qt[:, k, u * ROWS:(u + 1) * ROWS], K.kv[:, k, :],
                                                start=True, stop=True)
                    last.then_inc(a_done, 1)
                pe.wait_ge(att_ready, g + 1 + START)
                pe.wait_ge(att_t_ready, g + START)
                transpose_group(nc, K, att, ps_t).then_inc(t_done, 1)
                pe.wait_ge(att_t_ready, g + 1 + START)
                for u in range(GROUP):
                    t = g * GROUP + u
                    pe.wait_ge(o_used, (t if u == 0 else t - 1) + START)
                    for k in range(KC):
                        last = nc.tensor.matmul(ps_o[u % 2][0:ROWS, 0:C], att_t[:, k, u * ROWS:(u + 1) * ROWS],
                                                w[:, k, :], start=(k == 0), stop=(k == KC - 1))
                    last.then_inc(o_done, 1)


def gcn(nc, K, D):
    with ExitStack() as st:
        m = Memory(nc, st, "gcn")
        adj = [m.sb(f"adj{i}", (ROWS, TILES * ROWS), BF16) for i in range(2)]
        bias = m.sb("bias", (ROWS, C))
        acc = m.sb("acc", (ROWS, C))
        ps_a = [m.ps(f"ps_a{i}") for i in range(2)]
        ps_b = [m.ps(f"ps_b{i}") for i in range(2)]
        arrived = [m.sem(f"in{i}") for i in range(2)]
        b_in, done, used = m.sem("b_in"), m.sem("done"), m.sem("used")
        block = m.block()

        @block.sync
        def _(sp):
            sp.dma_start(bias[:], D["L1_gnn_b1"].partition_broadcast(ROWS)).then_inc(b_in, 16)
            load_tiles(sp, adj, K.adj, arrived, done)

        @block.tensor
        def _(pe):
            pe.nop().then_inc(done, 1)

            def tile(t, b, i):
                pe.wait_ge(arrived[b], (i + 1) * 32 + START)
                pe.wait_ge(used, (t if b == 0 else t - 1) + START)
                for s in range(TILES):
                    w = adj[b][:, s * ROWS:(s + 1) * ROWS]
                    nc.tensor.matmul(ps_a[b][0:ROWS, :], w, K.Yp[:, s, 0:512], start=(s == 0), stop=(s == TILES - 1))
                    last = nc.tensor.matmul(ps_b[b][0:ROWS, 0:C], w, K.Yp[:, s, 512:768],
                                            start=(s == 0), stop=(s == TILES - 1))
                last.then_inc(done, 1)
            two_by_two(pe, TILES, tile)

        @block.vector
        def _(dve):
            dve.wait_ge(b_in, 16 + START)

            def tile(t, b, i):
                dve.wait_ge(done, t + 2 + START)
                nc.vector.tensor_tensor(acc[:], ps_a[b][0:ROWS, 0:C], K.Y[:, t, :], ALU.add)
                dve.drain()
                nc.vector.tensor_tensor(acc[:], acc[:], ps_a[b][0:ROWS, C:2 * C], ALU.add)
                dve.drain()
                nc.vector.tensor_tensor(acc[:], acc[:], ps_b[b][0:ROWS, 0:C], ALU.add).then_inc(used, 1)
                dve.drain()
                nc.vector.scalar_tensor_tensor(acc[:], acc[:], K.DINV[:, bass.ds(t, 1)], bias[:], ALU.mult, ALU.add)
                dve.drain()
                nc.vector.tensor_scalar(K.XN[:, t, :], acc[:], 0.0, None, ALU.max)
                dve.drain()
            two_by_two(dve, TILES, tile)


def gat_project(nc, K, D):
    with ExitStack() as st:
        m = Memory(nc, st, "gatp")
        w = m.sb("w", (128, KC, C))
        vec = m.sb("vec", (ROWS, 2, C))
        row = m.sb("row", (ROWS, GROUP, C))
        xt = m.sb("xt", (128, KC, GROWS))
        prod, dots = m.sb("prod", (ROWS, 2, C)), m.sb("dots", (ROWS, 2, GROUP))
        y = m.sb("y", (ROWS, GROUP, C))
        at_src = m.sb("at_src", (ROWS, TILES))
        line = m.sb("line", (TILES, ROWS))
        ps_t = [m.ps(f"ps_t{i}") for i in range(3)]
        ps_y = [m.ps(f"ps_y{i}") for i in range(2)]
        w_in, row_ready, t_done, xt_ready, y_done, y_used, src_ready, turned, line_ready, line_out, spread = (
            m.sem(n) for n in ("w_in", "row_ready", "t_done", "xt_ready", "y_done", "y_used", "src_ready",
                               "turned", "line_ready", "line_out", "spread"))
        block = m.block()

        @block.sync
        def _(sp):
            sp.dma_start(w[:], D["L1_gnn_W2"].rearrange("(k p) o -> p k o", p=128)).then_inc(w_in, 16)
            sp.dma_start(vec[:, 0, :], D["L1_gnn_att_src"].partition_broadcast(ROWS)).then_inc(w_in, 16)
            sp.dma_start(vec[:, 1, :], D["L1_gnn_att_dst"].partition_broadcast(ROWS)).then_inc(w_in, 16)
            sp.wait_ge(w_in, 48 + START)
            sp.wait_ge(line_ready, 1 + START)
            sp.dma_start(K.src_line, line[:]).then_inc(line_out, 16)
            sp.wait_ge(line_out, 16 + START)
            sp.dma_start(K.SRC[:], K.src_line.rearrange("t p -> (t p)").partition_broadcast(ROWS)).then_inc(spread, 16)
            sp.wait_ge(spread, 16 + START)

        @block.gpsimd
        def _(pool):
            with pool.Fori(0, GROUPS) as g:
                pool.wait_ge(t_done, g + START)
                nc.gpsimd.tensor_copy(row[:], K.XN[:, bass.ds(g * GROUP, GROUP), :]).then_inc(row_ready, 1)

        @block.scalar
        def _(act):
            with act.Fori(0, GROUPS) as g:
                act.wait_ge(t_done, g + 1 + START)
                copy_transposed(nc, xt, ps_t).then_inc(xt_ready, 1)

        @block.vector
        def _(dve):
            dve.wait_ge(w_in, 48 + START)
            with dve.Fori(0, GROUPS) as g:
                for u in range(GROUP):
                    t = g * GROUP + u
                    dve.wait_ge(y_done, t + 1 + START)
                    nc.vector.tensor_copy(y[:, u, :], ps_y[u % 2][0:ROWS, 0:C]).then_inc(y_used, 1)
                    dve.drain()
                    for n in range(2):
                        nc.vector.tensor_tensor_reduce(out=prod[:, n, :], in0=y[:, u, :], in1=vec[:, n, :], scale=1.0,
                                                       scalar=0.0, op0=ALU.mult, op1=ALU.add,
                                                       accum_out=dots[:, n, u:u + 1])
                    dve.drain()
                tiles = bass.ds(g * GROUP, GROUP)
                nc.vector.tensor_copy(K.Y[:, tiles, :], y[:])
                nc.vector.tensor_copy(at_src[:, tiles], dots[:, 0, :])
                nc.vector.tensor_copy(K.AT_DST[:, tiles], dots[:, 1, :])
                dve.drain()
            dve.nop().then_inc(src_ready, 1)
            dve.wait_ge(turned, 1 + START)
            nc.vector.tensor_copy(line[:], ps_t[0][0:TILES, 0:ROWS]).then_inc(line_ready, 1)

        @block.tensor
        def _(pe):
            pe.wait_ge(w_in, 48 + START)
            with pe.Fori(0, GROUPS) as g:
                pe.wait_ge(row_ready, g + 1 + START)
                pe.wait_ge(xt_ready, g + START)
                transpose_group(nc, K, row, ps_t).then_inc(t_done, 1)
                pe.wait_ge(xt_ready, g + 1 + START)
                for u in range(GROUP):
                    t = g * GROUP + u
                    pe.wait_ge(y_used, (t if u == 0 else t - 1) + START)
                    for k in range(KC):
                        last = nc.tensor.matmul(ps_y[u % 2][0:ROWS, 0:C], xt[:, k, u * ROWS:(u + 1) * ROWS],
                                                w[:, k, :], start=(k == 0), stop=(k == KC - 1))
                    last.then_inc(y_done, 1)
            pe.wait_ge(src_ready, 1 + START)
            nc.tensor.transpose(ps_t[0][0:TILES, 0:ROWS], at_src[:], K.ident_f[0:ROWS, 0:ROWS]).then_inc(turned, 1)


def gat(nc, K, D):
    quads = [(a, min(a + 4, TILES)) for a in range(0, TILES, 4)]
    NQ = len(quads)
    with ExitStack() as st:
        m = Memory(nc, st, "gat")
        cnt = [m.sb(f"cnt{i}", (ROWS, NODES), BF16) for i in range(2)]
        absent = m.sb("absent", (ROWS, NODES), BF16)
        score = [m.sb(f"score{i}", (ROWS, NODES)) for i in range(2)]
        prob = [m.sb(f"prob{i}", (ROWS, NODES)) for i in range(2)]
        prob_t = m.sb("prob_t", (ROWS, NODES))
        bias = m.sb("bias", (ROWS, C))
        small = m.sb("small", (ROWS, 2, 8))
        acc = m.sb("acc", (ROWS, C))
        ps_t = [m.ps(f"ps_t{i}") for i in range(4)]
        ps_o = [m.ps(f"ps_o{i}") for i in range(2)]
        arrived = [m.sem(f"in{i}") for i in range(2)]
        b_in, cnt_used, scored, first_exp, exped, weighed, t_done, t_read, o_done, o_used = (
            m.sem(n) for n in ("b_in", "cnt_used", "scored", "first_exp", "exped", "weighed", "t_done",
                               "t_read", "o_done", "o_used"))
        block = m.block()
        greatest, dst, top, low, shift1, shift5, total, inv = range(8)

        def cell(b, n):
            return small[:, b, n:n + 1]

        @block.sync
        def _(sp):
            sp.dma_start(bias[:], D["L1_gnn_b2"].partition_broadcast(ROWS)).then_inc(b_in, 16)
            load_tiles(sp, cnt, K.adj_t, arrived, cnt_used)

        @block.vector
        def _(dve):
            v = nc.vector

            def scores(t, b, i):
                dve.wait_ge(arrived[b], (i + 1) * 32 + START)
                own = cnt[b][:, bass.ds(t * ROWS, ROWS)]
                v.tensor_tensor(own, own, K.ident_b[0:ROWS, 0:ROWS], ALU.add)
                v.tensor_copy(cell(b, dst), K.AT_DST[:, bass.ds(t, 1)])
                dve.drain()
                v.tensor_scalar(absent[:], cnt[b][:], 0.0, -1e30, ALU.is_equal, ALU.mult)
                dve.drain()
                v.tensor_tensor_reduce(out=score[b][:], in0=absent[:], in1=K.SRC[:], scale=1.0, scalar=-3e38,
                                       op0=ALU.add, op1=ALU.max, accum_out=cell(b, greatest))
                dve.drain()
                v.tensor_tensor(cell(b, top), cell(b, greatest), cell(b, dst), ALU.add)
                dve.drain()
                v.scalar_tensor_tensor(cell(b, low), cell(b, top), 0.2, cell(b, top), ALU.mult, ALU.max)
                dve.drain()
                v.tensor_tensor(cell(b, shift1), cell(b, dst), cell(b, low), ALU.subtract)
                v.scalar_tensor_tensor(cell(b, shift5), cell(b, dst), 0.2, cell(b, low), ALU.mult,
                                       ALU.subtract).then_inc(scored, 1)

            def weigh(t, b):
                dve.wait_ge(exped, t + 1 + START)
                v.tensor_tensor(score[b][:], score[b][:], prob[b][:], ALU.max)
                dve.drain()
                v.tensor_tensor_reduce(out=prob[b][:], in0=score[b][:], in1=cnt[b][:], scale=1.0, scalar=0.0,
                                       op0=ALU.mult, op1=ALU.add, accum_out=cell(b, total)).then_inc(weighed, 1)
                dve.drain()
                v.tensor_scalar(cell(b, inv), cell(b, total), 1e-16, None, ALU.add).then_inc(cnt_used, 1)
                dve.drain()
                v.reciprocal(cell(b, inv), cell(b, inv))
                dve.drain()

            def finish(t, b):
                dve.wait_ge(o_done, t + 1 + START)
                v.scalar_tensor_tensor(acc[:], ps_o[b][0:ROWS, 0:C], cell(b, inv), bias[:], ALU.mult,
                                       ALU.add).then_inc(o_used, 1)
                dve.drain()
                v.scalar_tensor_tensor(K.X[:, t, :], acc[:], 0.0, K.X[:, t, :], ALU.max, ALU.add)
                dve.drain()

            dve.nop().then_inc(cnt_used, 1)
            dve.wait_ge(b_in, 16 + START)
            scores(0, 0, 0)
            scores(1, 1, 0)
            weigh(0, 0)
            scores(2, 0, 1)
            weigh(1, 1)
            with dve.Fori(1, TILES // 2) as i:
                scores(i * 2 + 1, 1, i)
                finish(i * 2 - 2, 0)
                weigh(i * 2, 0)
                scores(i * 2 + 2, 0, i + 1)
                finish(i * 2 - 1, 1)
                weigh(i * 2 + 1, 1)
            finish(TILES - 3, 0)
            weigh(TILES - 1, 0)
            finish(TILES - 2, 1)
            finish(TILES - 1, 0)

        @block.scalar
        def _(act):
            def exponentials(t, b):
                act.wait_ge(scored, t + 1 + START)
                if not isinstance(t, int) or t >= 2:
                    act.wait_ge(t_done, (t - 1) * NQ + START)
                nc.scalar.activation(prob[b][:], score[b][:], ACT.Exp, bias=cell(b, shift1)).then_inc(first_exp, 1)
                act.wait_ge(first_exp, t + 1 + START)
                nc.scalar.activation(score[b][:], score[b][:], ACT.Exp, bias=cell(b, shift5),
                                     scale=0.2).then_inc(exped, 1)

            def move(t):
                for n, (a, z) in enumerate(quads):
                    act.wait_ge(t_done, t * NQ + n + 1 + START)
                    nc.scalar.activation(prob_t[:, a * ROWS:z * ROWS], ps_t[n % 4][0:ROWS, 0:(z - a) * ROWS],
                                         ACT.Copy).then_inc(t_read, 1)

            exponentials(0, 0)
            exponentials(1, 1)
            move(0)
            exponentials(2, 0)
            move(1)
            with act.Fori(1, TILES // 2) as i:
                exponentials(i * 2 + 1, 1)
                move(i * 2)
                exponentials(i * 2 + 2, 0)
                move(i * 2 + 1)
            move(TILES - 1)

        @block.tensor
        def _(pe):
            def tile(t, b, i):
                pe.wait_ge(weighed, t + 1 + START)
                for n, (a, z) in enumerate(quads):
                    pe.wait_ge(t_read, t * NQ + max(n - 3, 0) + START)
                    for s in range(a, z):
                        last = nc.tensor.transpose(ps_t[n % 4][0:ROWS, (s - a) * ROWS:(s - a + 1) * ROWS],
                                                   prob[b][:, s * ROWS:(s + 1) * ROWS], K.ident_f[0:ROWS, 0:ROWS])
                    last.then_inc(t_done, 1)
                pe.wait_ge(o_used, (t if b == 0 else t - 1) + START)
                for n, (a, z) in enumerate(quads):
                    pe.wait_ge(t_read, t * NQ + n + 1 + START)
                    for s in range(a, z):
                        last = nc.tensor.matmul(ps_o[b][0:ROWS, 0:C], prob_t[:, s * ROWS:(s + 1) * ROWS],
                                                K.Y[:, s, :], start=(s == 0), stop=(s == TILES - 1))
                last.then_inc(o_done, 1)
            two_by_two(pe, TILES, tile)


class Kept:
    pass


def program(nc, D, result):
    X0, X1 = Experts(0), Experts(1)
    slots = 128 * max(X0.slot_tiles, X1.slot_tiles)
    K = Kept()
    K.adj = nc.dram_tensor("adjacency", (TILES, ROWS, TILES * ROWS), BF16).ap()
    K.adj_t = nc.dram_tensor("adjacency_t", (TILES, ROWS, NODES), BF16).ap()
    K.rows_dram = nc.dram_tensor("expert_rows", (TILES, ROWS, C), F32).ap()
    K.slot_row = nc.dram_tensor("slot_row", (slots, 1), I32).ap()
    K.slot_out = nc.dram_tensor("slot_out", (slots, C), F32).ap()
    K.src_line = nc.dram_tensor("src_line", (TILES, ROWS), F32).ap()
    with ExitStack() as all_:
        def sb(stack, name, shape, dt=F32):
            return stack.enter_context(nc.sbuf_tensor(name, list(shape), dt))

        K.X = sb(all_, "X", (ROWS, TILES, C))
        K.ident_f, K.ident_b = sb(all_, "ident_f", (128, 128)), sb(all_, "ident_b", (128, 128), BF16)
        K.number_row, K.number_f = sb(all_, "number_row", (128, 128), F16), sb(all_, "number_f", (128, 128))
        K.zeros, K.ones = sb(all_, "zeros", (1, 512)), sb(all_, "ones", (128, 128))
        K.DEG, K.DINV, K.AT_DST = (sb(all_, n, (ROWS, TILES)) for n in ("DEG", "DINV", "AT_DST"))
        K.slot, K.gate = sb(all_, "slot", (ROWS, TILES * 2), I32), sb(all_, "gate", (ROWS, TILES, 2))
        K.owner = sb(all_, "owner", (1, 128), I32)
        K.kv = sb(all_, "kv", (128, KC, KVW))
        constants(nc, K)

        build_adjacency(nc, K, D)
        with ExitStack() as layer:
            K.XN, K.X1 = sb(layer, "XN0", (ROWS, TILES, C)), sb(layer, "X1", (ROWS, TILES, C))
            K.QT = sb(layer, "QT0", (128, KC, NODES))
            K.Y, K.AGG = sb(layer, "Y0", (ROWS, TILES, 64)), sb(layer, "AGG", (ROWS, TILES, 64))
            K.Yp = sb(layer, "Yp0", (ROWS, TILES, 256), BF16)
            front(nc, K, "front0", D["x"], D["L0_gnn_W1_down"], 64, D["L0_mix_Wkv"], D["L0_mix_Wq"], None)
            mix_tail_l0(nc, K, D)
            gin_down(nc, K)
            gin_tail(nc, K, "gin_down", D, "down", K.XN, K.X1)
            gin_up(nc, K)
            gin_tail(nc, K, "gin_up", D, "up", K.X1, None)
        route(nc, K, D, X0)
        experts(nc, K, D, X0)
        combine(nc, K, X0, None)
        with ExitStack() as layer:
            K.XN, K.Y = sb(layer, "XN1", (ROWS, TILES, C)), sb(layer, "Y1", (ROWS, TILES, C))
            with ExitStack() as early:
                K.QT = sb(early, "QT1", (128, KC, NODES))
                K.Yp = sb(early, "Yp1", (ROWS, TILES, 3 * C), BF16)
                degree_scale(nc, K)
                front(nc, K, "front1", None, D["L1_gnn_W1"], C, D["L1_mix_Wkv"], D["L1_mix_Wq"], K.DINV)
                mix_tail_l1(nc, K, D)
                gcn(nc, K, D)
            K.SRC = sb(layer, "SRC", (ROWS, NODES))
            gat_project(nc, K, D)
            gat(nc, K, D)
        route(nc, K, D, X1)
        experts(nc, K, D, X1)
        combine(nc, K, X1, result)


def lay_out(inputs):
    import numpy as np

    a = {k: np.ascontiguousarray(v) for k, v in inputs.items()}
    wqkv = a.pop("L0_mix_Wqkv")
    a["L0_mix_Wq"] = np.ascontiguousarray(wqkv[:C].T)
    a["L0_mix_Wkv"] = np.ascontiguousarray(wqkv[C:].T)
    for name in ("L0_mix_W1", "L0_mix_W2", "L1_mix_Wq", "L1_mix_Wkv", "L1_mix_Wproj"):
        a[name] = np.ascontiguousarray(a[name].T)
    a["L0_mix_b1"] = np.ascontiguousarray(a["L0_mix_b1"].reshape(KC, 128).T)
    a["L0_ffn_b1"] = np.ascontiguousarray(a["L0_ffn_b1"].reshape(8, 4, 128).transpose(0, 2, 1))
    for name in ("L0_gnn_eps_down", "L0_gnn_eps_up"):
        a[name] = a[name].reshape(1)
    src, dst = a.pop("src"), a.pop("dst")
    for name, e in (("src", src), ("dst", dst)):
        cols = np.full(CHUNKS_PAD * CH, NODES, np.int32)
        cols[:EDGES] = e
        a[name + "_cols"] = np.ascontiguousarray(cols.reshape(CHUNKS_PAD, CH).T)
    rows = np.full(CHUNK_ROWS * CH, NODES, np.int32)
    rows[:EDGES] = dst
    a["dst_rows"] = rows.reshape(128, 4 * CH)
    return a


def kernel(**inputs):
    import concourse.bacc as bacc
    import numpy as np
    from concourse.bass_utils import run_bass_kernel_spmd

    nc = bacc.Bacc("TRN2", target_bir_lowering=False, num_devices=1)
    arrays = {"in_" + k: v for k, v in lay_out(inputs).items()}
    D = {k[3:]: nc.dram_tensor(k, v.shape, mybir.dt.from_np(v.dtype), kind="ExternalInput").ap()
         for k, v in arrays.items()}
    out = nc.dram_tensor("out", (NODES, C), F32, kind="ExternalOutput").ap()
    program(nc, D, out)
    got = run_bass_kernel_spmd(nc, [arrays], core_ids=[0])
    return got.results[0]["out"]
```

```python
from contextlib import ExitStack

import concourse.bass as bass
from concourse import mybir

F32 = mybir.dt.float32
BF16 = mybir.dt.bfloat16
F16 = mybir.dt.float16
I32 = mybir.dt.int32
ALU = mybir.AluOpType
ACT = mybir.ActivationFunctionType
AX = mybir.AxisListType

NODES = 3125
EDGES = 53125
C = 256
KC = C // 128
ROWS = 125
TILES = NODES // ROWS
GROUP = 5
GROUPS = TILES // GROUP
GROWS = GROUP * ROWS
HEADS = 8
HD = C // HEADS
HPB = 128 // HD
KVW = 128 + HPB
WIN = 25
WINS = NODES // WIN
WPT = ROWS // WIN
CH = 128
CHUNKS = -(-EDGES // CH)
CHUNKS_PAD = CHUNKS + 4
FIXED = 4
MORE_MAX = CHUNKS
CHUNK_ROWS = 512
DMA_ROWS = 112
START = 1
LN_EPS = 1e-5
PAIRS = ((0, 2), (2, 4), (4, 5))
SPLIT = ((0, 500), (500, 625))


def rows_dma(eng, out, in_, sem):
    eng.dma_start(out[0:DMA_ROWS], in_[0:DMA_ROWS]).then_inc(sem, 16)
    eng.dma_start(out[DMA_ROWS:ROWS], in_[DMA_ROWS:ROWS]).then_inc(sem, 16)


class Memory:

    def __init__(self, nc, stack, stage):
        self.nc, self.stack, self.stage = nc, stack, stage
        self.sems, self.starts = [], []
        stack.callback(self.clear)
        self.tick = self.sem("tick")

    def sb(self, name, shape, dt=F32):
        return self.stack.enter_context(self.nc.sbuf_tensor(f"{self.stage}_{name}", list(shape), dt))

    def ps(self, name, shape=(128, 512), dt=F32):
        return self.stack.enter_context(self.nc.psum_tensor(f"{self.stage}_{name}", list(shape), dt))

    def sem(self, name, start=START):
        self.sems.append(self.nc.alloc_semaphore(f"{self.stage}_{name}"))
        self.starts.append(start)
        return self.sems[-1]

    def block(self):
        for sem, start in zip(self.sems, self.starts):
            if start:
                self.nc.gpsimd.sem_inc(sem, start)
        self.nc.all_engine_barrier()
        return self.stack.enter_context(self.nc.Block())

    def clear(self):
        self.nc.clear_and_free_semaphores(self.sems)


def carry(eng, m):
    eng.nop().then_inc(m.tick, 1)


def layer_norm_stats(dve, nc, src, stats, mv, var_eps, n):
    for u in range(n):
        nc.vector.bn_stats(stats[:, u, :], src(u))
    dve.drain()
    for u in range(n):
        nc.vector.bn_aggr(mv[:, u, :], stats[:, u, :])
    dve.drain()
    return nc.vector.tensor_scalar(var_eps[:], mv[:, :, 1], LN_EPS, None, ALU.add)


def layer_norm_affine(dve, nc, src, out, mv, std, rstd, std_ready, value, gain, shift):
    for u in range(GROUP):
        nc.vector.scalar_tensor_tensor(out(u), src(u), mv[:, u, 0:1], gain, ALU.subtract, ALU.mult)
    dve.wait_ge(std_ready, value)
    nc.vector.reciprocal(rstd[:], std[:])
    dve.drain()
    for u in range(GROUP):
        last = nc.vector.scalar_tensor_tensor(out(u), out(u), rstd[:, u:u + 1], shift, ALU.mult, ALU.add)
    return last


def split3(dve, nc, whole, rest, parts):
    nc.vector.tensor_copy(parts[0], whole)
    dve.drain()
    nc.vector.tensor_tensor(rest, whole, parts[0], ALU.subtract)
    dve.drain()
    nc.vector.tensor_copy(parts[1], rest)
    dve.drain()
    return nc.vector.tensor_tensor(parts[2], rest, parts[1], ALU.subtract)


def transpose_group(nc, K, rows, banks):
    for k in range(KC):
        for u in range(GROUP):
            out = banks[k][:, u * ROWS:(u + 1) * ROWS] if u < 4 else banks[2][:, k * ROWS:(k + 1) * ROWS]
            last = nc.tensor.transpose(out, rows[:, u, k * 128:(k + 1) * 128], K.ident_f[0:ROWS, 0:ROWS])
    return last


def copy_transposed(nc, dst, banks, fn=ACT.Copy, bias=None):
    for k in range(KC):
        more = {} if bias is None else {"bias": bias[:, k:k + 1]}
        nc.scalar.activation(dst[:, k, 0:4 * ROWS], banks[k][:, 0:4 * ROWS], fn, **more)
        last = nc.scalar.activation(dst[:, k, 4 * ROWS:GROWS], banks[2][:, k * ROWS:(k + 1) * ROWS], fn, **more)
    return last


def matmul_group(nc, banks, block, weight, xt):
    for lo, hi in SPLIT:
        out = banks[block][:, 0:4 * ROWS] if lo == 0 else banks[2][:, block * ROWS:(block + 1) * ROWS]
        for k in range(KC):
            last = nc.tensor.matmul(out, weight(k), xt[:, k, lo:hi], start=(k == 0), stop=(k == KC - 1))
    return last


def zero_bank(nc, K, bank, width, start):
    return nc.tensor.matmul(bank[:, 0:width], K.zeros[0:1, 0:128], K.zeros[0:1, 0:width],
                            start=start, stop=not start)


def two_by_two(eng, count, body):
    with eng.Fori(0, count // 2) as i:
        body(i * 2, 0, i)
        body(i * 2 + 1, 1, i)
    body(count - 1, 0, count // 2)


def overlapped(eng, count, early, late):
    for step in early:
        step(0, 0)
    with eng.Fori(0, count // 2) as i:
        late(i * 2, 0, lambda k: early[k](i * 2 + 1, 1))
        late(i * 2 + 1, 1, lambda k: early[k](i * 2 + 2, 0))
    late(count - 1, 0, lambda k: None)


def after_first(eng, body):
    with eng.Fori(0, GROUPS // 2) as i:
        body(i * 2 + 1, 1)
        body(i * 2 + 2, 0)


def constants(nc, K):
    with ExitStack() as st:
        m = Memory(nc, st, "const")
        zeroed = m.sem("zeroed")
        block = m.block()

        @block.gpsimd
        def _(pool):
            nc.gpsimd.memset(K.zeros[:], 0.0)
            nc.gpsimd.memset(K.ones[:], 1.0)
            nc.gpsimd.memset(K.ident_f[:], 0.0)
            nc.gpsimd.memset(K.ident_b[:], 0.0).then_inc(zeroed, 1)
            pool.wait_ge(zeroed, 1 + START)
            for ident in (K.ident_f, K.ident_b):
                nc.gpsimd.affine_select(out=ident[:], in_=ident[:], compare_op=ALU.not_equal, fill=1.0,
                                        base=0, pattern=[[-1, 128]], channel_multiplier=1)
            nc.gpsimd.iota(K.number_f[:], [[1, 128]], base=0, channel_multiplier=0,
                           allow_small_or_imprecise_dtypes=True)
            nc.gpsimd.iota(K.number_row[:], [[1, 128]], base=0, channel_multiplier=0,
                           allow_small_or_imprecise_dtypes=True)


def front(nc, K, stage, w_y, y_width, w_kv, w_q, y_scale):
    with ExitStack() as st:
        m = Memory(nc, st, stage)
        wy = m.sb("wy", (128, KC, y_width))
        wkv = m.sb("wkv", (128, KC, 2 * C))
        wq = m.sb("wq", (128, KC, C))
        stats, mv = m.sb("stats", (ROWS, GROUP, 6)), m.sb("mv", (ROWS, GROUP, 2))
        var_eps, std, rstd = (m.sb(n, (ROWS, GROUP)) for n in ("var_eps", "std", "rstd"))
        xn = m.sb("xn", (ROWS, GROUP, C))
        xt = [m.sb(f"xt{i}", (128, KC, GROWS)) for i in range(2)]
        e_kv, r_kv = m.sb("e_kv", (ROWS, 2, C)), m.sb("r_kv", (ROWS, 2, C))
        key, val = m.sb("key", (ROWS, 2, C)), m.sb("val", (ROWS, 2, KC, 129))
        e_q, r_q = m.sb("e_q", (128, KC, GROWS)), m.sb("r_q", (128, KC, GROWS))
        y_rest = m.sb("y_rest", (ROWS, GROUP, y_width))
        ps_t = [m.ps(f"ps_t{i}") for i in range(3)]
        ps_y = [m.ps(f"ps_y{i}") for i in range(2)]
        ps_kv = [m.ps(f"ps_kv{i}") for i in range(2)]
        acc = m.ps("acc")
        ps_acc = [acc[:, h * 129:(h + 1) * 129] for h in range(KC)]
        w_in, var_ready, std_ready, xn_ready, xn_saved = (
            m.sem(n) for n in ("w_in", "var_ready", "std_ready", "xn_ready", "xn_saved"))
        t_done, xt_ready, y_done, y_used, kv_done, kv_read, kv_exp, key_ready, key_used = (
            m.sem(n) for n in ("t_done", "xt_ready", "y_done", "y_used", "kv_done", "kv_read", "kv_exp",
                               "key_ready", "key_used"))
        q_done, q_read, q_used, sum_done = m.sem("q_done"), m.sem("q_read"), m.sem("q_used"), m.sem("sum_done")
        block = m.block()

        @block.sync
        def _(sp):
            sp.dma_start(wkv[:], w_kv.rearrange("(k p) o -> p k o", p=128)).then_inc(w_in, 16)
            sp.dma_start(wq[:], w_q.rearrange("(k p) o -> p k o", p=128)).then_inc(w_in, 16)
            sp.dma_start(wy[:], w_y.rearrange("(k p) o -> p k o", p=128)).then_inc(w_in, 16)
            sp.wait_ge(w_in, 48 + START)

        @block.vector
        def _(dve):
            nc.vector.memset(val[:], 1.0)
            nc.vector.memset(K.kv[:], 0.0)
            if y_width == 64:
                nc.vector.memset(K.Yp[:, :, 192:193], 1.0)

            def statistics(g, b):
                layer_norm_stats(dve, nc, lambda u: K.X[:, g * GROUP + u, :], stats, mv, var_eps,
                                 GROUP).then_inc(var_ready, 1)

            def normalise(g, b):
                dve.wait_ge(std_ready, g + 1 + START)
                nc.vector.reciprocal(rstd[:], std[:])
                dve.drain()
                dve.wait_ge(t_done, g + START)
                dve.wait_ge(xn_saved, g + START)
                for u in range(GROUP):
                    last = nc.vector.tensor_scalar(xn[:, u, :], K.X[:, g * GROUP + u, :], mv[:, u, 0:1],
                                                   rstd[:, u:u + 1], ALU.subtract, ALU.mult)
                last.then_inc(xn_ready, 1)

            def group(g, b, then):
                for u in range(GROUP):
                    t = g * GROUP + u
                    dve.wait_ge(y_done, t + 1 + START)
                    y = ps_y[u % 2][0:ROWS, 0:y_width]
                    if y_scale is None:
                        nc.vector.tensor_scalar(K.Y[:, t, 0:y_width], y, 0.0, None, ALU.add).then_inc(y_used, 1)
                    else:
                        nc.vector.tensor_scalar(K.Y[:, t, 0:y_width], y, y_scale[:, bass.ds(t, 1)], None,
                                                ALU.mult).then_inc(y_used, 1)
                    dve.wait_ge(kv_exp, t + 1 + START)
                    nc.vector.scalar_tensor_tensor(key[:, u % 2, :], e_kv[:, u % 2, :], 1.0, r_kv[:, u % 2, :],
                                                   ALU.min, ALU.add).then_inc(key_ready, 1)
                    if u < 2:
                        then(u)
                dve.drain()
                tiles = bass.ds(g * GROUP, GROUP)
                split3(dve, nc, K.Y[:, tiles, 0:y_width], y_rest[:],
                       [K.Yp[:, tiles, i * y_width:(i + 1) * y_width] for i in range(3)])
                dve.wait_ge(q_read, g + 2 + START)
                for h in range(KC):
                    last = nc.vector.scalar_tensor_tensor(K.QT[:, h, bass.ds(g * GROWS, GROWS)],
                                                          e_q[:, h, :], 1.0, r_q[:, h, :], ALU.min, ALU.add)
                last.then_inc(q_used, 1)

            overlapped(dve, GROUPS, (statistics, normalise), group)
            dve.wait_ge(sum_done, 1 + START)
            for h in range(KC):
                for a in range(HPB):
                    p = slice(HD * a, HD * a + HD)
                    nc.vector.tensor_copy(K.kv[p, h, HD * a:HD * a + HD], ps_acc[h][p, HD * a:HD * a + HD])
                    nc.vector.tensor_copy(K.kv[p, h, 128 + a:129 + a], ps_acc[h][p, 128:129])

        @block.gpsimd
        def _(pool):
            with pool.Fori(0, GROUPS) as g:
                pool.wait_ge(xn_ready, g + 1 + START)
                nc.gpsimd.tensor_copy(K.XN[:, bass.ds(g * GROUP, GROUP), :], xn[:]).then_inc(xn_saved, 1)

        @block.scalar
        def _(act):
            def root(g, b):
                act.wait_ge(var_ready, g + 1 + START)
                nc.scalar.activation(std[:], var_eps[:], ACT.Sqrt).then_inc(std_ready, 1)

            def transposed(g, b):
                act.wait_ge(t_done, g + 1 + START)
                copy_transposed(nc, xt[b], ps_t).then_inc(xt_ready, 1)

            def group(g, b, then):
                for u in range(GROUP):
                    t = g * GROUP + u
                    act.wait_ge(kv_done, t + 1 + START)
                    act.wait_ge(key_ready, (t if u == 0 else t - 1) + START)
                    act.wait_ge(key_used, (t if u == 0 else t - 1) + START)
                    nc.scalar.activation(e_kv[:, u % 2, :], ps_kv[u % 2][0:ROWS, 0:C], ACT.Exp)
                    nc.scalar.activation(r_kv[:, u % 2, :], ps_kv[u % 2][0:ROWS, 0:C], ACT.Relu)
                    nc.scalar.activation(val[:, u % 2, :, 0:128],
                                         ps_kv[u % 2][0:ROWS, C:2 * C].rearrange("p (k f) -> p k f", k=KC),
                                         ACT.Copy).then_inc(kv_exp, 1)
                    if u == 1:
                        then(0)
                    if u == 3:
                        then(1)
                act.wait_ge(q_done, g + 1 + START)
                act.wait_ge(q_used, g + START)
                for dst, fn in ((e_q, ACT.Exp), (r_q, ACT.Relu)):
                    last = copy_transposed(nc, dst, ps_t, fn)
                last.then_inc(q_read, 1)

            overlapped(act, GROUPS, (root, transposed), group)

        @block.tensor
        def _(pe):
            def key_value_sum(g, u):
                pe.wait_ge(key_ready, g * GROUP + u + 1 + START)
                for h in range(KC):
                    last = nc.tensor.matmul(ps_acc[h], key[:, u % 2, h * 128:(h + 1) * 128],
                                            val[:, u % 2, h, :], start=False, stop=False)
                last.then_inc(key_used, 1)

            zero_bank(nc, K, acc, KC * 129, start=True)
            pe.wait_ge(w_in, 48 + START)
            pe.nop().then_inc(q_read, 1)

            def transposes(g, b):
                pe.wait_ge(xn_ready, g + 1 + START)
                pe.wait_ge(q_read, g + START)
                transpose_group(nc, K, xn, ps_t).then_inc(t_done, 1)

            def transposed(g, b):
                pe.wait_ge(xt_ready, g + 1 + START)

            def group(g, b, then):
                for u in range(GROUP):
                    t = g * GROUP + u
                    cols = slice(u * ROWS, (u + 1) * ROWS)
                    pe.wait_ge(y_used, (t if u == 0 else t - 1) + START)
                    for k in range(KC):
                        last = nc.tensor.matmul(ps_y[u % 2][0:ROWS, 0:y_width], xt[b][:, k, cols], wy[:, k, :],
                                                start=(k == 0), stop=(k == KC - 1))
                    last.then_inc(y_done, 1)
                    pe.wait_ge(kv_exp, (t if u == 0 else t - 1) + START)
                    for k in range(KC):
                        last = nc.tensor.matmul(ps_kv[u % 2][0:ROWS, :], xt[b][:, k, cols], wkv[:, k, :],
                                                start=(k == 0), stop=(k == KC - 1))
                    last.then_inc(kv_done, 1)
                    if u:
                        key_value_sum(g, u - 1)
                    if u == 3:
                        then(0)
                then(1)
                for h in range(KC):
                    last = matmul_group(nc, ps_t, h, lambda k: wq[:, k, h * 128:(h + 1) * 128], xt[b])
                last.then_inc(q_done, 1)
                key_value_sum(g, GROUP - 1)

            overlapped(pe, GROUPS, (transposes, transposed), group)
            last = zero_bank(nc, K, acc, KC * 129, start=False)
            last.then_inc(sum_done, 1)


def mix_tail_l0(nc, K, D):
    with ExitStack() as st:
        m = Memory(nc, st, "mix0")
        w1, w2 = m.sb("w1", (128, KC, C)), m.sb("w2", (128, KC, C))
        b1 = m.sb("b1", (128, KC))
        vec = m.sb("vec", (ROWS, 5, C))
        stats, mv = m.sb("stats", (ROWS, GROUP, 6)), m.sb("mv", (ROWS, GROUP, 2))
        var_eps, std, rstd = (m.sb(n, (ROWS, GROUP)) for n in ("var_eps", "std", "rstd"))
        qt = [m.sb(f"qt{i}", (128, KC, GROWS)) for i in range(2)]
        den = m.sb("den", (ROWS, GROUP, KC, HPB))
        att = m.sb("att", (ROWS, GROUP, C))
        x1 = [m.sb(f"x1_{i}", (ROWS, GROUP, C)) for i in range(2)]
        x1t, ht = m.sb("x1t", (128, KC, GROWS)), m.sb("ht", (128, KC, GROWS))
        ps_t = [m.ps(f"ps_t{i}") for i in range(3)]
        ps_a = [m.ps(f"ps_a{i}") for i in range(2)]
        ps_o = [m.ps(f"ps_o{i}") for i in range(2)]
        w_in, qt_ready, a_done, a_used = (m.sem(n) for n in ("w_in", "qt_ready", "a_done", "a_used"))
        var_ready, std_ready = ([m.sem(n + str(i)) for i in range(2)] for n in ("var_ready", "std_ready"))
        x1_ready, t_done, x1t_ready, h_done, ht_ready, o_done, o_used = (
            m.sem(n) for n in ("x1_ready", "t_done", "x1t_ready", "h_done", "ht_ready", "o_done", "o_used"))
        block = m.block()

        @block.sync
        def _(sp):
            sp.dma_start(w1[:], D["L0_mix_W1"].rearrange("(k p) o -> p k o", p=128)).then_inc(w_in, 16)
            sp.dma_start(w2[:], D["L0_mix_W2"].rearrange("(k p) o -> p k o", p=128)).then_inc(w_in, 16)
            sp.dma_start(b1[:], D["L0_mix_b1"]).then_inc(w_in, 16)
            for n, name in enumerate(("ln1_g", "ln1_b", "ln2_g", "ln2_b", "b2")):
                sp.dma_start(vec[:, n, :], D["L0_mix_" + name].partition_broadcast(ROWS)).then_inc(w_in, 16)
            sp.wait_ge(w_in, 8 * 16 + START)

        @block.gpsimd
        def _(pool):
            def copy(g, b):
                pool.wait_ge(a_done, (g - 1) * GROUP + START)
                nc.gpsimd.tensor_copy(qt[b][:], K.QT[:, :, bass.ds(g * GROWS, GROWS)]).then_inc(qt_ready, 1)
            after_first(pool, copy)

        @block.vector
        def _(dve):
            def bc(n):
                return vec[:, n, :].unsqueeze(1).broadcast_to([ROWS, GROUP, C])

            def normalise(g, src, out, n):
                layer_norm_stats(dve, nc, lambda u: src[:, u, :], stats, mv, var_eps,
                                 GROUP).then_inc(var_ready[n], 1)
                return layer_norm_affine(dve, nc, lambda u: src[:, u, :], lambda u: out[:, u, :], mv, std, rstd,
                                         std_ready[n], g + 1 + START, vec[:, 2 * n, :], vec[:, 2 * n + 1, :])

            def attention(g, b):
                for u in range(GROUP):
                    t = g * GROUP + u
                    dve.wait_ge(a_done, t + 1 + START)
                    a = ps_a[u % 2][0:ROWS, 0:KC * KVW].rearrange("p (k w) -> p k w", k=KC)
                    nc.vector.tensor_scalar(den[:, u], a[:, :, 128:KVW], 1e-6, None, ALU.add)
                    dve.drain()
                    nc.vector.reciprocal(den[:, u], den[:, u])
                    dve.drain()
                    for k in range(KC):
                        last = nc.vector.tensor_tensor(
                            att[:, u, k * 128:(k + 1) * 128].rearrange("p (a d) -> p a d", d=HD),
                            a[:, k, 0:128].rearrange("p (a d) -> p a d", d=HD),
                            den[:, u, k, :].unsqueeze(2).broadcast_to([ROWS, HPB, HD]), ALU.mult)
                    last.then_inc(a_used, 1)
                dve.drain()
                nc.vector.tensor_tensor(att[:], att[:], K.XN[:, bass.ds(g * GROUP, GROUP), :], ALU.add)
                dve.drain()
                normalise(g, att, x1[b], 0).then_inc(x1_ready, 1)

            def mlp(g, b, then):
                then(0)
                for u in range(GROUP):
                    dve.wait_ge(o_done, g * GROUP + u + 1 + START)
                    nc.vector.tensor_tensor(att[:, u, :], ps_o[u % 2][0:ROWS, 0:C], x1[b][:, u, :],
                                            ALU.add).then_inc(o_used, 1)
                dve.drain()
                nc.vector.tensor_tensor(att[:], att[:], bc(4), ALU.add)
                dve.drain()
                normalise(g, att, x1[b], 1)
                dve.drain()
                nc.vector.tensor_tensor(K.X[:, bass.ds(g * GROUP, GROUP), :],
                                        K.X[:, bass.ds(g * GROUP, GROUP), :], x1[b][:], ALU.add)

            dve.wait_ge(w_in, 8 * 16 + START)
            overlapped(dve, GROUPS, (attention,), mlp)

        @block.scalar
        def _(act):
            def root(g, n):
                act.wait_ge(var_ready[n], g + 1 + START)
                nc.scalar.activation(std[:], var_eps[:], ACT.Sqrt).then_inc(std_ready[n], 1)

            def mlp(g, b, then):
                act.wait_ge(t_done, g + 1 + START)
                copy_transposed(nc, x1t, ps_t).then_inc(x1t_ready, 1)
                then(0)
                act.wait_ge(h_done, g + 1 + START)
                copy_transposed(nc, ht, ps_t, ACT.Gelu, b1).then_inc(ht_ready, 1)
                root(g, 1)

            act.wait_ge(w_in, 8 * 16 + START)
            overlapped(act, GROUPS, (lambda g, b: root(g, 0),), mlp)

        @block.tensor
        def _(pe):
            def attention(g, b, lo, hi):
                q = qt[b]
                if isinstance(g, int):
                    q = K.QT
                else:
                    pe.wait_ge(qt_ready, g + START)
                for u in range(lo, hi):
                    t = g * GROUP + u
                    pe.wait_ge(a_used, (t if u == 0 else t - 1) + START)
                    for k in range(KC):
                        last = nc.tensor.matmul(ps_a[u % 2][0:ROWS, k * KVW:(k + 1) * KVW],
                                                q[:, k, u * ROWS:(u + 1) * ROWS], K.kv[:, k, :],
                                                start=True, stop=True)
                    last.then_inc(a_done, 1)

            def mlp(g, b, then):
                then(0)
                pe.wait_ge(x1_ready, g + 1 + START)
                pe.wait_ge(ht_ready, g + START)
                transpose_group(nc, K, x1[b], ps_t).then_inc(t_done, 1)
                then(1)
                pe.wait_ge(x1t_ready, g + 1 + START)
                for h in range(KC):
                    last = matmul_group(nc, ps_t, h, lambda k: w1[:, k, h * 128:(h + 1) * 128], x1t)
                last.then_inc(h_done, 1)
                pe.wait_ge(ht_ready, g + 1 + START)
                for u in range(GROUP):
                    t = g * GROUP + u
                    pe.wait_ge(o_used, (t if u == 0 else t - 1) + START)
                    for k in range(KC):
                        last = nc.tensor.matmul(ps_o[u % 2][0:ROWS, 0:C], ht[:, k, u * ROWS:(u + 1) * ROWS],
                                                w2[:, k, :], start=(k == 0), stop=(k == KC - 1))
                    last.then_inc(o_done, 1)

            pe.wait_ge(w_in, 8 * 16 + START)
            overlapped(pe, GROUPS, (lambda g, b: attention(g, b, 0, 2), lambda g, b: attention(g, b, 2, GROUP)), mlp)


def build_adjacency(nc, K, D):
    with ExitStack() as st:
        m = Memory(nc, st, "adj")
        src_i, dst_i = m.sb("src_i", (CH, CHUNKS_PAD), I32), m.sb("dst_i", (CH, CHUNKS_PAD), I32)
        dst_rows_i = m.sb("dst_rows_i", (128, CHUNK_ROWS), I32)
        src_f, dst_f = m.sb("src_f", (CH, CHUNKS_PAD)), m.sb("dst_f", (CH, CHUNKS_PAD))
        dst_rows = m.sb("dst_rows", (128, 4, CH))
        hi = m.sb("hi", (CH, CHUNKS_PAD))
        low_all = m.sb("low", (CH, CHUNKS + FIXED + MORE_MAX))
        key_all = m.sb("key", (CH, CHUNKS + FIXED + MORE_MAX))
        low = low_all[:, 0:CHUNKS_PAD]
        key = key_all[:, 0:CHUNKS_PAD]
        hi_i = m.sb("hi_i", (CH, CHUNKS_PAD), I32)
        off = m.sb("off", (CH, CHUNKS_PAD))
        least, most = m.sb("least", (128, 4)), m.sb("most", (128, 4))
        win_first = m.sb("win_first", (128, WINS))
        most_chunks = m.sb("most_chunks", (1, 1))
        chunk_no = m.sb("chunk_no", (128, 4))
        rank_up, rank_down = m.sb("rank_up", (128, 4)), m.sb("rank_down", (128, 4))
        here, here2 = m.sb("here", (128, 4, WINS)), m.sb("here2", (128, 4, WINS))
        span = m.sb("span", (128, 2, 4, WINS))
        span_all = m.sb("span_all", (128, 2, 4, WINS))
        ends = m.sb("ends", (1, 2, WINS))
        row = m.sb("row", (1, 2, WINS))
        table = m.sb("table", (1, WINS + 1), I32)
        key_row = m.sb("key_row", (CH, TILES * WIN), F16)
        win_key = m.sb("win_key", (CH, WINS))
        one_s = [m.sb(f"one_s{i}", (CH, FIXED, ROWS), BF16) for i in range(2)]
        one_k = [m.sb(f"one_k{i}", (CH, FIXED, TILES * WIN), BF16) for i in range(2)]
        more_s = [m.sb(f"more_s{i}", (CH, ROWS), BF16) for i in range(2)]
        more_k = [m.sb(f"more_k{i}", (CH, TILES * WIN), BF16) for i in range(2)]
        key_here = [m.sb(f"key_here{i}", (CH, FIXED)) for i in range(2)]
        adj = [m.sb(f"tile{i}", (ROWS, TILES, ROWS), BF16) for i in range(2)]
        adj_t = [m.sb(f"tile_t{i}", (ROWS, NODES), BF16) for i in range(2)]
        ps_w = [[m.ps(f"ps_w{i}{j}") for j in range(2)] for i in range(2)]
        ps_t = [m.ps(f"ps_t{i}", (128, 1024), BF16) for i in range(4)]
        x_in, e_in, made, span_ready, spread, table_ready = (
            m.sem(n) for n in ("x_in", "e_in", "made", "span_ready", "spread", "table_ready"))
        more_ready, more_used = ([m.sem(n + str(i)) for i in range(2)] for n in ("more_ready", "more_used"))
        keyed, one_ready, win_done, win_read, t_done, t_read, stored, tile_used = (
            m.sem(n) for n in ("keyed", "one_ready", "win_done", "win_read", "t_done", "t_read",
                               "stored", "tile_used"))
        block = m.block()

        @block.sync
        def _(sp):
            sp.dma_start(src_i[:], D["src_cols"]).then_inc(e_in, 16)
            sp.dma_start(dst_i[:], D["dst_cols"]).then_inc(e_in, 16)
            sp.dma_start(dst_rows_i[:], D["dst_rows"]).then_inc(e_in, 16)
            rows_dma(sp, K.X, D["x"].rearrange("(t p) c -> p t c", p=ROWS), x_in)

            def store(t, b, i):
                sp.wait_ge(win_read, t * WPT + WPT + START)
                rows_dma(sp, K.adj[bass.ds(t, 1)].rearrange("t p n -> (t p) n"),
                         adj[b][:].rearrange("p t d -> p (t d)"), stored)
                sp.wait_ge(t_read, t + 1 + START)
                rows_dma(sp, K.adj_t[bass.ds(t, 1)].rearrange("t p n -> (t p) n"), adj_t[b][:], stored)
                sp.wait_ge(stored, t * 64 + 64 + START)
                sp.nop().then_inc(tile_used, 1)

            sp.nop().then_inc(tile_used, 2)
            two_by_two(sp, TILES, store)
            sp.wait_ge(x_in, 32 + START)

        @block.gpsimd
        def _(pool):
            nc.gpsimd.iota(key_row[:], [[1, TILES], [TILES, WIN]], base=0, channel_multiplier=0,
                           allow_small_or_imprecise_dtypes=True)
            nc.gpsimd.iota(win_first[:], [[WIN, WINS]], base=0, channel_multiplier=0,
                           allow_small_or_imprecise_dtypes=True)
            nc.gpsimd.iota(win_key[:], [[WIN * TILES, WINS]], base=0, channel_multiplier=0,
                           allow_small_or_imprecise_dtypes=True)
            nc.gpsimd.iota(chunk_no[:], [[1, 4]], base=0, channel_multiplier=4,
                           allow_small_or_imprecise_dtypes=True).then_inc(made, 1)
            pool.wait_ge(span_ready, 1 + START)
            nc.gpsimd.partition_all_reduce(span_all[:].rearrange("p a q w -> p (a q w)"),
                                           span[:].rearrange("p a q w -> p (a q w)"), 128,
                                           bass.bass_isa.ReduceOp.max).then_inc(spread, 1)

        @block.vector
        def _(dve):
            v = nc.vector
            dve.wait_ge(e_in, 48 + START)
            v.tensor_copy(src_f[:], src_i[:])
            v.tensor_copy(dst_f[:], dst_i[:])
            v.tensor_copy(dst_rows[:].rearrange("p q e -> p (q e)"), dst_rows_i[:])
            dve.drain()
            v.tensor_scalar(off[:], src_f[:], 0.5, 1.0 / ROWS, ALU.add, ALU.mult)
            dve.drain()
            v.tensor_copy(hi_i[:], off[:])
            dve.drain()
            v.tensor_copy(hi[:], hi_i[:])
            dve.drain()
            v.scalar_tensor_tensor(off[:], hi[:], float(ROWS), src_f[:], ALU.mult, ALU.is_gt)
            dve.drain()
            v.tensor_tensor(hi[:], hi[:], off[:], ALU.subtract)
            dve.drain()
            v.memset(low_all[:, CHUNKS_PAD:], -1.0)
            v.memset(key_all[:, CHUNKS_PAD:], -1.0)
            v.scalar_tensor_tensor(low, hi[:], -float(ROWS), src_f[:], ALU.mult, ALU.add)
            v.scalar_tensor_tensor(key, dst_f[:], float(TILES), hi[:], ALU.mult, ALU.add)
            v.tensor_reduce(least[:], dst_rows[:], AX.X, ALU.min)
            v.tensor_reduce(most[:], dst_rows[:], AX.X, ALU.max)
            dve.wait_ge(made, 1 + START)
            v.tensor_scalar(rank_up[:], chunk_no[:], 1.0, None, ALU.add)
            v.tensor_scalar(rank_down[:], chunk_no[:], -1.0, float(CHUNK_ROWS), ALU.mult, ALU.add)
            dve.drain()
            for q in range(4):
                v.tensor_scalar(here[:, q, :], win_first[:], float(WIN - 1), least[:, q:q + 1], ALU.add, ALU.is_ge)
                v.tensor_scalar(here2[:, q, :], win_first[:], most[:, q:q + 1], None, ALU.is_le)
            dve.drain()
            v.tensor_tensor(here[:], here[:], here2[:], ALU.mult)
            dve.drain()
            for q in range(4):
                v.tensor_scalar(span[:, 0, q, :], here[:, q, :], rank_up[:, q:q + 1], None, ALU.mult)
                last = v.tensor_scalar(span[:, 1, q, :], here[:, q, :], rank_down[:, q:q + 1], None, ALU.mult)
            last.then_inc(span_ready, 1)
            dve.wait_ge(spread, 1 + START)
            v.tensor_reduce(ends[:], span_all[0:1].rearrange("p a q w -> p a w q"), AX.X, ALU.max)
            dve.drain()
            v.tensor_scalar(row[:, 0, :], ends[:, 1, :], -1.0, float(CHUNK_ROWS), ALU.mult, ALU.add)
            dve.drain()
            v.tensor_scalar(row[:, 0, :], row[:, 0, :], float(CHUNKS), None, ALU.min)
            dve.drain()
            v.tensor_tensor(row[:, 1, :], ends[:, 0, :], row[:, 0, :], ALU.subtract)
            dve.drain()
            v.tensor_copy(table[:, 0:WINS], row[:, 0, :])
            v.tensor_reduce(most_chunks[:], row[:, 1, :], AX.X, ALU.max)
            dve.drain()
            v.tensor_scalar(most_chunks[:], most_chunks[:], -float(FIXED), 1.0, ALU.add, ALU.max)
            dve.drain()
            v.tensor_copy(table[:, WINS:WINS + 1], most_chunks[:]).then_inc(table_ready, 1)
            dve.wait_ge(table_ready, 1 + START)
            more = dve.value_load(table[:, WINS:WINS + 1], min_val=1, max_val=MORE_MAX)

            def tile(t, b, i):
                for w in range(WPT):
                    win, half = t * WPT + w, (b * WPT + w) % 2
                    first = dve.value_load(table[:, bass.ds(win, 1)], min_val=0, max_val=CHUNKS)
                    with dve.Fori(0, more) as n:
                        dve.wait_ge(more_used[half], (i * WPT + (b * WPT + w) // 2) * more + n + 1 + START)
                        v.tensor_scalar(more_s[half][:], K.number_row[:, 0:ROWS],
                                        low_all[:, bass.ds(first + n + FIXED, 1)], None, ALU.is_equal)
                        v.tensor_scalar(more_k[half][:], key_row[:], win_key[:, bass.ds(win, 1)],
                                        key_all[:, bass.ds(first + n + FIXED, 1)], ALU.add,
                                        ALU.is_equal).then_inc(more_ready[half], 1)
                    dve.wait_ge(win_done, win + 1 + START)
                    v.tensor_scalar(key_here[half][:], key_all[:, bass.ds(first, FIXED)],
                                    win_key[:, bass.ds(win, 1)], None, ALU.subtract).then_inc(keyed, 1)
                    v.tensor_tensor(one_s[half][:], K.number_row[:, None, 0:ROWS].to_broadcast((CH, FIXED, ROWS)),
                                    low_all[:, bass.ds(first, FIXED)][:, :, None].to_broadcast((CH, FIXED, ROWS)),
                                    ALU.is_equal)
                    dve.wait_ge(keyed, win + 1 + START)
                    for j in range(FIXED):
                        v.tensor_scalar(one_k[half][:, j, :], key_row[:], key_here[half][:, j:j + 1], None,
                                        ALU.is_equal).then_inc(one_ready, 1)

            two_by_two(dve, TILES, tile)

        @block.scalar
        def _(act):
            def tile(t, b, i):
                for w in range(WPT):
                    win = t * WPT + w
                    act.wait_ge(win_done, win + 3 + START)
                    if w == 0:
                        act.wait_ge(tile_used, t + 1 + START)
                    for bank, (a, z) in enumerate(((0, 20), (20, 25))):
                        last = nc.scalar.activation(
                            adj[b][:, a:z, w * WIN:(w + 1) * WIN],
                            ps_w[w % 2][bank][0:ROWS, 0:(z - a) * WIN].rearrange("p (s d) -> p s d", d=WIN),
                            ACT.Copy)
                    last.then_inc(win_read, 1)
                act.wait_ge(t_done, t + 1 + START)
                for n in range(4):
                    z = min((n + 1) * 8, TILES) - n * 8
                    last = nc.scalar.activation(
                        adj_t[b][:, n * 8 * ROWS:(n * 8 + z) * ROWS].rearrange("p (u s) -> p u s", s=ROWS),
                        ps_t[n][0:ROWS, 0:z * 128].rearrange("p (u s) -> p u s", s=128)[:, :, 0:ROWS], ACT.Copy)
                last.then_inc(t_read, 1)

            two_by_two(act, TILES, tile)

        @block.tensor
        def _(pe):
            pe.nop().then_inc(win_done, 2)
            pe.nop().then_inc(more_used[0], 1)
            pe.nop().then_inc(more_used[1], 1)
            pe.wait_ge(table_ready, 1 + START)
            more = pe.value_load(table[:, WINS:WINS + 1], min_val=1, max_val=MORE_MAX)

            def add(banks, ones, keys, start, stop):
                for bank, (a, z) in enumerate(SPLIT):
                    last = nc.tensor.matmul(banks[bank][0:ROWS, 0:z - a], ones, keys[:, a:z],
                                            start=start, stop=stop)
                return last

            def tile(t, b, i):
                for w in range(WPT):
                    win, half = t * WPT + w, (b * WPT + w) % 2

                    def fixed(j, start, stop):
                        pe.wait_ge(one_ready, win * FIXED + j + 1 + START)
                        return add(ps_w[w % 2], one_s[half][:, j, :], one_k[half][:, j, :], start, stop)

                    pe.wait_ge(win_read, (win if w == 0 else win - 1) + START)
                    fixed(0, True, False)
                    with pe.Fori(0, more) as n:
                        pe.wait_ge(more_ready[half], (i * WPT + (b * WPT + w) // 2) * more + n + 1 + START)
                        add(ps_w[w % 2], more_s[half][:], more_k[half][:], False, False).then_inc(more_used[half], 1)
                    for j in range(1, FIXED - 1):
                        fixed(j, False, False)
                    fixed(FIXED - 1, False, True).then_inc(win_done, 1)
                pe.wait_ge(win_read, t * WPT + WPT + START)
                pe.wait_ge(t_read, t + START)
                for s in range(TILES):
                    last = nc.tensor.transpose(ps_t[s // 8][0:ROWS, (s % 8) * 128:(s % 8) * 128 + ROWS],
                                               adj[b][:, s, :], K.ident_b[0:ROWS, 0:ROWS])
                last.then_inc(t_done, 1)

            two_by_two(pe, TILES, tile)


def load_tiles(sp, buffers, source, arrived, used):
    def load(t, c):
        rows_dma(sp, buffers[c], source[bass.ds(t, 1)].rearrange("t p n -> (t p) n"), arrived[c])

    for t in range(4):
        load(t, t)
    with sp.Fori(1, TILES // 4) as j:
        for c in range(4):
            sp.wait_ge(used, j * 4 + (c - 3) + START)
            load(j * 4 + c, c)
    sp.wait_ge(used, TILES - 4 + START)
    load(TILES - 1, (TILES - 1) % 4)
    for c in range(4):
        sp.wait_ge(arrived[c], (TILES + 3 - c) // 4 * 32 + START)


def four_by_four(eng, body):
    with eng.Fori(0, TILES // 4) as j:
        for c in range(4):
            body(j * 4 + c, c, j)
    body(TILES - 1, 0, TILES // 4)


def gin_down(nc, K):
    with ExitStack() as st:
        m = Memory(nc, st, "down")
        adj = [m.sb(f"adj{i}", (ROWS, TILES * ROWS), BF16) for i in range(4)]
        ps = [m.ps(f"ps{i}") for i in range(2)]
        arrived = [m.sem(f"in{i}") for i in range(4)]
        adj_used, done, used = m.sem("adj_used"), m.sem("done"), m.sem("used")
        block = m.block()

        @block.sync
        def _(sp):
            load_tiles(sp, adj, K.adj, arrived, done)

        @block.tensor
        def _(pe):
            def tile(t, c, j):
                b = c % 2
                pe.wait_ge(arrived[c], (j + 1) * 32 + START)
                pe.wait_ge(used, (t if c == 0 else t - 1) + START)
                for s in range(TILES):
                    last = nc.tensor.matmul(ps[b][0:ROWS, 0:193], adj[c][:, s * ROWS:(s + 1) * ROWS],
                                            K.Yp[:, s, 0:193], start=(s == 0), stop=(s == TILES - 1))
                last.then_inc(done, 1)
            four_by_four(pe, tile)

        @block.vector
        def _(dve):
            def tile(t, b, i):
                dve.wait_ge(done, t + 1 + START)
                nc.vector.tensor_reduce(K.AGG[:, t, :], ps[b][0:ROWS, 0:192].rearrange("p (i f) -> p f i", i=3),
                                        AX.X, ALU.add)
                nc.vector.tensor_copy(K.DEG[:, bass.ds(t, 1)], ps[b][0:ROWS, 192:193]).then_inc(used, 1)
            two_by_two(dve, TILES, tile)


def gin_up(nc, K):
    cuts = [(a, min(a + 500, NODES)) for a in range(0, NODES, 500)]
    with ExitStack() as st:
        m = Memory(nc, st, "up")
        adj_t = [m.sb(f"adj_t{i}", (ROWS, NODES), BF16) for i in range(4)]
        agg_t = m.sb("agg_t", (128, NODES))
        ps = [m.ps(f"ps{i}") for i in range(7)]
        arrived = [m.sem(f"in{i}") for i in range(4)]
        used, summed, moved, turned = m.sem("used"), m.sem("summed"), m.sem("moved"), m.sem("turned")
        block = m.block()

        @block.sync
        def _(sp):
            load_tiles(sp, adj_t, K.adj_t, arrived, used)

        @block.tensor
        def _(pe):
            for i, (a, z) in enumerate(cuts):
                zero_bank(nc, K, ps[i], z - a, start=True)

            def tile(t, b, i):
                pe.wait_ge(arrived[b], (i + 1) * 32 + START)
                for half in range(2):
                    for n, (a, z) in enumerate(cuts):
                        last = nc.tensor.matmul(ps[n][:, 0:z - a], K.Yp[:, t, half * 128:half * 128 + 128],
                                                adj_t[b][:, a:z], start=False, stop=False)
                last.then_inc(used, 1)
            four_by_four(pe, tile)
            for i, (a, z) in enumerate(cuts):
                last = zero_bank(nc, K, ps[i], z - a, start=False)
            last.then_inc(summed, 1)
            pe.wait_ge(moved, len(cuts) + START)
            for t in range(TILES):
                last = nc.tensor.transpose(ps[t // 4][0:ROWS, (t % 4) * 128:(t % 4) * 128 + 128],
                                           agg_t[:, t * ROWS:(t + 1) * ROWS], K.ident_f[:])
            last.then_inc(turned, 1)

        @block.scalar
        def _(act):
            act.wait_ge(summed, 1 + START)
            for i, (a, z) in enumerate(cuts):
                nc.scalar.activation(agg_t[:, a:z], ps[i][:, 0:z - a], ACT.Copy).then_inc(moved, 1)

        @block.vector
        def _(dve):
            dve.wait_ge(turned, 1 + START)
            for i in range(7):
                n = min(4, TILES - 4 * i)
                nc.vector.tensor_reduce(K.AGG[:, 4 * i:4 * i + n, :],
                                        ps[i][0:ROWS, 0:n * 128].rearrange("p (t i f) -> p t f i", i=2, f=64),
                                        AX.X, ALU.add)


def gin_tail(nc, K, stage, D, way, base, out):
    first = way == "down"
    with ExitStack() as st:
        m = Memory(nc, st, stage)
        w2 = m.sb("w2", (64, C))
        wy = m.sb("wy", (128, KC, 64))
        eps1 = m.sb("eps1", (ROWS, 1))
        narrow = m.sb("narrow", (ROWS, 2, 64))
        wide = m.sb("wide", (ROWS, 2, C))
        direction = m.sb("direction", (ROWS, C))
        base_d = [m.sb(f"base_d{i}", (ROWS, GROUP, C)) for i in range(2)]
        stats, mv = m.sb("stats", (ROWS, GROUP, 6)), m.sb("mv", (ROWS, GROUP, 2))
        var_eps, std, rstd = (m.sb(n, (ROWS, GROUP)) for n in ("var_eps", "std", "rstd"))
        hid = m.sb("hid", (ROWS, GROUP, 64))
        hid_t = m.sb("hid_t", (64, GROWS))
        row = m.sb("row", (ROWS, GROUP, C))
        xt = m.sb("xt", (128, KC, GROWS))
        rest = m.sb("rest", (ROWS, GROUP, 64))
        ps_t = [m.ps(f"ps_t{i}") for i in range(3)]
        ps_h = [m.ps(f"ps_h{i}") for i in range(2)]
        ps_o = [m.ps(f"ps_o{i}") for i in range(2)]
        ps_y = m.ps("ps_y")
        w_in, hid_ready, h_done, hid_moved, o_done, o_used = (
            m.sem(n) for n in ("w_in", "hid_ready", "h_done", "hid_moved", "o_done", "o_used"))
        var_ready, std_ready = ([m.sem(n + str(i)) for i in range(2)] for n in ("var_ready", "std_ready"))
        row_ready, t_done, xt_ready, y_done, y_used = (
            m.sem(n) for n in ("row_ready", "t_done", "xt_ready", "y_done", "y_used"))
        base_ready, row_saved = m.sem("base_ready"), m.sem("row_saved")
        block = m.block()
        loads = 8 if first else 7

        @block.gpsimd
        def _(pool):
            pool.wait_ge(w_in, loads * 16 + START)

            def tile(g, b, i):
                tiles = bass.ds(g * GROUP, GROUP)
                pool.wait_ge(o_used, (g if b == 0 else g - 1) * 3 + START)
                nc.gpsimd.tensor_tensor(base_d[b][:], base[:, tiles, :],
                                        direction[:].unsqueeze(1).broadcast_to([ROWS, GROUP, C]),
                                        ALU.add).then_inc(base_ready, 1)
                if first:
                    pool.wait_ge(row_ready, g + 1 + START)
                    nc.gpsimd.tensor_copy(out[:, tiles, :], row[:]).then_inc(row_saved, 1)

            two_by_two(pool, GROUPS, tile)

        @block.sync
        def _(sp):
            g = "L0_gnn_"
            sp.dma_start(w2[:], D[g + "W2_" + way]).then_inc(w_in, 16)
            sp.dma_start(eps1[:], D[g + "eps_" + way].partition_broadcast(ROWS)).then_inc(w_in, 16)
            sp.dma_start(narrow[:, 0, :], D[g + "lng_" + way].partition_broadcast(ROWS)).then_inc(w_in, 16)
            sp.dma_start(narrow[:, 1, :], D[g + "lnb_" + way].partition_broadcast(ROWS)).then_inc(w_in, 16)
            n = "1" if first else "2"
            sp.dma_start(wide[:, 0, :], D[g + f"ln{n}_g"].partition_broadcast(ROWS)).then_inc(w_in, 16)
            sp.dma_start(wide[:, 1, :], D[g + f"ln{n}_b"].partition_broadcast(ROWS)).then_inc(w_in, 16)
            sp.dma_start(direction[:], D[g + "dir_emb"][0 if first else 1].partition_broadcast(ROWS)).then_inc(w_in, 16)
            if first:
                sp.dma_start(wy[:], D[g + "W1_up"].rearrange("(k p) o -> p k o", p=128)).then_inc(w_in, 16)
            sp.wait_ge(w_in, loads * 16 + START)

        @block.vector
        def _(dve):
            v = nc.vector

            def normalise(buf, scale, shift, n, g):
                layer_norm_stats(dve, nc, lambda u: buf[:, u, :], stats, mv, var_eps, GROUP).then_inc(var_ready[n], 1)
                return layer_norm_affine(dve, nc, lambda u: buf[:, u, :], lambda u: buf[:, u, :], mv, std, rstd,
                                         std_ready[n], g + 1 + START, scale, shift)

            dve.wait_ge(w_in, loads * 16 + START)
            v.tensor_scalar(eps1[:], eps1[:], 1.0, None, ALU.add)
            if first:
                v.memset(K.Yp[:, :, 192:256], 0.0)
            dve.drain()

            def hidden(g, b):
                tiles = bass.ds(g * GROUP, GROUP)
                dve.wait_ge(h_done, g + START)
                v.scalar_tensor_tensor(hid[:], K.Y[:, tiles, 0:64], eps1[:], K.AGG[:, tiles, :], ALU.mult, ALU.add)
                dve.drain()
                normalise(hid, narrow[:, 0, :], narrow[:, 1, :], 0, g)
                dve.drain()
                v.tensor_scalar(hid[:], hid[:], 0.0, None, ALU.max).then_inc(hid_ready, 1)

            def group(g, b, then):
                tiles = bass.ds(g * GROUP, GROUP)
                if first:
                    dve.wait_ge(t_done, g + START)
                    dve.wait_ge(row_saved, g + START)
                else:
                    then(0)
                    dve.drain()
                dve.wait_ge(base_ready, g + 1 + START)
                for k, (lo, hi) in enumerate(PAIRS):
                    dve.wait_ge(o_done, g * 3 + k + 1 + START)
                    v.tensor_tensor(row[:, lo:hi, :],
                                    ps_o[k % 2][0:ROWS, 0:(hi - lo) * C].rearrange("p (u c) -> p u c", c=C),
                                    base_d[b][:, lo:hi, :], ALU.add).then_inc(o_used, 1)
                dve.drain()
                v.tensor_scalar(row[:], row[:], 0.0, None, ALU.max)
                dve.drain()
                last = normalise(row, wide[:, 0, :], wide[:, 1, :], 1, g)
                if first:
                    last.then_inc(row_ready, 1)
                    dve.drain()
                    then(0)
                    dve.wait_ge(y_done, g + 1 + START)
                    v.tensor_scalar(K.Y[:, tiles, 0:64], ps_y[0:ROWS, 0:GROUP * 64].rearrange("p (u f) -> p u f", f=64),
                                    0.0, None, ALU.add).then_inc(y_used, 1)
                    dve.drain()
                    split3(dve, nc, K.Y[:, tiles, 0:64], rest[:],
                           [K.Yp[:, tiles, i * 64:(i + 1) * 64] for i in range(3)])
                else:
                    dve.drain()
                    v.tensor_tensor(K.X[:, tiles, :], K.X[:, tiles, :], row[:], ALU.add)

            overlapped(dve, GROUPS, (hidden,), group)

        @block.scalar
        def _(act):
            def hidden(g, b):
                act.wait_ge(var_ready[0], g + 1 + START)
                nc.scalar.activation(std[:], var_eps[:], ACT.Sqrt).then_inc(std_ready[0], 1)
                act.wait_ge(h_done, g + 1 + START)
                nc.scalar.activation(hid_t[:, 0:500], ps_h[0][0:64, 0:500], ACT.Copy)
                nc.scalar.activation(hid_t[:, 500:625], ps_h[1][0:64, 0:125], ACT.Copy).then_inc(hid_moved, 1)

            def group(g, b, then):
                if not first:
                    then(0)
                act.wait_ge(var_ready[1], g + 1 + START)
                nc.scalar.activation(std[:], var_eps[:], ACT.Sqrt).then_inc(std_ready[1], 1)
                if first:
                    act.wait_ge(t_done, g + 1 + START)
                    copy_transposed(nc, xt, ps_t).then_inc(xt_ready, 1)
                    then(0)

            overlapped(act, GROUPS, (hidden,), group)

        @block.tensor
        def _(pe):
            def hidden(g, b):
                pe.wait_ge(hid_ready, g + 1 + START)
                pe.wait_ge(hid_moved, g + START)
                carry(pe, m)
                for u in range(GROUP):
                    out_h = ps_h[0][0:64, u * ROWS:(u + 1) * ROWS] if u < 4 else ps_h[1][0:64, 0:ROWS]
                    last = nc.tensor.transpose(out_h, hid[:, u, :], K.ident_f[0:ROWS, 0:ROWS])
                last.then_inc(h_done, 1)

            def group(g, b, then):
                pe.wait_ge(hid_moved, g + 1 + START)
                for k, (lo, hi) in enumerate(PAIRS):
                    pe.wait_ge(o_used, (g * 3 + 1 if k == 2 else g * 3) + START)
                    for u in range(lo, hi):
                        last = nc.tensor.matmul(ps_o[k % 2][0:ROWS, (u - lo) * C:(u - lo + 1) * C],
                                                hid_t[:, u * ROWS:(u + 1) * ROWS], w2[:], start=True, stop=True)
                    last.then_inc(o_done, 1)
                if not first:
                    then(0)
                else:
                    pe.wait_ge(row_ready, g + 1 + START)
                    pe.wait_ge(xt_ready, g + START)
                    transpose_group(nc, K, row, ps_t).then_inc(t_done, 1)
                    pe.wait_ge(xt_ready, g + 1 + START)
                    pe.wait_ge(y_used, g + START)
                    for u in range(GROUP):
                        for k in range(KC):
                            last = nc.tensor.matmul(ps_y[0:ROWS, u * 64:(u + 1) * 64], xt[:, k, u * ROWS:(u + 1) * ROWS],
                                                    wy[:, k, :], start=(k == 0), stop=(k == KC - 1))
                    last.then_inc(y_done, 1)
                    then(0)

            pe.wait_ge(w_in, loads * 16 + START)
            overlapped(pe, GROUPS, (hidden,), group)


class Experts:

    def __init__(self, layer):
        self.layer = layer
        self.n = 8 if layer == 0 else 16
        self.slot_tiles = 2 * NODES // 128 + self.n
        self.slot_tiles += 1 - self.slot_tiles % 2
        self.hidden = 512


def route(nc, K, D, X):
    E, L0 = X.n, X.layer == 0
    names = ("L0_ffn_Wr", "L0_ffn_br") if L0 else ("L1_ffn_gate_w", "L1_ffn_gate_b")
    with ExitStack() as st:
        m = Memory(nc, st, f"route{X.layer}")
        wr = m.sb("wr", (128, KC, E))
        bias = m.sb("bias", (ROWS, E))
        wide = m.sb("wide", (ROWS, 2, C))
        stats, mv = m.sb("stats", (ROWS, GROUP, 6)), m.sb("mv", (ROWS, GROUP, 2))
        var_eps, std, rstd = (m.sb(n, (ROWS, GROUP)) for n in ("var_eps", "std", "rstd"))
        row = [m.sb(f"row{i}", (ROWS, GROUP, C)) for i in range(2)]
        xt = m.sb("xt", (128, KC, GROWS))
        logit = m.sb("logit", (ROWS, GROUP, E))
        top, top_at = m.sb("top", (ROWS, GROUP, 8)), m.sb("top_at", (ROWS, GROUP, 8), mybir.dt.uint32)
        at_f = m.sb("at_f", (ROWS, GROUP, 8))
        gap, grown, denom = (m.sb(n, (ROWS, GROUP)) for n in ("gap", "grown", "denom"))
        pick = m.sb("pick", (ROWS, TILES, 2, E))
        both = m.sb("both", (ROWS, TILES, E))
        below = m.sb("below", (ROWS, ROWS))
        keep = m.sb("keep", (ROWS, E, TILES))
        total = m.sb("total", (ROWS, E, TILES))
        run = m.sb("run", (ROWS, E, TILES))
        base = m.sb("base", (ROWS, 4, E))
        base_i = m.sb("base_i", (ROWS, E), I32)
        place = m.sb("place", (ROWS, TILES, E))
        picked = m.sb("picked", (ROWS, TILES, 2, E))
        slot_f = m.sb("slot_f", (ROWS, TILES, 2))
        tile_no = m.sb("tile_no", (ROWS, X.slot_tiles))
        passed = m.sb("passed", (1, X.slot_tiles, E))
        owner = m.sb("owner", (1, X.slot_tiles))
        fresh = m.sb("fresh", (1, X.slot_tiles))
        part_i = m.sb("part_i", (ROWS, 2, TILES * 2), I32)
        part = m.sb("part", (ROWS, 2, TILES * 2))
        node = m.sb("node", (ROWS, TILES))
        low_hot = m.sb("low_hot", (ROWS, GROUP * 2, 128))
        high_hot = m.sb("high_hot", (ROWS, GROUP * 2, X.slot_tiles))
        ps_t = [m.ps(f"ps_t{i}") for i in range(3)]
        ps_l, ps_p, ps_s, ps_r = m.ps("ps_l"), m.ps("ps_p"), m.ps("ps_s"), m.ps("ps_r")
        w_in, var_ready, std_ready, row_ready, saved, t_done, xt_ready, l_done, l_used, gap_ready, grown_ready = (
            m.sem(n) for n in ("w_in", "var_ready", "std_ready", "row_ready", "saved", "t_done", "xt_ready",
                               "l_done", "l_used", "gap_ready", "grown_ready"))
        picks_ready, counted, made, filled, hot_ready, hot_used, rows_found = (
            m.sem(n) for n in ("picks_ready", "counted", "made", "filled", "hot_ready", "hot_used", "rows_found"))
        block = m.block()
        loads = 4 if L0 else 2
        norms = 2 if L0 else 1

        @block.sync
        def _(sp):
            sp.dma_start(wr[:], D[names[0]].rearrange("(k p) o -> p k o", p=128)).then_inc(w_in, 16)
            sp.dma_start(bias[:], D[names[1]].partition_broadcast(ROWS)).then_inc(w_in, 16)
            if L0:
                sp.dma_start(wide[:, 0, :], D["L0_ffn_gamma"].partition_broadcast(ROWS)).then_inc(w_in, 16)
                sp.dma_start(wide[:, 1, :], D["L0_ffn_beta"].partition_broadcast(ROWS)).then_inc(w_in, 16)

            def save(g, b, i):
                sp.wait_ge(row_ready, g + 1 + START)
                rows_dma(sp, K.rows_dram[bass.ds(g * GROUP, GROUP)].rearrange("t p c -> p t c"), row[b], saved)
                sp.wait_ge(saved, g * 32 + 32 + START)
                carry(sp, m)
            two_by_two(sp, GROUPS, save)
            sp.wait_ge(saved, GROUPS * 32 + START)
            sp.wait_ge(w_in, loads * 16 + START)

        @block.gpsimd
        def _(pool):
            nc.gpsimd.memset(below[:], 1.0).then_inc(filled, 1)
            pool.wait_ge(filled, 1 + START)
            nc.gpsimd.affine_select(out=below[:], in_=below[:], compare_op=ALU.is_gt, fill=0.0,
                                    base=0, pattern=[[1, ROWS]], channel_multiplier=-1)
            nc.gpsimd.iota(tile_no[:], [[128, X.slot_tiles]], base=0, channel_multiplier=0,
                           allow_small_or_imprecise_dtypes=True)
            nc.gpsimd.iota(node[:], [[ROWS, TILES]], base=0, channel_multiplier=1,
                           allow_small_or_imprecise_dtypes=True).then_inc(made, 1)

        @block.vector
        def _(dve):
            v = nc.vector

            def normalise(src, out, g):
                layer_norm_stats(dve, nc, src, stats, mv, var_eps, GROUP).then_inc(var_ready, 1)
                dve.wait_ge(std_ready, g * norms + 1 + START)
                v.reciprocal(rstd[:], std[:])
                dve.drain()
                for u in range(GROUP):
                    last = v.tensor_scalar(out[:, u, :], src(u), mv[:, u, 0:1], rstd[:, u:u + 1],
                                           ALU.subtract, ALU.mult)
                return last

            dve.wait_ge(w_in, loads * 16 + START)
            dve.wait_ge(made, 1 + START)

            def prepare(g, b):
                r = row[b]
                if not isinstance(g, int):
                    dve.wait_ge(t_done, (g - 1) + START)
                    dve.wait_ge(saved, (g - 1) * 32 + START)
                last = normalise(lambda u: K.X[:, g * GROUP + u, :], r, g)
                if L0:
                    dve.drain()
                    layer_norm_stats(dve, nc, lambda u: r[:, u, :], stats, mv, var_eps, GROUP).then_inc(var_ready, 1)
                    last = layer_norm_affine(dve, nc, lambda u: r[:, u, :], lambda u: r[:, u, :], mv, std, rstd,
                                             std_ready, g * norms + 2 + START, wide[:, 0, :], wide[:, 1, :])
                last.then_inc(row_ready, 1)

            def choose(g, b, then):
                tiles = bass.ds(g * GROUP, GROUP)
                then(0)
                dve.wait_ge(l_done, g + 1 + START)
                v.tensor_tensor(logit[:], ps_l[0:ROWS, 0:GROUP * E].rearrange("p (u e) -> p u e", e=E),
                                bias[:].unsqueeze(1).broadcast_to([ROWS, GROUP, E]), ALU.add).then_inc(l_used, 1)
                dve.drain()
                for u in range(GROUP):
                    v.max(top[:, u, :], logit[:, u, :])
                dve.drain()
                for u in range(GROUP):
                    v.max_index(top_at[:, u, :], top[:, u, :], logit[:, u, :])
                v.tensor_tensor(gap[:], top[:, :, 1], top[:, :, 0], ALU.subtract).then_inc(gap_ready, 1)
                dve.drain()
                v.tensor_copy(at_f[:], top_at[:])
                dve.drain()
                for n in range(2):
                    v.tensor_tensor(pick[:, tiles, n, :],
                                    K.number_f[0:ROWS, 0:E].unsqueeze(1).broadcast_to([ROWS, GROUP, E]),
                                    at_f[:, :, n:n + 1].broadcast_to([ROWS, GROUP, E]), ALU.is_equal)
                dve.wait_ge(grown_ready, g + 1 + START)
                v.tensor_scalar(denom[:], grown[:], 1.0, None, ALU.add)
                dve.drain()
                v.reciprocal(denom[:], denom[:])
                dve.drain()
                v.tensor_copy(K.gate[:, tiles, 0], denom[:])
                v.tensor_tensor(K.gate[:, tiles, 1], grown[:], denom[:], ALU.mult)
                dve.drain()

            overlapped(dve, GROUPS, (prepare,), choose)
            v.tensor_tensor(both[:], pick[:, :, 0, :], pick[:, :, 1, :], ALU.add).then_inc(picks_ready, 1)
            v.memset(keep[:], 1.0)
            dve.drain()
            v.memset(keep[:, :, 0:1], 0.0)
            dve.wait_ge(counted, 1 + START)
            v.tensor_copy(total[:], ps_s[0:ROWS, 0:TILES * E].rearrange("p (t e) -> p e t", e=E))
            dve.drain()
            v.tensor_tensor_scan(run[:].rearrange("p e t -> p (e t)"), keep[:].rearrange("p e t -> p (e t)"),
                                 total[:].rearrange("p e t -> p (e t)"), 0.0, ALU.mult, ALU.add)
            dve.drain()
            v.tensor_scalar(base[:, 0, :], run[:, :, TILES - 1], 127.0, None, ALU.add)
            v.tensor_tensor(total[:], run[:], total[:], ALU.subtract)
            dve.drain()
            v.tensor_copy(base_i[:], base[:, 0, :])
            dve.drain()
            v.tensor_scalar(base_i[:], base_i[:], 7, 7, ALU.arith_shift_right, ALU.logical_shift_left)
            dve.drain()
            v.tensor_copy(base[:, 0, :], base_i[:])
            v.memset(base[:, 1, :], 1.0)
            dve.drain()
            v.tensor_tensor_scan(base[:, 2, :], base[:, 1, :], base[:, 0, :], 0.0, ALU.mult, ALU.add)
            dve.drain()
            v.tensor_tensor(base[:, 3, :], base[:, 2, :], base[:, 0, :], ALU.subtract)
            v.tensor_tensor(place[:], ps_p[0:ROWS, 0:TILES * E].rearrange("p (t e) -> p t e", e=E),
                            total[:].rearrange("p e t -> p t e"), ALU.add)
            v.tensor_tensor(passed[:], tile_no[0:1].unsqueeze(2).broadcast_to([1, X.slot_tiles, E]),
                            base[0:1, 2, :].unsqueeze(1).broadcast_to([1, X.slot_tiles, E]), ALU.is_ge)
            dve.drain()
            v.tensor_tensor(place[:], place[:], base[:, 3, :].unsqueeze(1).broadcast_to([ROWS, TILES, E]), ALU.add)
            v.tensor_reduce(owner[:], passed[:], AX.X, ALU.add)
            dve.drain()
            v.tensor_scalar(owner[:], owner[:], float(E - 1), None, ALU.min)
            v.memset(fresh[:], 1.0)
            dve.drain()
            v.tensor_copy(K.owner[:, 0:X.slot_tiles], owner[:])
            v.tensor_tensor(fresh[:, 2:X.slot_tiles], owner[:, 2:X.slot_tiles], owner[:, 0:X.slot_tiles - 2],
                            ALU.not_equal)
            dve.drain()
            v.tensor_copy(K.fresh[:, 0:X.slot_tiles], fresh[:])
            for n in range(2):
                v.tensor_tensor(picked[:, :, n, :], pick[:, :, n, :], place[:], ALU.mult)
            dve.drain()
            v.tensor_reduce(slot_f[:], picked[:], AX.X, ALU.add)
            dve.drain()
            v.tensor_copy(K.slot[:], slot_f[:].rearrange("p t n -> p (t n)"))
            dve.drain()
            v.tensor_scalar(part_i[:, 0, :], K.slot[:], 7, None, ALU.arith_shift_right)
            v.tensor_scalar(part_i[:, 1, :], K.slot[:], 127, None, ALU.bitwise_and)
            dve.drain()
            v.tensor_copy(part[:], part_i[:])
            dve.drain()
            with dve.Fori(0, GROUPS) as g:
                dve.wait_ge(hot_used, g + START)
                for u in range(GROUP):
                    for n in range(2):
                        at = bass.ds(g * (GROUP * 2) + u * 2 + n, 1)
                        v.tensor_scalar(low_hot[:, u * 2 + n, :], K.number_row[0:ROWS, :], part[:, 1, at], None,
                                        ALU.is_equal)
                        v.tensor_scalar(high_hot[:, u * 2 + n, :], K.number_row[0:ROWS, 0:X.slot_tiles],
                                        part[:, 0, at], node[:, bass.ds(g * GROUP + u, 1)],
                                        ALU.is_equal, ALU.mult).then_inc(hot_ready, 1)
            dve.wait_ge(rows_found, 1 + START)
            v.tensor_copy(K.slot_row[:, 0:X.slot_tiles], ps_r[:, 0:X.slot_tiles])

        @block.scalar
        def _(act):
            def root(g, n):
                act.wait_ge(var_ready, g * norms + n + 1 + START)
                nc.scalar.activation(std[:], var_eps[:], ACT.Sqrt).then_inc(std_ready, 1)

            def group(g, b, then):
                if L0:
                    then(0)
                act.wait_ge(t_done, g + 1 + START)
                copy_transposed(nc, xt, ps_t).then_inc(xt_ready, 1)
                then(norms - 1)
                act.wait_ge(gap_ready, g + 1 + START)
                nc.scalar.activation(grown[:], gap[:], ACT.Exp).then_inc(grown_ready, 1)

            overlapped(act, GROUPS, (lambda g, b: root(g, 0), lambda g, b: root(g, 1))[:norms], group)

        @block.tensor
        def _(pe):
            pe.wait_ge(w_in, loads * 16 + START)

            def group(g, b, i):
                pe.wait_ge(row_ready, g + 1 + START)
                pe.wait_ge(xt_ready, g + START)
                transpose_group(nc, K, row[b], ps_t).then_inc(t_done, 1)
                pe.wait_ge(xt_ready, g + 1 + START)
                pe.wait_ge(l_used, g + START)
                for u in range(GROUP):
                    for k in range(KC):
                        last = nc.tensor.matmul(ps_l[0:ROWS, u * E:(u + 1) * E], xt[:, k, u * ROWS:(u + 1) * ROWS],
                                                wr[:, k, :], start=(k == 0), stop=(k == KC - 1))
                last.then_inc(l_done, 1)
            two_by_two(pe, GROUPS, group)
            pe.wait_ge(picks_ready, 1 + START)
            flat = both[:].rearrange("p t e -> p (t e)")
            nc.tensor.matmul(ps_p[0:ROWS, 0:TILES * E], below[:], flat, start=True, stop=True)
            nc.tensor.matmul(ps_s[0:ROWS, 0:TILES * E], K.ones[0:ROWS, 0:ROWS], flat, start=True, stop=True).then_inc(counted, 1)
            zero_bank(nc, K, ps_r, X.slot_tiles, start=True)
            with pe.Fori(0, GROUPS) as g:
                for n in range(GROUP * 2):
                    pe.wait_ge(hot_ready, g * (GROUP * 2) + n + 1 + START)
                    last = nc.tensor.matmul(ps_r[:, 0:X.slot_tiles], low_hot[:, n, :], high_hot[:, n, :],
                                            start=False, stop=False)
                last.then_inc(hot_used, 1)
            zero_bank(nc, K, ps_r, X.slot_tiles, start=False).then_inc(rows_found, 1)


def ahead(eng, count, early, late):
    early(0, 0, 0)
    with eng.Fori(0, count // 2) as i:
        early(i * 2 + 1, 1, i)
        late(i * 2, 0, i)
        early(i * 2 + 2, 0, i + 1)
        late(i * 2 + 1, 1, i)
    late(count - 1, 0, count // 2)


def experts(nc, K, D, X):
    L0, H = X.layer == 0, X.hidden
    HB = H // 128
    with ExitStack() as st:
        m = Memory(nc, st, f"experts{X.layer}")
        idx = [m.sb(f"idx{i}", (128, 1), I32) for i in range(2)]
        rows = [m.sb(f"rows{i}", (128, C)) for i in range(2)]
        xt = [m.sb(f"xt{i}", (128, KC, 128)) for i in range(2)]
        w1 = [m.sb(f"w1_{i}", (128, KC, H)) for i in range(2)]
        w2 = [m.sb(f"w2_{i}", (128, KC, H)) for i in range(2)]
        w3 = [m.sb(f"w3_{i}", (128, HB, C)) for i in range(2)]
        b1 = [m.sb(f"b1_{i}", (128, HB)) for i in range(2)]
        b2 = [m.sb(f"b2_{i}", (128, C)) for i in range(2)]
        gate = [m.sb(f"gate{i}", (128, HB * 128)) for i in range(2)]
        hid = [m.sb(f"hid{i}", (128, HB * 128)) for i in range(2)]
        out = [m.sb(f"out{i}", (128, C)) for i in range(2)]
        ps_t = m.ps("ps_t")
        ps_h = [m.ps(f"ps_h{i}") for i in range(2)]
        ps_g = [m.ps(f"ps_g{i}") for i in range(2)]
        ps_o = [m.ps(f"ps_o{i}") for i in range(2)]
        rows_in = [m.sem(f"rows_in{i}", start=0) for i in range(2)]
        idx_ready = m.sem("idx_ready")
        up_in, gate_in, down_in, stored = ([m.sem(f"{n}{i}") for i in range(2)]
                                           for n in ("up_in", "gate_in", "down_in", "stored"))
        w1_used, rows_used, xt_ready, h_done, h_ready, hid_ready, o_done, out_ready = (
            m.sem(n) for n in ("w1_used", "rows_used", "xt_ready", "h_done", "h_ready", "hid_ready", "o_done", "out_ready"))
        block = m.block()
        names = ("L0_ffn_W1", None, "L0_ffn_W2") if L0 else ("L1_ffn_w1", "L1_ffn_w2", "L1_ffn_w3")
        UP, DOWN = (2 if L0 else 1) * 16, (2 if L0 else 1) * 16

        @block.sync
        def _(sp):
            def tile(t, b, i):
                e = sp.value_load(K.owner[:, bass.ds(t, 1)], min_val=0, max_val=X.n - 1)
                one = bass.ds(e, 1)
                fresh = sp.value_load(K.fresh[:, bass.ds(t, 1)], min_val=0, max_val=1)

                def matrix(buf, name, sem):
                    sp.dma_start(buf[b][:], D[name][one].rearrange("e (k p) h -> p (e k) h", p=128)).then_inc(sem[b], 16)

                sp.wait_ge(h_done if L0 else w1_used, t + START)
                if L0:
                    sp.wait_ge(hid_ready, t + START)
                carry(sp, m)
                with sp.If(fresh > 0):
                    matrix(w1, names[0], up_in)
                    if L0:
                        sp.dma_start(b1[b][:], D["L0_ffn_b1"][one].rearrange("e p h -> p (e h)")).then_inc(up_in[b], 16)
                with sp.Else():
                    sp.nop().then_inc(up_in[b], UP)
                if not L0:
                    sp.wait_ge(h_done, t + START)
                    carry(sp, m)
                    with sp.If(fresh > 0):
                        matrix(w2, names[1], gate_in)
                    with sp.Else():
                        sp.nop().then_inc(gate_in[b], 16)
                sp.wait_ge(o_done, t + START)
                if L0:
                    sp.wait_ge(out_ready, t + START)
                carry(sp, m)
                with sp.If(fresh > 0):
                    matrix(w3, names[2], down_in)
                    if L0:
                        sp.dma_start(b2[b][:], D["L0_ffn_b2"][one].rearrange("e o -> (e o)").partition_broadcast(128)).then_inc(down_in[b], 16)
                with sp.Else():
                    sp.nop().then_inc(down_in[b], DOWN)
            two_by_two(sp, X.slot_tiles, tile)

        @block.gpsimd
        def _(pool):
            def gather(t, b, i):
                pool.wait_ge(rows_used, t + START)
                nc.gpsimd.tensor_copy(idx[b][:], K.slot_row[:, bass.ds(t, 1)]).then_inc(idx_ready, 1)
                pool.wait_ge(idx_ready, t + 1 + START)
                carry(pool, m)
                nc.gpsimd.indirect_dma_start(
                    out=rows[b][:], out_offset=None, in_=K.rows_dram.rearrange("t p c -> (t p) c"),
                    in_offset=bass.IndirectOffsetOnAxis(ap=idx[b][:, 0:1], axis=0)).then_inc(rows_in[b], 16)
            two_by_two(pool, X.slot_tiles, gather)

        @block.tensor
        def _(pe):
            pe.nop().then_inc(rows_used, 1)
            pe.nop().then_inc(w1_used, 1)
            pe.nop().then_inc(h_done, 1)
            pe.nop().then_inc(hid_ready, 1)
            pe.nop().then_inc(o_done, 1)

            def turn(t, b, i):
                pe.wait_ge(rows_in[b], (i + 1) * 16)
                pe.wait_ge(xt_ready, t + START)
                for k in range(KC):
                    last = nc.tensor.transpose(ps_t[:, k * 128:(k + 1) * 128], rows[b][:, k * 128:(k + 1) * 128],
                                               K.ident_f[:])
                last.then_inc(rows_used, 1)

            def up(t, b, i):
                pe.wait_ge(xt_ready, t + 1 + START)
                pe.wait_ge(up_in[b], (i + 1) * UP + START)
                for w, ps in ((w1, ps_h),) if L0 else ((w1, ps_h), (w2, ps_g)):
                    if w is w2:
                        last.then_inc(w1_used, 1)
                        pe.wait_ge(gate_in[b], (i + 1) * 16 + START)
                    for h in range(HB):
                        for k in range(KC):
                            last = nc.tensor.matmul(ps[b][:, h * 128:(h + 1) * 128],
                                                    w[b][:, k, h * 128:(h + 1) * 128], xt[b][:, k, :],
                                                    start=(k == 0), stop=(k == KC - 1))
                last.then_inc(h_done, 1)

            def down(t, b, i):
                pe.wait_ge(hid_ready, t + 2 + START)
                pe.wait_ge(down_in[b], (i + 1) * DOWN + START)
                pe.wait_ge(out_ready, t + START)
                for h in range(HB):
                    last = nc.tensor.matmul(ps_o[b][:, 0:C], hid[b][:, h * 128:(h + 1) * 128], w3[b][:, h, :],
                                            start=(h == 0), stop=(h == HB - 1))
                last.then_inc(o_done, 1)

            last = X.slot_tiles - 1
            turn(0, 0, 0)
            up(0, 0, 0)
            turn(1, 1, 0)
            with pe.Fori(0, (last - 2) // 2) as i:
                up(i * 2 + 1, 1, i)
                turn(i * 2 + 2, 0, i + 1)
                down(i * 2, 0, i)
                up(i * 2 + 2, 0, i + 1)
                turn(i * 2 + 3, 1, i + 1)
                down(i * 2 + 1, 1, i)
            up(last - 1, 1, last // 2 - 1)
            turn(last, 0, last // 2)
            down(last - 2, 0, last // 2 - 1)
            up(last, 0, last // 2)
            down(last - 1, 1, last // 2 - 1)
            down(last, 0, last // 2)

        @block.scalar
        def _(act):
            def move(t, b, i):
                act.wait_ge(rows_used, t + 2 + START)
                nc.scalar.activation(xt[b][:].rearrange("p k s -> p (k s)"), ps_t[:, 0:C], ACT.Copy).then_inc(xt_ready, 1)

            def activate(t, b, i):
                act.wait_ge(h_done, t + 2 + START)
                if L0:
                    act.wait_ge(up_in[b], (i + 1) * UP + START)
                    act.wait_ge(o_done, t + START)
                    for h in range(HB):
                        last = nc.scalar.activation(hid[b][:, h * 128:(h + 1) * 128], ps_h[b][:, h * 128:(h + 1) * 128],
                                                    ACT.Gelu, bias=b1[b][:, h:h + 1])
                    last.then_inc(hid_ready, 1)
                else:
                    act.wait_ge(hid_ready, t + START)
                    nc.scalar.activation(gate[b][:], ps_h[b][:], ACT.Silu).then_inc(h_ready, 1)

            def store(t, b, i):
                act.wait_ge(out_ready, t + 2 + START)
                act.dma_start(K.slot_out[bass.ds(t * 128, 128), :], out[b][:]).then_inc(stored[b], 16)

            last = X.slot_tiles - 1
            move(0, 0, 0)
            move(1, 1, 0)
            activate(0, 0, 0)
            with act.Fori(0, (last - 2) // 2) as i:
                move(i * 2 + 2, 0, i + 1)
                activate(i * 2 + 1, 1, i)
                store(i * 2, 0, i)
                move(i * 2 + 3, 1, i + 1)
                activate(i * 2 + 2, 0, i + 1)
                store(i * 2 + 1, 1, i)
            move(last, 0, last // 2)
            activate(last - 1, 1, last // 2 - 1)
            store(last - 2, 0, last // 2 - 1)
            activate(last, 0, last // 2)
            store(last - 1, 1, last // 2 - 1)
            store(last, 0, last // 2)
            act.wait_ge(stored[0], (X.slot_tiles // 2 + 1) * 16 + START)
            act.wait_ge(stored[1], (X.slot_tiles // 2) * 16 + START)

        @block.vector
        def _(dve):
            dve.nop().then_inc(out_ready, 1)

            def product(t, b, i):
                if not L0:
                    dve.wait_ge(h_ready, t + 1 + START)
                    dve.wait_ge(o_done, t + START)
                    nc.vector.tensor_tensor(hid[b][:], gate[b][:], ps_g[b][:], ALU.mult).then_inc(hid_ready, 1)

            def result(t, b, i):
                dve.wait_ge(o_done, t + 2 + START)
                dve.wait_ge(stored[b], i * 16 + START)
                if L0:
                    dve.wait_ge(down_in[b], (i + 1) * DOWN + START)
                    nc.vector.tensor_tensor(out[b][:], ps_o[b][:, 0:C], b2[b][:], ALU.add).then_inc(out_ready, 1)
                else:
                    nc.vector.tensor_copy(out[b][:], ps_o[b][:, 0:C]).then_inc(out_ready, 1)
            ahead(dve, X.slot_tiles, product, result)


def combine(nc, K, X, result):
    with ExitStack() as st:
        m = Memory(nc, st, f"combine{X.layer}")
        slot_g = [m.sb(f"slot_g{i}", (ROWS, GROUP * 2), I32) for i in range(2)]
        got = [m.sb(f"got{i}", (ROWS, GROUP * 2, C)) for i in range(2)]
        copied, added, stored = m.sem("copied"), m.sem("added"), m.sem("stored")
        gathered = [m.sem(f"gathered{i}", start=0) for i in range(2)]
        block = m.block()

        @block.gpsimd
        def _(pool):
            def group(g, b, i):
                pool.wait_ge(added, (g if b == 0 else g - 1) + START)
                nc.gpsimd.tensor_copy(slot_g[b][:], K.slot[:, bass.ds(g * (GROUP * 2), GROUP * 2)]).then_inc(copied, 1)
                pool.wait_ge(copied, g + 1 + START)
                carry(pool, m)
                for n in range(GROUP * 2):
                    nc.gpsimd.indirect_dma_start(
                        out=got[b][:, n, :], out_offset=None, in_=K.slot_out[0:X.slot_tiles * 128, :],
                        in_offset=bass.IndirectOffsetOnAxis(ap=slot_g[b][:, n:n + 1], axis=0)).then_inc(gathered[b], 16)
            two_by_two(pool, GROUPS, group)

        @block.vector
        def _(dve):
            def group(g, b, i):
                dve.wait_ge(gathered[b], (i + 1) * (GROUP * 2 * 16))
                for n in range(2):
                    for u in range(GROUP):
                        t = g * GROUP + u
                        last = nc.vector.scalar_tensor_tensor(K.X[:, t, :], got[b][:, 2 * u + n, :],
                                                              K.gate[:, t, n:n + 1], K.X[:, t, :],
                                                              ALU.mult, ALU.add)
                    if n == 0:
                        dve.drain()
                last.then_inc(added, 1)
            two_by_two(dve, GROUPS, group)

        @block.sync
        def _(sp):
            if result is not None:
                view = result.rearrange("(t p) c -> p t c", p=ROWS)
                with sp.Fori(0, GROUPS) as g:
                    sp.wait_ge(added, g + 1 + START)
                    tiles = bass.ds(g * GROUP, GROUP)
                    for a, z in ((0, DMA_ROWS), (DMA_ROWS, ROWS)):
                        sp.dma_start(view[a:z, tiles, :], K.X[a:z, tiles, :]).then_inc(stored, 16)
                sp.wait_ge(stored, GROUPS * 32 + START)


def degree_scale(nc, K):
    with ExitStack() as st:
        m = Memory(nc, st, "degree")
        deg = m.sb("deg", (ROWS, TILES))
        ready, rooted = m.sem("ready"), m.sem("rooted")
        block = m.block()

        @block.vector
        def _(dve):
            nc.vector.tensor_scalar(deg[:], K.DEG[:], 1.0, None, ALU.add).then_inc(ready, 1)
            dve.wait_ge(rooted, 1 + START)
            nc.vector.reciprocal(K.DINV[:], K.DINV[:])

        @block.scalar
        def _(act):
            act.wait_ge(ready, 1 + START)
            nc.scalar.activation(K.DINV[:], deg[:], ACT.Sqrt).then_inc(rooted, 1)


def mix_tail_l1(nc, K, D):
    with ExitStack() as st:
        m = Memory(nc, st, "mix1")
        w = m.sb("w", (128, KC, C))
        bias = m.sb("bias", (ROWS, C))
        qt = [m.sb(f"qt{i}", (128, KC, GROWS)) for i in range(2)]
        den = m.sb("den", (ROWS, GROUP, KC, HPB))
        att = m.sb("att", (ROWS, GROUP, C))
        att_t = m.sb("att_t", (128, KC, GROWS))
        ps_t = [m.ps(f"ps_t{i}") for i in range(3)]
        ps_a = [m.ps(f"ps_a{i}") for i in range(2)]
        ps_o = [m.ps(f"ps_o{i}") for i in range(2)]
        w_in, qt_ready, a_done, a_used, att_ready, t_done, att_t_ready, o_done, o_used = (
            m.sem(n) for n in ("w_in", "qt_ready", "a_done", "a_used", "att_ready", "t_done", "att_t_ready",
                               "o_done", "o_used"))
        block = m.block()

        @block.sync
        def _(sp):
            sp.dma_start(w[:], D["L1_mix_Wproj"].rearrange("(k p) o -> p k o", p=128)).then_inc(w_in, 16)
            sp.dma_start(bias[:], D["L1_mix_bproj"].partition_broadcast(ROWS)).then_inc(w_in, 16)
            sp.wait_ge(w_in, 32 + START)

        @block.gpsimd
        def _(pool):
            def copy(g, b):
                pool.wait_ge(a_done, (g - 1) * GROUP + START)
                nc.gpsimd.tensor_copy(qt[b][:], K.QT[:, :, bass.ds(g * GROWS, GROWS)]).then_inc(qt_ready, 1)
            after_first(pool, copy)

        @block.vector
        def _(dve):
            dve.wait_ge(w_in, 32 + START)

            def attention(g, b):
                dve.wait_ge(t_done, g + START)
                for u in range(GROUP):
                    t = g * GROUP + u
                    dve.wait_ge(a_done, t + 1 + START)
                    a = ps_a[u % 2][0:ROWS, 0:KC * KVW].rearrange("p (k w) -> p k w", k=KC)
                    nc.vector.tensor_scalar(den[:, u], a[:, :, 128:KVW], 1e-6, None, ALU.max)
                    dve.drain()
                    nc.vector.reciprocal(den[:, u], den[:, u])
                    dve.drain()
                    for k in range(KC):
                        last = nc.vector.tensor_tensor(
                            att[:, u, k * 128:(k + 1) * 128].rearrange("p (a d) -> p a d", d=HD),
                            a[:, k, 0:128].rearrange("p (a d) -> p a d", d=HD),
                            den[:, u, k, :].unsqueeze(2).broadcast_to([ROWS, HPB, HD]), ALU.mult)
                    last.then_inc(a_used, 1)
                dve.drain()
                dve.nop().then_inc(att_ready, 1)

            def project(g, b, then):
                tiles = bass.ds(g * GROUP, GROUP)
                nc.vector.tensor_tensor(K.X[:, tiles, :], K.X[:, tiles, :],
                                        bias[:].unsqueeze(1).broadcast_to([ROWS, GROUP, C]), ALU.add)
                then(0)
                dve.drain()
                for u in range(GROUP):
                    t = g * GROUP + u
                    dve.wait_ge(o_done, t + 1 + START)
                    nc.vector.tensor_tensor(K.X[:, t, :], ps_o[u % 2][0:ROWS, 0:C], K.X[:, t, :],
                                            ALU.add).then_inc(o_used, 1)

            overlapped(dve, GROUPS, (attention,), project)

        @block.scalar
        def _(act):
            with act.Fori(0, GROUPS) as g:
                act.wait_ge(t_done, g + 1 + START)
                copy_transposed(nc, att_t, ps_t).then_inc(att_t_ready, 1)

        @block.tensor
        def _(pe):
            pe.wait_ge(w_in, 32 + START)

            def attention(g, b):
                q = qt[b]
                if isinstance(g, int):
                    q = K.QT
                else:
                    pe.wait_ge(qt_ready, g + START)
                for u in range(GROUP):
                    t = g * GROUP + u
                    pe.wait_ge(a_used, (t if u == 0 else t - 1) + START)
                    for k in range(KC):
                        last = nc.tensor.matmul(ps_a[u % 2][0:ROWS, k * KVW:(k + 1) * KVW],
                                                q[:, k, u * ROWS:(u + 1) * ROWS], K.kv[:, k, :],
                                                start=True, stop=True)
                    last.then_inc(a_done, 1)

            def project(g, b, then):
                pe.wait_ge(att_ready, g + 1 + START)
                pe.wait_ge(att_t_ready, g + START)
                transpose_group(nc, K, att, ps_t).then_inc(t_done, 1)
                then(0)
                pe.wait_ge(att_t_ready, g + 1 + START)
                for u in range(GROUP):
                    t = g * GROUP + u
                    pe.wait_ge(o_used, (t if u == 0 else t - 1) + START)
                    for k in range(KC):
                        last = nc.tensor.matmul(ps_o[u % 2][0:ROWS, 0:C], att_t[:, k, u * ROWS:(u + 1) * ROWS],
                                                w[:, k, :], start=(k == 0), stop=(k == KC - 1))
                    last.then_inc(o_done, 1)

            overlapped(pe, GROUPS, (attention,), project)


def gcn(nc, K, D):
    with ExitStack() as st:
        m = Memory(nc, st, "gcn")
        adj = [m.sb(f"adj{i}", (ROWS, TILES * ROWS), BF16) for i in range(4)]
        bias = m.sb("bias", (ROWS, C))
        acc = m.sb("acc", (ROWS, C))
        ps_a = [m.ps(f"ps_a{i}") for i in range(2)]
        ps_b = [m.ps(f"ps_b{i}") for i in range(2)]
        arrived = [m.sem(f"in{i}") for i in range(4)]
        b_in, done, used = m.sem("b_in"), m.sem("done"), m.sem("used")
        block = m.block()

        @block.sync
        def _(sp):
            sp.dma_start(bias[:], D["L1_gnn_b1"].partition_broadcast(ROWS)).then_inc(b_in, 16)
            load_tiles(sp, adj, K.adj, arrived, done)

        @block.tensor
        def _(pe):
            def tile(t, c, j):
                b = c % 2
                pe.wait_ge(arrived[c], (j + 1) * 32 + START)
                pe.wait_ge(used, (t if c == 0 else t - 1) + START)
                for s in range(TILES):
                    w = adj[c][:, s * ROWS:(s + 1) * ROWS]
                    nc.tensor.matmul(ps_a[b][0:ROWS, :], w, K.Yp[:, s, 0:512], start=(s == 0), stop=(s == TILES - 1))
                    last = nc.tensor.matmul(ps_b[b][0:ROWS, 0:C], w, K.Yp[:, s, 512:768],
                                            start=(s == 0), stop=(s == TILES - 1))
                last.then_inc(done, 1)
            four_by_four(pe, tile)

        @block.vector
        def _(dve):
            dve.wait_ge(b_in, 16 + START)

            def tile(t, b, i):
                dve.wait_ge(done, t + 1 + START)
                nc.vector.tensor_tensor(acc[:], ps_a[b][0:ROWS, 0:C], K.Y[:, t, :], ALU.add)
                dve.drain()
                nc.vector.tensor_tensor(acc[:], acc[:], ps_a[b][0:ROWS, C:2 * C], ALU.add)
                dve.drain()
                nc.vector.tensor_tensor(acc[:], acc[:], ps_b[b][0:ROWS, 0:C], ALU.add).then_inc(used, 1)
                dve.drain()
                nc.vector.scalar_tensor_tensor(acc[:], acc[:], K.DINV[:, bass.ds(t, 1)], bias[:], ALU.mult, ALU.add)
                dve.drain()
                nc.vector.tensor_scalar(K.XN[:, t, :], acc[:], 0.0, None, ALU.max)
                dve.drain()
            two_by_two(dve, TILES, tile)


def gat_project(nc, K, D):
    with ExitStack() as st:
        m = Memory(nc, st, "gatp")
        w = m.sb("w", (128, KC, C))
        vec = m.sb("vec", (ROWS, 2, C))
        row = [m.sb(f"row{i}", (ROWS, GROUP, C)) for i in range(2)]
        xt = m.sb("xt", (128, KC, GROWS))
        prod, dots = m.sb("prod", (ROWS, GROUP, 2, C)), m.sb("dots", (ROWS, 2, GROUP))
        at_src = m.sb("at_src", (ROWS, TILES))
        line = m.sb("line", (TILES, ROWS))
        ps_t = [m.ps(f"ps_t{i}") for i in range(3)]
        ps_y = [m.ps(f"ps_y{i}") for i in range(2)]
        w_in, row_ready, t_done, xt_ready, y_done, y_used, src_ready, turned, line_ready, line_out, spread = (
            m.sem(n) for n in ("w_in", "row_ready", "t_done", "xt_ready", "y_done", "y_used", "src_ready",
                               "turned", "line_ready", "line_out", "spread"))
        block = m.block()

        @block.sync
        def _(sp):
            sp.dma_start(w[:], D["L1_gnn_W2"].rearrange("(k p) o -> p k o", p=128)).then_inc(w_in, 16)
            sp.dma_start(vec[:, 0, :], D["L1_gnn_att_src"].partition_broadcast(ROWS)).then_inc(w_in, 16)
            sp.dma_start(vec[:, 1, :], D["L1_gnn_att_dst"].partition_broadcast(ROWS)).then_inc(w_in, 16)
            sp.wait_ge(w_in, 48 + START)
            sp.wait_ge(line_ready, 1 + START)
            sp.dma_start(K.src_line, line[:]).then_inc(line_out, 16)
            sp.wait_ge(line_out, 16 + START)
            sp.dma_start(K.SRC[:], K.src_line.rearrange("t p -> (t p)").partition_broadcast(ROWS)).then_inc(spread, 16)
            sp.wait_ge(spread, 16 + START)

        @block.gpsimd
        def _(pool):
            def copy(g, b):
                pool.wait_ge(t_done, (g - 1) + START)
                nc.gpsimd.tensor_copy(row[b][:], K.XN[:, bass.ds(g * GROUP, GROUP), :]).then_inc(row_ready, 1)
            after_first(pool, copy)

        @block.scalar
        def _(act):
            with act.Fori(0, GROUPS) as g:
                act.wait_ge(t_done, g + 1 + START)
                copy_transposed(nc, xt, ps_t).then_inc(xt_ready, 1)

        @block.vector
        def _(dve):
            dve.wait_ge(w_in, 48 + START)
            with dve.Fori(0, GROUPS) as g:
                for u in range(GROUP):
                    t = g * GROUP + u
                    dve.wait_ge(y_done, t + 1 + START)
                    bank = ps_y[u % 2][0:ROWS, 0:C]
                    nc.vector.tensor_scalar(K.Y[:, t, :], bank, 0.0, None, ALU.add)
                    for n in range(2):
                        last = nc.vector.tensor_tensor_reduce(out=prod[:, u, n, :], in0=bank, in1=vec[:, n, :],
                                                              scale=1.0, scalar=0.0, op0=ALU.mult, op1=ALU.add,
                                                              accum_out=dots[:, n, u:u + 1])
                    last.then_inc(y_used, 1)
                dve.drain()
                tiles = bass.ds(g * GROUP, GROUP)
                nc.vector.tensor_copy(at_src[:, tiles], dots[:, 0, :])
                nc.vector.tensor_copy(K.AT_DST[:, tiles], dots[:, 1, :])
                dve.drain()
            dve.nop().then_inc(src_ready, 1)
            dve.wait_ge(turned, 1 + START)
            nc.vector.tensor_copy(line[:], ps_t[0][0:TILES, 0:ROWS]).then_inc(line_ready, 1)

        @block.tensor
        def _(pe):
            pe.wait_ge(w_in, 48 + START)

            def group(g, b):
                rows = row[b]
                if isinstance(g, int):
                    rows = K.XN
                else:
                    pe.wait_ge(row_ready, g + START)
                pe.wait_ge(xt_ready, g + START)
                transpose_group(nc, K, rows, ps_t).then_inc(t_done, 1)
                pe.wait_ge(xt_ready, g + 1 + START)
                for u in range(GROUP):
                    t = g * GROUP + u
                    pe.wait_ge(y_used, (t if u == 0 else t - 1) + START)
                    for k in range(KC):
                        last = nc.tensor.matmul(ps_y[u % 2][0:ROWS, 0:C], xt[:, k, u * ROWS:(u + 1) * ROWS],
                                                w[:, k, :], start=(k == 0), stop=(k == KC - 1))
                    last.then_inc(y_done, 1)

            group(0, 0)
            after_first(pe, group)
            pe.wait_ge(src_ready, 1 + START)
            nc.tensor.transpose(ps_t[0][0:TILES, 0:ROWS], at_src[:], K.ident_f[0:ROWS, 0:ROWS]).then_inc(turned, 1)


def gat(nc, K, D):
    quads = [(a, min(a + 4, TILES)) for a in range(0, TILES, 4)]
    NQ = len(quads)
    with ExitStack() as st:
        m = Memory(nc, st, "gat")
        cnt = [m.sb(f"cnt{i}", (ROWS, NODES), BF16) for i in range(4)]
        absent = m.sb("absent", (ROWS, NODES), BF16)
        score = [m.sb(f"score{i}", (ROWS, NODES)) for i in range(2)]
        prob = [m.sb(f"prob{i}", (ROWS, NODES)) for i in range(2)]
        prob_t = m.sb("prob_t", (ROWS, NODES))
        bias = m.sb("bias", (ROWS, C))
        small = m.sb("small", (ROWS, 2, 8))
        acc = m.sb("acc", (ROWS, C))
        ps_t = [m.ps(f"ps_t{i}") for i in range(4)]
        ps_o = [m.ps(f"ps_o{i}") for i in range(2)]
        arrived = [m.sem(f"in{i}") for i in range(4)]
        b_in, scored, first_exp, exped, weighed, t_done, t_read, o_done, o_used = (
            m.sem(n) for n in ("b_in", "scored", "first_exp", "exped", "weighed", "t_done",
                               "t_read", "o_done", "o_used"))
        block = m.block()
        greatest, dst, top, low, shift1, shift5, total, inv = range(8)

        def cell(b, n):
            return small[:, b, n:n + 1]

        @block.sync
        def _(sp):
            sp.dma_start(bias[:], D["L1_gnn_b2"].partition_broadcast(ROWS)).then_inc(b_in, 16)
            load_tiles(sp, cnt, K.adj_t, arrived, weighed)

        @block.vector
        def _(dve):
            v = nc.vector

            def own_loop(t, b, c, use):
                dve.wait_ge(arrived[c], use * 32 + START)
                own = cnt[c][:, bass.ds(t * ROWS, ROWS)]
                v.tensor_tensor(own, own, K.ident_b[0:ROWS, 0:ROWS], ALU.add)
                v.tensor_copy(cell(b, dst), K.AT_DST[:, bass.ds(t, 1)])

            def mask(c):
                v.tensor_scalar(absent[:], cnt[c][:], 0.0, -1e30, ALU.is_equal, ALU.mult)

            def scores(b):
                v.tensor_tensor_reduce(out=score[b][:], in0=absent[:], in1=K.SRC[:], scale=1.0, scalar=-3e38,
                                       op0=ALU.add, op1=ALU.max, accum_out=cell(b, greatest))

            def greatest_score(b):
                v.tensor_tensor(cell(b, top), cell(b, greatest), cell(b, dst), ALU.add)

            def shifts(b):
                v.scalar_tensor_tensor(cell(b, low), cell(b, top), 0.2, cell(b, top), ALU.mult, ALU.max)
                dve.drain()
                v.tensor_tensor(cell(b, shift1), cell(b, dst), cell(b, low), ALU.subtract)
                v.scalar_tensor_tensor(cell(b, shift5), cell(b, dst), 0.2, cell(b, low), ALU.mult,
                                       ALU.subtract).then_inc(scored, 1)

            def weigh(t, b, c):
                dve.wait_ge(exped, t + 1 + START)
                v.tensor_tensor(score[b][:], score[b][:], prob[b][:], ALU.max)
                dve.drain()
                v.tensor_tensor_reduce(out=prob[b][:], in0=score[b][:], in1=cnt[c][:], scale=1.0, scalar=0.0,
                                       op0=ALU.mult, op1=ALU.add, accum_out=cell(b, total)).then_inc(weighed, 1)

            def guard(b):
                v.tensor_scalar(cell(b, inv), cell(b, total), 1e-16, None, ALU.add)

            def invert(b):
                v.reciprocal(cell(b, inv), cell(b, inv))

            def divide(t, b):
                dve.wait_ge(o_done, t + 1 + START)
                v.scalar_tensor_tensor(acc[:], ps_o[b][0:ROWS, 0:C], cell(b, inv), bias[:], ALU.mult,
                                       ALU.add).then_inc(o_used, 1)

            def add(t):
                v.scalar_tensor_tensor(K.X[:, t, :], acc[:], 0.0, K.X[:, t, :], ALU.max, ALU.add)

            def step(j, r):
                t, b = j * 4 + r, r % 2
                after = not isinstance(t, int) or t + 1 < TILES
                before, finish = (not isinstance(t, int) or t >= n for n in (1, 2))
                if after:
                    own_loop(t + 1, 1 - b, (r + 1) % 4, j + (r + 1) // 4 + 1)
                dve.drain()
                if after:
                    mask((r + 1) % 4)
                if before:
                    guard(1 - b)
                dve.drain()
                if after:
                    scores(1 - b)
                if before:
                    invert(1 - b)
                if finish:
                    divide(t - 2, b)
                dve.drain()
                if after:
                    greatest_score(1 - b)
                if finish:
                    add(t - 2)
                dve.drain()
                if after:
                    shifts(1 - b)
                weigh(t, b, r % 4)

            dve.wait_ge(b_in, 16 + START)
            own_loop(0, 0, 0, 1)
            dve.drain()
            mask(0)
            dve.drain()
            scores(0)
            dve.drain()
            greatest_score(0)
            dve.drain()
            shifts(0)
            step(0, 0)
            step(0, 1)
            with dve.Fori(0, TILES // 4 - 1) as j:
                for r in range(2, 6):
                    step(j, r)
            for r in range(2, 5):
                step(TILES // 4 - 1, r)
            divide(TILES - 2, 1)
            dve.drain()
            add(TILES - 2)
            guard(0)
            dve.drain()
            invert(0)
            dve.drain()
            divide(TILES - 1, 0)
            dve.drain()
            add(TILES - 1)

        @block.scalar
        def _(act):
            def exponentials(t, b):
                act.wait_ge(scored, t + 1 + START)
                if not isinstance(t, int) or t >= 2:
                    act.wait_ge(t_done, (t - 1) * NQ + START)
                nc.scalar.activation(prob[b][:], score[b][:], ACT.Exp, bias=cell(b, shift1)).then_inc(first_exp, 1)
                act.wait_ge(first_exp, t + 1 + START)
                nc.scalar.activation(score[b][:], score[b][:], ACT.Exp, bias=cell(b, shift5),
                                     scale=0.2).then_inc(exped, 1)

            def move(t):
                for n, (a, z) in enumerate(quads):
                    act.wait_ge(t_done, t * NQ + n + 1 + START)
                    nc.scalar.activation(prob_t[:, a * ROWS:z * ROWS], ps_t[n % 4][0:ROWS, 0:(z - a) * ROWS],
                                         ACT.Copy).then_inc(t_read, 1)

            exponentials(0, 0)
            exponentials(1, 1)
            move(0)
            exponentials(2, 0)
            move(1)
            with act.Fori(1, TILES // 2) as i:
                exponentials(i * 2 + 1, 1)
                move(i * 2)
                exponentials(i * 2 + 2, 0)
                move(i * 2 + 1)
            move(TILES - 1)

        @block.tensor
        def _(pe):
            def tile(t, b, i):
                pe.wait_ge(weighed, t + 1 + START)
                for n, (a, z) in enumerate(quads):
                    pe.wait_ge(t_read, t * NQ + max(n - 3, 0) + START)
                    for s in range(a, z):
                        last = nc.tensor.transpose(ps_t[n % 4][0:ROWS, (s - a) * ROWS:(s - a + 1) * ROWS],
                                                   prob[b][:, s * ROWS:(s + 1) * ROWS], K.ident_f[0:ROWS, 0:ROWS])
                    last.then_inc(t_done, 1)
                pe.wait_ge(o_used, (t if b == 0 else t - 1) + START)
                for n, (a, z) in enumerate(quads):
                    pe.wait_ge(t_read, t * NQ + n + 1 + START)
                    for s in range(a, z):
                        last = nc.tensor.matmul(ps_o[b][0:ROWS, 0:C], prob_t[:, s * ROWS:(s + 1) * ROWS],
                                                K.Y[:, s, :], start=(s == 0), stop=(s == TILES - 1))
                last.then_inc(o_done, 1)
            two_by_two(pe, TILES, tile)


class Kept:
    pass


def program(nc, D, result):
    X0, X1 = Experts(0), Experts(1)
    slots = 128 * max(X0.slot_tiles, X1.slot_tiles)
    K = Kept()
    K.adj = nc.dram_tensor("adjacency", (TILES, ROWS, TILES * ROWS), BF16).ap()
    K.adj_t = nc.dram_tensor("adjacency_t", (TILES, ROWS, NODES), BF16).ap()
    K.rows_dram = nc.dram_tensor("expert_rows", (TILES, ROWS, C), F32).ap()
    K.slot_out = nc.dram_tensor("slot_out", (slots, C), F32).ap()
    K.src_line = nc.dram_tensor("src_line", (TILES, ROWS), F32).ap()
    with ExitStack() as all_:
        def sb(stack, name, shape, dt=F32):
            return stack.enter_context(nc.sbuf_tensor(name, list(shape), dt))

        K.X = sb(all_, "X", (ROWS, TILES, C))
        K.ident_f, K.ident_b = sb(all_, "ident_f", (128, 128)), sb(all_, "ident_b", (128, 128), BF16)
        K.number_row, K.number_f = sb(all_, "number_row", (128, 128), F16), sb(all_, "number_f", (128, 128))
        K.zeros, K.ones = sb(all_, "zeros", (1, 512)), sb(all_, "ones", (128, 128))
        K.DEG, K.DINV, K.AT_DST = (sb(all_, n, (ROWS, TILES)) for n in ("DEG", "DINV", "AT_DST"))
        K.slot, K.gate = sb(all_, "slot", (ROWS, TILES * 2), I32), sb(all_, "gate", (ROWS, TILES, 2))
        K.slot_row = sb(all_, "slot_row", (128, slots // 128), I32)
        K.owner, K.fresh = sb(all_, "owner", (1, 128), I32), sb(all_, "fresh", (1, 128), I32)
        K.kv = sb(all_, "kv", (128, KC, KVW))
        constants(nc, K)

        build_adjacency(nc, K, D)
        with ExitStack() as layer:
            K.XN, K.X1 = sb(layer, "XN0", (ROWS, TILES, C)), sb(layer, "X1", (ROWS, TILES, C))
            K.QT = sb(layer, "QT0", (128, KC, NODES))
            K.Y, K.AGG = sb(layer, "Y0", (ROWS, TILES, 64)), sb(layer, "AGG", (ROWS, TILES, 64))
            K.Yp = sb(layer, "Yp0", (ROWS, TILES, 256), BF16)
            front(nc, K, "front0", D["L0_gnn_W1_down"], 64, D["L0_mix_Wkv"], D["L0_mix_Wq"], None)
            mix_tail_l0(nc, K, D)
            gin_down(nc, K)
            gin_tail(nc, K, "gin_down", D, "down", K.XN, K.X1)
            gin_up(nc, K)
            gin_tail(nc, K, "gin_up", D, "up", K.X1, None)
        route(nc, K, D, X0)
        experts(nc, K, D, X0)
        combine(nc, K, X0, None)
        with ExitStack() as layer:
            K.XN, K.Y = sb(layer, "XN1", (ROWS, TILES, C)), sb(layer, "Y1", (ROWS, TILES, C))
            with ExitStack() as early:
                K.QT = sb(early, "QT1", (128, KC, NODES))
                K.Yp = sb(early, "Yp1", (ROWS, TILES, 3 * C), BF16)
                degree_scale(nc, K)
                front(nc, K, "front1", D["L1_gnn_W1"], C, D["L1_mix_Wkv"], D["L1_mix_Wq"], K.DINV)
                mix_tail_l1(nc, K, D)
                gcn(nc, K, D)
            K.SRC = sb(layer, "SRC", (ROWS, NODES))
            gat_project(nc, K, D)
            gat(nc, K, D)
        route(nc, K, D, X1)
        experts(nc, K, D, X1)
        combine(nc, K, X1, result)


def lay_out(inputs):
    import numpy as np

    a = {k: np.ascontiguousarray(v) for k, v in inputs.items()}
    wqkv = a.pop("L0_mix_Wqkv")
    a["L0_mix_Wq"] = np.ascontiguousarray(wqkv[:C].T)
    a["L0_mix_Wkv"] = np.ascontiguousarray(wqkv[C:].T)
    for name in ("L0_mix_W1", "L0_mix_W2", "L1_mix_Wq", "L1_mix_Wkv", "L1_mix_Wproj"):
        a[name] = np.ascontiguousarray(a[name].T)
    a["L0_mix_b1"] = np.ascontiguousarray(a["L0_mix_b1"].reshape(KC, 128).T)
    a["L0_ffn_b1"] = np.ascontiguousarray(a["L0_ffn_b1"].reshape(8, 4, 128).transpose(0, 2, 1))
    for name in ("L0_gnn_eps_down", "L0_gnn_eps_up"):
        a[name] = a[name].reshape(1)
    src, dst = a.pop("src"), a.pop("dst")
    for name, e in (("src", src), ("dst", dst)):
        cols = np.full(CHUNKS_PAD * CH, NODES, np.int32)
        cols[:EDGES] = e
        a[name + "_cols"] = np.ascontiguousarray(cols.reshape(CHUNKS_PAD, CH).T)
    rows = np.full(CHUNK_ROWS * CH, NODES, np.int32)
    rows[:EDGES] = dst
    a["dst_rows"] = rows.reshape(128, 4 * CH)
    return a


def kernel(**inputs):
    import concourse.bacc as bacc
    import numpy as np
    from concourse.bass_utils import run_bass_kernel_spmd

    nc = bacc.Bacc("TRN2", target_bir_lowering=False, num_devices=1)
    arrays = {"in_" + k: v for k, v in lay_out(inputs).items()}
    D = {k[3:]: nc.dram_tensor(k, v.shape, mybir.dt.from_np(v.dtype), kind="ExternalInput").ap()
         for k, v in arrays.items()}
    out = nc.dram_tensor("out", (NODES, C), F32, kind="ExternalOutput").ap()
    program(nc, D, out)
    got = run_bass_kernel_spmd(nc, [arrays], core_ids=[0])
    return got.results[0]["out"]
```
